# Optimizing a Trainium2 kernel written in Bass

```python
import numpy as np
import jax
import jax.numpy as jnp

def _softmax(x, axis=-1):
    return jax.nn.softmax(x, axis=axis)

def _gelu(x):
    return jax.nn.gelu(x, approximate=True)

def _silu(x):
    return jax.nn.silu(x)

def _sigmoid(x):
    return jax.nn.sigmoid(x)

def _layernorm(x, axis=-1, eps=1e-05):
    m = jnp.mean(x, axis=axis, keepdims=True)
    v = jnp.var(x, axis=axis, keepdims=True)
    return (x - m) / jnp.sqrt(v + eps)

def _scatter_add(tgt, idx, src, axis=0):
    return tgt.at[idx].add(src)

def _segment_sum(src, seg, n):
    return jax.ops.segment_sum(src, seg, n)
kernel_name = 'mk_vit_tower_d1_tok_img768_r4_17024e'

def setup_inputs(seed: int=0):
    np.random.seed(seed)
    _w = jnp.asarray

    def _rec_inputs():
        import jax
        import jax.numpy as jnp
        _rk = jax.random.key(seed)
        x = 7.57192e-06 + 1.00007 * jax.random.normal(jax.random.fold_in(_rk, 1), (16, 3, 96, 96), jnp.float32)
        return x
    x = _rec_inputs()

    def _L0_tok_setup():
        import jax, jax.numpy as jnp
        import numpy as np
        PATCH = 16

        def _shift2d(x, shift):
            l, r, t, b = shift
            H, W = (x.shape[2], x.shape[3])
            xp = jnp.pad(x, ((0, 0), (0, 0), (max(t, 0), max(b, 0)), (max(l, 0), max(r, 0))))
            h0 = max(-t, 0)
            w0 = max(-l, 0)
            return xp[:, :, h0:h0 + H, w0:w0 + W]
        key = jax.random.key(seed)
        k1, k2 = jax.random.split(key)
        B, C, H, W = (64, 3, 224, 224)
        dim = 192
        patch_dim = PATCH * PATCH * 5 * C
        x = jax.random.normal(k1, (B, C, H, W), dtype=jnp.float32)
        ln_weight = jnp.ones((patch_dim,), dtype=jnp.float32)
        ln_bias = jnp.zeros((patch_dim,), dtype=jnp.float32)
        proj_weight = jax.random.normal(k2, (dim, patch_dim), dtype=jnp.float32) * patch_dim ** (-0.5)
        proj_bias = jnp.zeros((dim,), dtype=jnp.float32)
        return {'x': x, 'ln_weight': ln_weight, 'ln_bias': ln_bias, 'proj_weight': proj_weight, 'proj_bias': proj_bias}
    _L0_tok_all = _L0_tok_setup()
    _L0_tok_in = {k: v for k, v in _L0_tok_all.items() if k in ('ln_weight', 'ln_bias', 'proj_weight', 'proj_bias')}
    del _L0_tok_all

    def _L0_attn_setup():
        import jax, jax.numpy as jnp
        import numpy as np
        B, N, DIM = (16, 577, 192)
        HEADS, DIM_HEAD = (12, 64)
        INNER = HEADS * DIM_HEAD
        key = jax.random.key(seed)
        k1, k2, k3, k4 = jax.random.split(key, 4)
        x = jax.random.normal(k1, (B, N, DIM), dtype=jnp.float32)
        w_qkv = jax.random.normal(k2, (DIM, 3 * INNER), dtype=jnp.float32) * 0.02
        scale = jnp.full((HEADS,), DIM_HEAD ** (-0.5), dtype=jnp.float32)
        w_out = jax.random.normal(k3, (INNER, DIM), dtype=jnp.float32) * 0.02
        b_out = jnp.zeros((DIM,), dtype=jnp.float32)
        return {'x': x, 'w_qkv': w_qkv, 'scale': scale, 'w_out': w_out, 'b_out': b_out}
    _L0_attn_all = _L0_attn_setup()
    _L0_attn_in = {k: v for k, v in _L0_attn_all.items() if k in ('w_qkv', 'scale', 'w_out', 'b_out')}
    del _L0_attn_all

    def _L0_ffn_setup():
        import jax, jax.numpy as jnp
        import numpy as np
        D_MODEL = 192
        D_FF = 768
        N_EXPERTS = 9
        key = jax.random.key(seed)
        ks = jax.random.split(key, 7)
        scale = 0.02
        return {'x': jax.random.normal(ks[0], (2, 256, D_MODEL), jnp.float32), 'Ws': jax.random.normal(ks[1], (D_MODEL, N_EXPERTS), jnp.float32) * scale, 'bs': jnp.zeros((N_EXPERTS,), jnp.float32), 'W1': jax.random.normal(ks[2], (N_EXPERTS, D_MODEL, D_FF), jnp.float32) * scale, 'b1': jnp.zeros((N_EXPERTS, D_FF), jnp.float32), 'W2': jax.random.normal(ks[3], (N_EXPERTS, D_FF, D_MODEL), jnp.float32) * scale, 'b2': jnp.zeros((N_EXPERTS, D_MODEL), jnp.float32)}
    _L0_ffn_all = _L0_ffn_setup()
    _L0_ffn_in = {k: v for k, v in _L0_ffn_all.items() if k in ('Ws', 'bs', 'W1', 'b1', 'W2', 'b2')}
    del _L0_ffn_all
    return {'x': x, 'L0_tok_ln_weight': _L0_tok_in['ln_weight'], 'L0_tok_ln_bias': _L0_tok_in['ln_bias'], 'L0_tok_proj_weight': _L0_tok_in['proj_weight'], 'L0_tok_proj_bias': _L0_tok_in['proj_bias'], 'L0_attn_w_qkv': _L0_attn_in['w_qkv'], 'L0_attn_scale': _L0_attn_in['scale'], 'L0_attn_w_out': _L0_attn_in['w_out'], 'L0_attn_b_out': _L0_attn_in['b_out'], 'L0_ffn_Ws': _L0_ffn_in['Ws'], 'L0_ffn_bs': _L0_ffn_in['bs'], 'L0_ffn_W1': _L0_ffn_in['W1'], 'L0_ffn_b1': _L0_ffn_in['b1'], 'L0_ffn_W2': _L0_ffn_in['W2'], 'L0_ffn_b2': _L0_ffn_in['b2']}

def reference(x, L0_tok_ln_weight, L0_tok_ln_bias, L0_tok_proj_weight, L0_tok_proj_bias, L0_attn_w_qkv, L0_attn_scale, L0_attn_w_out, L0_attn_b_out, L0_ffn_Ws, L0_ffn_bs, L0_ffn_W1, L0_ffn_b1, L0_ffn_W2, L0_ffn_b2):
    import jax
    import jax.numpy as jnp

    def _L0_tok_ref(x, ln_weight, ln_bias, proj_weight, proj_bias):
        import jax, jax.numpy as jnp
        import numpy as np
        PATCH = 16

        def _shift2d(x, shift):
            l, r, t, b = shift
            H, W = (x.shape[2], x.shape[3])
            xp = jnp.pad(x, ((0, 0), (0, 0), (max(t, 0), max(b, 0)), (max(l, 0), max(r, 0))))
            h0 = max(-t, 0)
            w0 = max(-l, 0)
            return xp[:, :, h0:h0 + H, w0:w0 + W]
        shifts = ((1, -1, 0, 0), (-1, 1, 0, 0), (0, 0, 1, -1), (0, 0, -1, 1))
        xc = jnp.concatenate([x] + [_shift2d(x, s) for s in shifts], axis=1)
        B, C5, H, W = xc.shape
        p = PATCH
        h, w = (H // p, W // p)
        t = xc.reshape(B, C5, h, p, w, p)
        t = t.transpose(0, 2, 4, 3, 5, 1).reshape(B, h * w, p * p * C5)
        mu = jnp.mean(t, axis=-1, keepdims=True)
        var = jnp.mean(jnp.square(t - mu), axis=-1, keepdims=True)
        tn = (t - mu) * jax.lax.rsqrt(var + 1e-05) * ln_weight + ln_bias
        return jnp.einsum('bnk,dk->bnd', tn, proj_weight) + proj_bias

    def _L0_attn_ref(x, w_qkv, scale, w_out, b_out):
        import jax, jax.numpy as jnp
        import numpy as np
        B, N, DIM = (16, 577, 192)
        HEADS, DIM_HEAD = (12, 64)
        INNER = HEADS * DIM_HEAD
        b, n, _ = x.shape
        h = scale.shape[0]
        dh = w_qkv.shape[1] // (3 * h)
        qkv = x @ w_qkv
        q, k, v = jnp.split(qkv, 3, axis=-1)
        to_heads = lambda t: t.reshape(b, n, h, dh).transpose(0, 2, 1, 3)
        q, k, v = (to_heads(q), to_heads(k), to_heads(v))
        dots = jnp.einsum('bhid,bhjd->bhij', q, k) * scale[None, :, None, None]
        se = dots.mean(axis=1, keepdims=True)
        diag = jnp.eye(n, dtype=bool)
        neg_inf = jnp.array(-jnp.inf, dots.dtype)
        dots = jnp.where(diag, neg_inf, dots)
        top_k = int(n * 0.75)
        _, idx = jax.lax.top_k(dots, top_k)
        bi = jnp.arange(b)[:, None, None, None]
        hi = jnp.arange(h)[None, :, None, None]
        ii = jnp.arange(n)[None, None, :, None]
        keep = jnp.zeros((b, h, n, n), dtype=bool).at[bi, hi, ii, idx].set(True)
        dots = jnp.where(keep, dots, neg_inf) + se
        attn = jax.nn.softmax(dots, axis=-1)
        out = jnp.einsum('bhij,bhjd->bhid', attn, v)
        out = out.transpose(0, 2, 1, 3).reshape(b, n, h * dh)
        return out @ w_out + b_out

    def _L0_ffn_ref(x, Ws, bs, W1, b1, W2, b2):
        import jax, jax.numpy as jnp
        import numpy as np
        D_MODEL = 192
        D_FF = 768
        N_EXPERTS = 9
        B, S, d = x.shape
        xt = x.reshape(-1, d)
        route_prob = jax.nn.softmax(xt @ Ws + bs, axis=-1)
        p = jnp.max(route_prob, axis=-1)
        routes = jnp.argmax(route_prob, axis=-1)
        h = jax.nn.gelu(jnp.einsum('td,edf->tef', xt, W1) + b1, approximate=False)
        out = jnp.einsum('tef,efd->ted', h, W2) + b2
        common = out[:, 0, :]
        sel = jnp.take_along_axis(out, routes[:, None, None], axis=1)[:, 0, :]
        scaling = (p / jax.lax.stop_gradient(p))[:, None]
        pe = p[:, None]
        final = jnp.where((routes == 0)[:, None], common * scaling, pe * sel + (1.0 - pe) * common)
        return final.reshape(B, S, d)
    h = _L0_tok_ref(x, L0_tok_ln_weight, L0_tok_ln_bias, L0_tok_proj_weight, L0_tok_proj_bias)
    h = h + _L0_attn_ref(_layernorm(h, axis=-1), L0_attn_w_qkv, L0_attn_scale, L0_attn_w_out, L0_attn_b_out)
    h = h + _L0_ffn_ref(_layernorm(h, axis=-1), L0_ffn_Ws, L0_ffn_bs, L0_ffn_W1, L0_ffn_b1, L0_ffn_W2, L0_ffn_b2)
    return h

_drawn_inputs = setup_inputs


def setup_inputs(seed=0):
    import zlib

    import numpy as np

    out = dict(_drawn_inputs(seed))
    spreads = {'L0_tok_ln_weight': (1.0, 0.2),
     'L0_tok_ln_bias': (0.0, 0.1),
     'L0_tok_proj_bias': (0.0, 0.1),
     'L0_attn_scale': (0.125, 0.6),
     'L0_attn_b_out': (0.0, 0.1),
     'L0_ffn_bs': (0.0, 0.596),
     'L0_ffn_b1': (0.0, 0.338),
     'L0_ffn_b2': (0.0, 0.1)}
    factors = {'L0_ffn_Ws': 2.854}
    for name, (base, spread) in spreads.items():
        noise = np.random.default_rng([zlib.crc32(name.encode()), seed]).standard_normal(out[name].shape)
        drawn = base * np.exp(spread * noise) if base else spread * noise
        out[name] = jnp.asarray(drawn.astype(out[name].dtype))
    for name, factor in factors.items():
        out[name] = (out[name] * factor).astype(out[name].dtype)
    return out
```

```python
import numpy as np
import concourse.bass as bass
from concourse import mybir
from contextlib import ExitStack

B, C, IMG, PATCH, SIDE = 16, 3, 96, 16, 6
N = SIDE * SIDE
TOK = B * N
D = 192
DH = D // 2
XL = 8
PIX = C * PATCH * 2
HALO = 4 * C * PATCH // XL
ROWS = PIX + HALO
SHIFTS = 5
PATCH_DIM = PATCH * PATCH * C * SHIFTS
HEADS, HD = 12, 64
INNER = HEADS * HD
HP = HEADS // 2
KEEP = int(N * 0.75)
assert N - 1 - KEEP == 8
PAIRS = B // 2
PT = 2 * N
EXP, FF = 9, 768
FM = FF // 128
P = 128
TT = (TOK + P - 1) // P
SEL = TOK // P + (EXP - 1)
BIG = 1e30
EPS = 1e-5


PROJ_BANK = (4, 5, 6, 1, 4)


def rows(t):
    return min(P, TOK - t * P)


CONST = {}
_at = 0
for _n, _w in (("ident", P), ("upper", P), ("diag", N), ("diag_out", N), ("tri", 64), ("iota", EXP),
               ("steps", 40), ("tile", SEL), ("spare", TT), ("count", XL)):
    CONST[_n] = (_at, _at + _w)
    _at += _w
CONST_W = _at


def constants():
    t = np.zeros((P, CONST_W), np.float32)

    def col(n):
        return t[:, CONST[n][0]:CONST[n][1]]

    col("ident")[:] = np.eye(P)
    col("upper")[:] = np.triu(np.ones((P, P)), 1)
    for p in range(P):
        if p % 64 < N:
            col("diag")[p, p % 64] = -BIG
            col("diag_out")[p, N - 1 - p % 64] = -3 * BIG
    col("tri")[:] = np.tril(np.ones((8, 8))).reshape(-1)
    col("iota")[:] = np.arange(EXP)
    col("steps")[:] = np.tile(np.arange(5) * P, 8)
    col("tile")[:] = np.arange(SEL)
    col("spare")[:] = SEL * P + np.arange(P)[:, None] + P * np.arange(TT)
    cnt = np.ones((C, PATCH, PATCH))
    cnt[:, :, 1:] += 1
    cnt[:, :, :-1] += 1
    cnt[:, 1:, :] += 1
    cnt[:, :-1, :] += 1
    col("count")[:PIX] = cnt.reshape(PIX, XL)
    col("count")[PIX:ROWS] = 1
    return t


def build(nc, xk, pk, ph, lnw, lnb, pb, wqkv, scale, wout, bout, ws, bs, w1, b1, w2, b2, b1c, consts, out):
    fp32 = mybir.dt.float32
    u32 = mybir.dt.uint32
    i32 = mybir.dt.int32
    ALU = mybir.AluOpType
    ACT = mybir.ActivationFunctionType
    AX = mybir.AxisListType

    xg_dram = nc.dram_tensor("xg_scratch", (SEL * P + TT * P, D), fp32).ap()
    yg_dram = nc.dram_tensor("yg_scratch", (SEL * P, D), fp32).ap()

    with ExitStack() as ctx:
        def sb(name, shape, dt=fp32):
            return ctx.enter_context(nc.sbuf_tensor(name, shape, dt))

        def sem(name):
            return ctx.enter_context(nc.semaphore(name))

        A_W = 2 * EXP * FF + EXP * FM * D
        region = sb("region", [P, A_W])
        at = 0

        def take(width, shape, **kw):
            nonlocal at
            v = region[:, at:at + width].rearrange(shape, **kw)
            at += width
            return v
        xs = take(XL * TOK, "p (s n) -> p s n", s=XL)
        xc = take(XL * TOK, "p (s n) -> p s n", s=XL)
        pw = take(SHIFTS * XL * D, "p (f s d) -> p f s d", f=SHIFTS, s=XL)
        weff = take(XL * D, "p (s d) -> p s d", s=XL)
        sq = take(XL * TOK, "p (s n) -> p s n", s=XL)
        assert at <= A_W, (at, A_W)
        w1a = region[:, 0:EXP * FF].rearrange("p (e f) -> p e f", e=EXP)
        w1b = region[:, EXP * FF:2 * EXP * FF].rearrange("p (e f) -> p e f", e=EXP)
        w2s = region[:, 2 * EXP * FF:A_W].rearrange("p (e m d) -> p e m d", e=EXP, m=FM)

        cst = sb("cst", [P, CONST_W])

        def const(n, p0=0, p1=P):
            return cst[p0:p1, CONST[n][0]:CONST[n][1]]
        ones = sb("ones", [P, P])
        half = sb("half", [P, 1])
        lnw_s = sb("lnw_s", [P, SHIFTS * XL])
        lnb_s = sb("lnb_s", [P, SHIFTS * XL])
        rowv = sb("rowv", [1, 3 * D + EXP])
        wq_s = sb("wq_s", [DH, 2, 3 * INNER])
        wo_s = sb("wo_s", [P, HP, D])
        ws_s = sb("ws_s", [DH, 2, EXP])
        b2_s = sb("b2_s", [EXP, D])
        b1_s = sb("b1_s", [P, FM])
        scq = sb("scq", [P, HP])
        bias = sb("bias", [P, D])
        var = sb("var", [P, TT, 1])
        rs = sb("rs", [P, TT, 1])
        h = sb("h", [P, TT, D])
        hn = sb("hn", [P, TT, D])
        st = sb("st", [P, TT, 6])
        mv = sb("mv", [P, TT, 2])
        ve = sb("ve", [P, TT, 1])
        rl = sb("rl", [P, TT, 1])
        hnT = sb("hnT", [DH, 2, TOK + PT])
        xnT = hnT
        oT = sb("oT", [P, HP, TOK])
        hcT = oT[:, :, :]

        work = sb("work", [P, 7300])
        at = 0

        def take2(width, shape, **kw):
            nonlocal at
            v = work[:, at:at + width].rearrange(shape, **kw)
            at += width
            return v
        hc = [take2(2 * P, "p (k b n) -> p k b n", k=2, b=2)[0:DH] for _ in range(2)]
        qT = [take2(HP * P, "p (m b n) -> p m b n", m=HP, b=2) for _ in range(2)]
        kT = [take2(HP * PT, "p (m b n) -> p m b n", m=HP, b=2) for _ in range(2)]
        vv = [take2(INNER, "p (h d) -> p h d", h=HEADS) for _ in range(2)]
        dd = [take2(HEADS * N, "p (h n) -> p h n", h=HEADS) for _ in range(2)]
        rr = [take2(HEADS * N, "p (h n) -> p h n", h=HEADS) for _ in range(2)]
        pT = take2(HEADS * PT, "p (h b n) -> p h b n", h=HEADS, b=2)
        mx = take2(HEADS * 8, "p (h n) -> p h n", h=HEADS)
        se = take2(N, "p (h n) -> p h n", h=1)
        rowm = take2(HEADS, "p (h n) -> p h n", h=HEADS)
        sums = take2(HEADS, "p (h n) -> p h n", h=HEADS)
        inv = take2(HEADS, "p (h n) -> p h n", h=HEADS)
        pblk = [sb(f"pblk{i}", [P, HEADS, P]) for i in range(2)]

        at = 0
        xg = [take2(D, "p (a d) -> p a d", a=1) for _ in range(2)]
        xT = [take2(2 * P, "p (k n) -> p k n", k=2) for _ in range(2)]
        hs = [take2(FF, "p (m n) -> p m n", m=FM) for _ in range(2)]
        hT = [take2(FF, "p (m n) -> p m n", m=FM) for _ in range(2)]
        ys = [take2(D, "p (a d) -> p a d", a=1) for _ in range(2)]
        acc = take2(TT * D, "p (t d) -> p t d", t=TT)
        yg = take2(TT * D, "p (t d) -> p t d", t=TT)
        cT = take2(TT * P, "p (t n) -> p t n", t=TT)

        lg = sb("lg", [P, TT, EXP])
        le = sb("le", [P, TT, EXP])
        lm = sb("lm", [P, TT, 1])
        ls = sb("ls", [P, TT, 1])
        pr = sb("pr", [P, TT, 1])
        mx8 = sb("mx8", [P, TT, 8])
        ix8 = sb("ix8", [P, TT, 8], u32)
        ixf = sb("ixf", [P, TT, 1])
        oh = sb("oh", [P, TT, EXP])
        routed = sb("routed", [P, TT, 1])
        pe_w = sb("pe_w", [P, TT, 1])
        ome = sb("ome", [P, TT, 1])
        cmix = sb("cmix", [P, TT, EXP])
        over = sb("over", [P, 8, 5])
        ntile = sb("ntile", [P, 8, 1])
        prod = sb("prod", [P, 8, 8])
        cum = sb("cum", [P, 8, 1])
        base = sb("base", [P, 1, 8])
        rb = sb("rb", [P, TT, 8])
        rb2 = sb("rb2", [P, TT, 8])
        slot = sb("slot", [P, TT, 1])
        spare = sb("spare", [P, TT, 1])
        slot_s = sb("slot_s", [P, TT, 1])
        idx_s = sb("idx_s", [P, TT], u32)
        idx_g = sb("idx_g", [P, TT], u32)
        tge = sb("tge", [1, SEL, 8])
        tex = sb("tex", [1, SEL, 1])
        tex2 = sb("tex2", [1, SEL, 1])
        texi = sb("texi", [1, SEL], i32)
        nsum = sb("nsum", [P, 8, 1])

        ps = ctx.enter_context(nc.psum_tensor("ps", [P, 8, 512], fp32))

        x_in, lnw_in, cst_in, ph_in, wq_in, wo_in, small_in = (sem(f"{n}_in") for n in (
            "x", "lnw", "cst", "halo_w", "wqkv", "wout", "small"))
        pw_in = [sem(f"pw_in{f}") for f in range(SHIFTS)]
        w1_in, w2_in, wc_in = sem("w1_in"), sem("w2_in"), sem("common_w_in")
        set_up, pads = sem("ones_set"), sem("pads_zeroed")
        mean_mm, xc_done, sq_done, var_mm, bias_mm, bias_ev = (sem(n) for n in (
            "mean_mm", "centred", "squared", "var_mm", "bias_mm", "bias_ev"))
        fold, first_w, var_ev, rs_done, proj_mm = (sem(n) for n in (
            "folded", "fold_first", "var_ev", "rstd_done", "proj_mm"))
        h_done = sem("h_done")
        ln_chain, ve_done, rl_done, hn_done, hT_mm, hT_ev = (sem(n) for n in (
            "ln_chain", "ln_var", "ln_rstd", "hn_done", "hnT_mm", "hnT_ev"))
        hc_ev, q_mm, k_mm, v_mm, s_mm, t_mm, av_mm = (sem(n) for n in (
            "pair_tokens", "q_mm", "k_mm", "v_mm", "s_mm", "pT_mm", "av_mm"))
        q_ev, k_ev, v_ev, d_ev, t_ev, o_ev = (sem(n) for n in (
            "q_ev", "k_ev", "v_ev", "dots_ev", "pT_ev", "oT_ev"))
        top8, dropped, se_sum, se_done, logit, rmax, shifted, expd, summed, invd, probs = (sem(n) for n in (
            "top8", "dropped", "se_sum", "se_done", "logits_ready", "row_max", "shifted", "exp_done",
            "row_sum", "row_inv", "probs_ready"))
        zeros_out = sem("zero_rows_written")
        om_mm, h2_done, lg_mm, lg_ev, le_exp, route, oh_done, rank_mm, cm_done, cT_mm, cT_ev = (
            sem(n) for n in ("out_mm", "h2_done", "router_mm", "router_ev", "router_exp", "route",
                             "onehot", "rank_mm", "mix_done", "mixT_mm", "mixT_ev"))
        sexp_in, lsub, dispatch, slots_done, texp_done, scattered = (sem(n) for n in (
            "sexp_in", "lsub", "dispatch", "slots_done", "tile_expert", "scattered"))
        c1_mm, c1_ev, c2_mm, b2_mm, acc_a, acc_b = (sem(n) for n in (
            "common1_mm", "common1_ev", "common2_mm", "b2_mm", "acc_a", "acc_b"))
        xg_in = [sem(f"xg_in{i}") for i in range(2)]
        ys_out = [sem(f"ys_out{i}") for i in range(2)]
        xT_mm, xT_ev, f1_mm, f1_ev, f2T_mm, f2T_ev, f2_mm, y_ev = (sem(n) for n in (
            "xT_mm", "xT_ev", "up_mm", "gelu_done", "hT_mm", "hT_ev2", "down_mm", "y_ev"))
        yg_in = [sem(f"yg_in{t}") for t in range(TT)]
        fin, stored = sem("final"), sem("stored")

        def wait(eng, s, n):
            if not isinstance(n, int) or n > 0:
                eng.wait_ge(s, n)

        block = ctx.enter_context(nc.Block())

        @block.sync
        def _(sp):
            sp.dma_start(xs[0:ROWS], xk).then_inc(x_in, 16)
            sp.dma_start(cst[:, :], consts).then_inc(cst_in, 16)
            sp.dma_start(lnw_s[0:ROWS], lnw).then_inc(lnw_in, 16)
            sp.dma_start(lnb_s[0:ROWS], lnb).then_inc(lnw_in, 16)
            for f in range(SHIFTS):
                sp.dma_start(pw[0:PIX, f], pk[:, f]).then_inc(pw_in[f], 16)
                if f == 0:
                    sp.dma_start(pw[PIX:ROWS, 0], ph).then_inc(ph_in, 16)
            sp.dma_start(rowv[0:1, 0:D], pb).then_inc(small_in, 16)
            sp.dma_start(rowv[0:1, D:2 * D], bout).then_inc(small_in, 16)
            sp.dma_start(rowv[0:1, 3 * D:], bs).then_inc(small_in, 16)
            sp.dma_start(scq[:, :], scale).then_inc(small_in, 16)
            sp.dma_start(ws_s[:, :, :], ws).then_inc(small_in, 16)
            sp.dma_start(b2_s[:, :], b2).then_inc(small_in, 16)
            sp.dma_start(b1_s[:, :], b1c).then_inc(small_in, 16)
            sp.dma_start(wq_s[:, :, :], wqkv).then_inc(wq_in, 16)
            sp.dma_start(wo_s[:, :, :], wout).then_inc(wo_in, 16)
            sp.wait_ge(pads, 2)
            zero = pblk[0][:, :, :].rearrange("p h n -> p (h n)")[:, 0:SEL // 2 * D]
            for i in range(2):
                half_rows = SEL * P // 2
                sp.dma_start(xg_dram[i * half_rows:(i + 1) * half_rows, :]
                             .rearrange("(p a) d -> p (a d)", p=P), zero).then_inc(zeros_out, 16)
            sp.wait_ge(proj_mm, TT)
            sp.dma_start(w1a[0:DH, 0], w1[0:DH, 0]).then_inc(wc_in, 16)
            sp.dma_start(w1b[0:DH, 0], w1[DH:D, 0]).then_inc(wc_in, 16)
            sp.dma_start(w2s[:, 0], w2[:, 0]).then_inc(wc_in, 16)
            sp.dma_start(w1a[0:DH, 1:EXP], w1[0:DH, 1:EXP]).then_inc(w1_in, 16)
            sp.dma_start(w1b[0:DH, 1:EXP], w1[DH:D, 1:EXP]).then_inc(w1_in, 16)
            sp.dma_start(w1b[DH:DH + 1, :], b1).then_inc(w1_in, 16)
            sp.dma_start(w2s[:, 1:EXP], w2[:, 1:EXP]).then_inc(w2_in, 16)

            sp.wait_ge(scattered, 16 * TT)

            def load_tile(s, par):
                wait(sp, xT_mm, s - 1)
                sp.dma_start(xg[par][:, 0, :], xg_dram[bass.ds(s * P, P), :]).then_inc(xg_in[par], 16)
            load_tile(0, 0)
            load_tile(1, 1)
            with sp.Fori(1, SEL // 2) as i:
                for par in range(2):
                    load_tile(2 * i + par, par)
            for t in range(TT):
                sp.wait_ge(fin, t + 1)
                sp.dma_start(out[t * P:t * P + rows(t), :], acc[0:rows(t), t, :]).then_inc(stored, 16)
            sp.wait_ge(stored, 16 * TT)

        @block.tensor
        def _(pe):
            pe.wait_ge(x_in, 16)
            pe.wait_ge(cst_in, 16)
            cnt = const("count", 0, ROWS)
            for half_ in range(2):
                for s in range(XL):
                    mm = nc.tensor.matmul(ps[0:ROWS, half_, 0:288], cnt[:, s:s + 1].broadcast_to([ROWS, ROWS]),
                                          xs[0:ROWS, s, half_ * 288:half_ * 288 + 288],
                                          start=(s == 0), stop=(s == XL - 1))
                mm.then_inc(mean_mm, 1)
            pe.wait_ge(lnw_in, 32)
            pe.wait_ge(set_up, 2)
            for f in range(SHIFTS):
                pe.wait_ge(pw_in[f], 16)
                if f == 0:
                    pe.wait_ge(ph_in, 16)
                n = ROWS if f == 0 else PIX
                for s in range(XL):
                    nc.tensor.matmul(ps[:, 2, 0:D], lnb_s[0:n, f * XL + s:f * XL + s + 1].broadcast_to([n, P]),
                                     pw[0:n, f, s, :], start=(f == 0 and s == 0), stop=False)
            pe.wait_ge(small_in, 16 * 7)
            nc.tensor.matmul(ps[:, 2, 0:D], ones[0:1, :], rowv[0:1, 0:D], start=False, stop=True)\
                .then_inc(bias_mm, 1)
            for s in range(XL):
                pe.wait_ge(sq_done, s + 1)
                for t in range(TT):
                    mm = nc.tensor.matmul(ps[0:rows(t), 3, t * XL + s:t * XL + s + 1],
                                          sq[0:ROWS, s, t * P:t * P + rows(t)], cnt[:, s:s + 1],
                                          start=True, stop=True)
                mm.then_inc(var_mm, 1)
            pe.wait_ge(xc_done, 2)
            pe.wait_ge(fold, SHIFTS - 1)

            def transposes(t, ready, bank):
                pe.wait_ge(hn_done, ready)
                for k in range(2):
                    mm = nc.tensor.transpose(ps[0:DH, bank, k * P:k * P + rows(t)],
                                             hn[0:rows(t), t, k * DH:(k + 1) * DH],
                                             const("ident", 0, rows(t))[:, 0:rows(t)])
                mm.then_inc(hT_mm, 1)
            for t in range(TT):
                if t == 4:
                    pe.wait_ge(h_done, 1)
                for s in range(XL):
                    mm = nc.tensor.matmul(ps[0:rows(t), PROJ_BANK[t], 0:D],
                                          xc[0:ROWS, s, t * P:t * P + rows(t)], weff[0:ROWS, s, :],
                                          start=(s == 0), stop=(s == XL - 1))
                mm.then_inc(proj_mm, 1)
                if t >= 2:
                    if t == 4:
                        pe.wait_ge(hT_ev, 1)
                    transposes(t - 2, t - 1, (7, 0)[t % 2])
            for t in (3, 4):
                pe.wait_ge(hT_ev, t - 1)
                transposes(t, t + 1, (7, 0)[t % 2])

            pe.wait_ge(wq_in, 16)

            def qk(s, par):
                pe.wait_ge(hc_ev, s + 1)
                for which, ev, mm_sem in ((0, q_ev, q_mm), (1, k_ev, k_mm)):
                    wait(pe, ev, s)
                    for m in range(HP):
                        for k in range(2):
                            mm = nc.tensor.matmul(ps[:, which, m * PT:(m + 1) * PT],
                                                  wq_s[:, k, which * INNER + m * P:which * INNER + (m + 1) * P],
                                                  hc[par][:, k, :, 0:N], start=(k == 0), stop=(k == 1))
                    mm.then_inc(mm_sem, 1)

            def probs_T(s, par, values_before):
                pe.wait_ge(probs, 2 * s + 2)
                pe.wait_ge(v_ev, values_before)
                wait(pe, t_ev, 3 * s)
                for c in range(3):
                    if c == 2:
                        pe.wait_ge(t_ev, 3 * s + 1)
                    for g in range(4):
                        mm = nc.tensor.transpose(ps[:, 2 + c % 2, g * P:(g + 1) * P],
                                                 pblk[par][:, 4 * c + g, :], const("ident"))
                    mm.then_inc(t_mm, 1)

            def av(s, par):
                wait(pe, o_ev, s)
                pe.wait_ge(t_ev, 3 * s + 3)
                for g in range(HEADS):
                    odd, m = g // HP, g % HP
                    mm = nc.tensor.matmul(ps[64 * odd:64 * odd + 64, 6, m * PT:(m + 1) * PT],
                                          vv[par][:, 2 * m + odd, :], pT[:, g, :, :], start=True, stop=True)
                mm.then_inc(av_mm, 1)

            def values(s, par):
                wait(pe, v_ev, s)
                for c in range(2):
                    for k in range(2):
                        if c == 1 and k == 1:
                            pe.wait_ge(q_ev, s + 1)
                            pe.wait_ge(k_ev, s + 1)
                            wait(pe, d_ev, 2 * s)
                        mm = nc.tensor.matmul(ps[:, 2 + c, 0:384], hc[par][:, k, :, :],
                                              wq_s[:, k, 2 * INNER + c * 384:2 * INNER + (c + 1) * 384],
                                              start=(k == 0), stop=(k == 1))
                mm.then_inc(v_mm, 1)

            def dots(s, par):
                for m in range(HP):
                    for odd in range(2):
                        o = 64 * odd
                        for b in range(2):
                            mm = nc.tensor.matmul(ps[64 * b:64 * b + 64, 4 + odd, m * N:(m + 1) * N],
                                                  qT[par][o:o + 64, m, b, :], kT[par][o:o + 64, m, b, :],
                                                  start=True, stop=True)
                mm.then_inc(s_mm, 1)

            def pair(s, par):
                qk(s, par)
                if not isinstance(s, int) or s >= 2:
                    probs_T(s - 2, par, s)
                    av(s - 2, par)
                values(s, par)
                dots(s, par)
            for s in range(4):
                pair(s, s % 2)
            with pe.Fori(2, PAIRS // 2) as i:
                for par in range(2):
                    pair(2 * i + par, par)
            for s in (PAIRS - 2, PAIRS - 1):
                probs_T(s, s % 2, PAIRS)
                av(s, s % 2)

            pe.wait_ge(wo_in, 16)
            pe.wait_ge(o_ev, PAIRS)

            def out_proj(t):
                wait(pe, h2_done, t - 1)
                for m in range(HP):
                    nc.tensor.matmul(ps[0:rows(t), t % 2, 0:D], oT[:, m, t * P:t * P + rows(t)],
                                     wo_s[:, m, :], start=(m == 0), stop=False)
                nc.tensor.matmul(ps[0:rows(t), t % 2, 0:D], ones[0:1, 0:rows(t)], rowv[0:1, D:2 * D],
                                 start=False, stop=True).then_inc(om_mm, 1)

            def router(t):
                pe.wait_ge(hT_ev, TT + t + 1)
                for k in range(2):
                    nc.tensor.matmul(ps[0:rows(t), 7, t * EXP:(t + 1) * EXP],
                                     xnT[:, k, t * P:t * P + rows(t)], ws_s[:, k, :],
                                     start=(k == 0), stop=False)
                nc.tensor.matmul(ps[0:rows(t), 7, t * EXP:(t + 1) * EXP], ones[0:1, 0:rows(t)],
                                 rowv[0:1, 3 * D:], start=False, stop=True).then_inc(lg_mm, 1)
            for t in range(TT):
                out_proj(t)
                if t >= 2:
                    if t >= 4:
                        pe.wait_ge(hT_ev, TT + t - 3)
                    transposes(t - 2, TT + t - 1, 2 + t % 2)
            for t in (3, 4):
                pe.wait_ge(hT_ev, TT + t - 1)
                transposes(t, TT + t + 1, 2 + t % 2)
            for t in range(TT):
                router(t)

            pe.wait_ge(wc_in, 48)
            for m in range(FM):
                if m >= 2:
                    pe.wait_ge(c1_ev, m - 1)
                else:
                    pe.wait_ge(hT_ev, 2 * TT)
                for half_ in range(2):
                    for k, w in enumerate((w1a, w1b)):
                        mm = nc.tensor.matmul(ps[:, m % 2 * 2 + half_, 0:288], w[0:DH, 0, m * P:(m + 1) * P],
                                              xnT[:, k, half_ * 288:half_ * 288 + 288],
                                              start=(k == 0), stop=(k == 1))
                mm.then_inc(c1_mm, 1)
                if m == 3:
                    pe.wait_ge(oh_done, 1)
                    for t in range(TT):
                        nc.tensor.matmul(ps[:, 6, t * 8:t * 8 + 8], const("upper"), oh[:, t, 1:EXP],
                                         start=True, stop=(t == 0))
                        for u in range(t):
                            nc.tensor.matmul(ps[:, 6, t * 8:t * 8 + 8], ones[:, :], oh[:, u, 1:EXP],
                                             start=False, stop=(u == t - 1))
                    for u in range(TT):
                        mm = nc.tensor.matmul(ps[:, 6, TT * 8:TT * 8 + 8], ones[:, :], oh[:, u, 1:EXP],
                                              start=(u == 0), stop=(u == TT - 1))
                    mm.then_inc(rank_mm, 1)
            pe.wait_ge(cm_done, 2)
            for t in range(TT):
                mm = nc.tensor.transpose(ps[0:EXP, (7 if t < 4 else 5), t % 4 * P:t % 4 * P + P], cmix[:, t, :], const("ident"))
            mm.then_inc(cT_mm, 1)
            pe.wait_ge(c1_ev, FM)
            for t in range(TT):
                if t >= 2:
                    pe.wait_ge(acc_a, t - 1)
                    pe.wait_ge(acc_b, t - 1)
                for m in range(FM):
                    mm = nc.tensor.matmul(ps[0:rows(t), t % 2, 0:D], hcT[:, m, t * P:t * P + rows(t)],
                                          w2s[:, 0, m, :], start=(m == 0), stop=(m == FM - 1))
                mm.then_inc(c2_mm, 1)
                if t == 0:
                    pe.wait_ge(cT_ev, 2)
                nc.tensor.matmul(ps[0:rows(t), 2 + t % 2, 0:D], cT[0:EXP, t, 0:rows(t)], b2_s[:, :],
                                 start=True, stop=True).then_inc(b2_mm, 1)

            pe.wait_ge(texp_done, 1)
            pe.wait_ge(w1_in, 48)
            pe.wait_ge(w2_in, 16)
            pe.wait_ge(acc_b, TT)

            def tile_T(s, par):
                pe.wait_ge(xg_in[par], (s // 2 + 1) * 16 if isinstance(s, int) else (s - par) * 8 + 16)
                wait(pe, xT_ev, s - 1)
                for k in range(2):
                    mm = nc.tensor.transpose(ps[0:DH, (4, 7)[par], k * P:(k + 1) * P],
                                             xg[par][:, 0, k * DH:(k + 1) * DH], const("ident"))
                mm.then_inc(xT_mm, 1)

            def up(s, par):
                e = pe.value_load(texi[0:1, bass.ds(s, 1)], min_val=1, max_val=EXP - 1)
                pe.wait_ge(xT_ev, s + 1)
                wait(pe, f1_ev, s)
                for c in range(2):
                    nc.tensor.matmul(ps[:, c, 0:384], xT[par][0:DH, 0, :],
                                     w1a[0:DH, bass.ds(e, 1), c * 384:(c + 1) * 384], start=True, stop=False)
                    mm = nc.tensor.matmul(ps[:, c, 0:384], xT[par][0:DH + 1, 1, :],
                                          w1b[0:DH + 1, bass.ds(e, 1), c * 384:(c + 1) * 384],
                                          start=False, stop=True)
                mm.then_inc(f1_mm, 1)

            def hidden_T(s, par):
                pe.wait_ge(f1_ev, s + 1)
                wait(pe, f2T_ev, s)
                for m in range(FM):
                    mm = nc.tensor.transpose(ps[:, 2 + m // 3, m % 3 * P:(m % 3 + 1) * P], hs[par][:, m, :],
                                             const("ident"))
                mm.then_inc(f2T_mm, 1)

            def down(s, par):
                e = pe.value_load(texi[0:1, bass.ds(s, 1)], min_val=1, max_val=EXP - 1)
                pe.wait_ge(f2T_ev, s + 1)
                wait(pe, y_ev, s - 1)
                for m in range(FM):
                    mm = nc.tensor.matmul(ps[:, 5 + par, 0:D], hT[par][:, m, :], w2s[:, bass.ds(e, 1), m, :],
                                          start=(m == 0), stop=(m == FM - 1))
                mm.then_inc(f2_mm, 1)

            def step(s, par):
                up(s + 1, 1 - par)
                tile_T(s + 2, par)
                down(s - 1, 1 - par)
                hidden_T(s, par)
            tile_T(0, 0)
            up(0, 0)
            tile_T(1, 1)
            up(1, 1)
            tile_T(2, 0)
            hidden_T(0, 0)
            step(1, 1)
            step(2, 0)
            with pe.Fori(1, (SEL - 4) // 2) as i:
                step(2 * i + 1, 1)
                step(2 * i + 2, 0)
            s = SEL - 3
            step(s, 1)
            s = SEL - 2
            up(s + 1, 1)
            down(s - 1, 1)
            hidden_T(s, 0)
            down(s, 0)
            hidden_T(s + 1, 1)
            down(s + 1, 1)

        @block.vector
        def _(dve):
            nc.vector.memset(ones[:, :], 1.0).then_inc(set_up, 1)
            nc.vector.memset(half[:, :], -0.5).then_inc(set_up, 1)
            for i in range(2):
                nc.vector.memset(pblk[i][:, :, :], 0.0).then_inc(pads, 1)
            for i in range(2):
                nc.vector.memset(hc[i], 0.0)
                last = nc.vector.memset(qT[i], 0.0)
            last.then_inc(pads, 1)
            nc.vector.memset(hnT[:, :, TOK:], 0.0)
            nc.vector.memset(lg[:, :, :], 0.0).then_inc(pads, 1)
            dve.wait_ge(x_in, 16)
            for half_ in range(2):
                dve.wait_ge(mean_mm, half_ + 1)
                c0 = half_ * 288
                nc.vector.scalar_tensor_tensor(
                    out=xc[0:ROWS, :, c0:c0 + 288],
                    in0=ps[0:ROWS, half_:half_ + 1, 0:288].broadcast_to([ROWS, XL, 288]),
                    scalar=-1.0 / PATCH_DIM, in1=xs[0:ROWS, :, c0:c0 + 288], op0=ALU.mult, op1=ALU.add)\
                    .then_inc(xc_done, 1)
            dve.wait_ge(first_w, XL)
            for f in range(1, SHIFTS):
                dve.wait_ge(pw_in[f], 16)
                if f > 1:
                    dve.wait_ge(fold, f - 1)
                for s in range(XL):
                    c = f * XL + s
                    ins = nc.vector.scalar_tensor_tensor(
                        out=weff[0:PIX, s, :], in0=pw[0:PIX, f, s, :], scalar=lnw_s[0:PIX, c:c + 1],
                        in1=weff[0:PIX, s, :], op0=ALU.mult, op1=ALU.add)
                ins.then_inc(fold, 1)
            dve.wait_ge(bias_mm, 1)
            nc.vector.tensor_copy(bias[:, :], ps[:, 2, 0:D]).then_inc(bias_ev, 1)
            dve.wait_ge(var_mm, XL)
            nc.vector.tensor_reduce(var[:, 0:4, :], ps[:, 3, 0:4 * XL].rearrange("p (t s) -> p t s", s=XL),
                                    axis=AX.X, op=ALU.add)
            nc.vector.tensor_reduce(var[0:64, 4:5, :],
                                    ps[0:64, 3, 4 * XL:5 * XL].rearrange("p (t s) -> p t s", s=XL),
                                    axis=AX.X, op=ALU.add).then_inc(ln_chain, 1)
            dve.wait_ge(ln_chain, 1)
            nc.vector.tensor_scalar(var[:, 0:4, :], var[:, 0:4, :], 1.0 / PATCH_DIM, EPS, ALU.mult, ALU.add)
            nc.vector.tensor_scalar(var[0:64, 4:5, :], var[0:64, 4:5, :], 1.0 / PATCH_DIM, EPS,
                                    ALU.mult, ALU.add).then_inc(var_ev, 1)
            dve.wait_ge(rs_done, 2)
            chain = 1

            def norm(t, which, chain):
                n = rows(t)
                nc.vector.bn_stats(st[0:n, t, :], h[0:n, t, :]).then_inc(ln_chain, 1)
                dve.wait_ge(ln_chain, chain + 1)
                nc.vector.bn_aggr(mv[0:n, t, :], st[0:n, t, :]).then_inc(ln_chain, 1)
                dve.wait_ge(ln_chain, chain + 2)
                nc.vector.tensor_scalar(ve[0:n, t, :], mv[0:n, t, 1:2], EPS, None, ALU.add)\
                    .then_inc(ve_done, 1)
                return chain + 2

            def normed(t, which):
                n = rows(t)
                dve.wait_ge(rl_done, which * TT + t + 1)
                nc.vector.tensor_scalar(hn[0:n, t, :], h[0:n, t, :], mv[0:n, t, 0:1], rl[0:n, t, :],
                                        ALU.subtract, ALU.mult).then_inc(hn_done, 1)
            dve.wait_ge(bias_ev, 1)
            for t in range(TT):
                n = rows(t)
                dve.wait_ge(proj_mm, t + 1)
                nc.vector.scalar_tensor_tensor(out=h[0:n, t, :], in0=ps[0:n, PROJ_BANK[t], 0:D],
                                               scalar=rs[0:n, t, :], in1=bias[0:n, :], op0=ALU.mult,
                                               op1=ALU.add).then_inc(h_done, 1)
                dve.wait_ge(h_done, t + 1)
                chain = norm(t, 0, chain)
                if t >= 1:
                    normed(t - 1, 0)
            normed(TT - 1, 0)

            dve.wait_ge(small_in, 16 * 7)

            def q_out(s, par):
                dve.wait_ge(q_mm, s + 1)
                wait(dve, s_mm, s - 1)
                nc.vector.tensor_tensor(out=qT[par][:, :, :, 0:N],
                                        in0=ps[:, 0, 0:HP * PT].rearrange("p (m b n) -> p m b n", m=HP, b=2),
                                        in1=scq[:, :].unsqueeze(2).unsqueeze(3).broadcast_to([P, HP, 2, N]),
                                        op=ALU.mult).then_inc(q_ev, 1)

            def selection(s, par):
                dve.wait_ge(s_mm, s + 1)
                wait(dve, probs, 2 * s - 2)
                for odd in range(2):
                    nc.vector.scalar_tensor_tensor(
                        out=dd[par][:, odd * HP:(odd + 1) * HP, ::-1],
                        in0=ps[:, 4 + odd, 0:HP * N].rearrange("p (m n) -> p m n", m=HP), scalar=-1.0,
                        in1=const("diag").unsqueeze(1).broadcast_to([P, HP, N]), op0=ALU.mult, op1=ALU.add)\
                        .then_inc(d_ev, 1)
                dve.wait_ge(d_ev, 2 * s + 2)
                nc.vector.tensor_reduce(se[:, 0, :], dd[par].rearrange("p h n -> p n h"), axis=AX.X,
                                        op=ALU.add).then_inc(se_sum, 1)
                for g in range(HEADS):
                    ins = nc.vector.max(out=mx[:, g, :], in_=dd[par][:, g, :])
                ins.then_inc(top8, 1)
                dve.wait_ge(se_sum, s + 1)
                dve.wait_ge(top8, s + 1)
                nc.vector.scalar_tensor_tensor(out=se[:, 0, :], in0=se[:, 0, :], scalar=-1.0 / HEADS,
                                               in1=const("diag_out"), op0=ALU.mult, op1=ALU.add)\
                    .then_inc(se_done, 1)
                for g in range(HEADS):
                    ins = nc.vector.match_replace(out=rr[par][:, g, :], in_to_replace=mx[:, g, :],
                                                  in_values=dd[par][:, g, :], imm_value=BIG)
                ins.then_inc(dropped, 1)

            def softmax(s, par):
                dve.wait_ge(logit, s + 1)
                nc.vector.tensor_reduce(rowm[:, :, 0:1], rr[par], axis=AX.X, op=ALU.max).then_inc(rmax, 1)
                dve.wait_ge(rmax, s + 1)
                nc.vector.tensor_tensor(out=rr[par], in0=rr[par], in1=rowm.broadcast_to([P, HEADS, N]),
                                        op=ALU.subtract).then_inc(shifted, 1)
                dve.wait_ge(expd, s + 1)
                nc.vector.tensor_reduce(sums[:, :, 0:1], dd[par], axis=AX.X, op=ALU.add).then_inc(summed, 1)
                dve.wait_ge(summed, s + 1)
                wait(dve, probs, 2 * s)
                nc.vector.reciprocal(inv, sums).then_inc(invd, 1)

            dve.wait_ge(pads, 4)
            q_out(0, 0)
            selection(0, 0)
            q_out(1, 1)
            softmax(0, 0)
            selection(1, 1)
            with dve.Fori(1, PAIRS // 2) as i:
                for par in range(2):
                    s = 2 * i + par
                    q_out(s, par)
                    softmax(s - 1, 1 - par)
                    selection(s, par)
            softmax(PAIRS - 1, 1)

            for t in range(TT):
                n = rows(t)
                dve.wait_ge(om_mm, t + 1)
                nc.vector.tensor_tensor(out=h[0:n, t, :], in0=ps[0:n, t % 2, 0:D], in1=h[0:n, t, :],
                                        op=ALU.add).then_inc(h2_done, 1)
                dve.wait_ge(h2_done, t + 1)
                chain = norm(t, 1, chain)
                if t >= 1:
                    normed(t - 1, 1)
            normed(TT - 1, 1)
            for i in range(2):
                ins = nc.vector.memset(xT[i][DH:DH + 1, 1, :], 1.0)
            ins.then_inc(set_up, 1)

            n_route = 0

            def link(ins):
                nonlocal n_route
                n_route += 1
                ins.then_inc(route, 1)
                dve.wait_ge(route, n_route)
            dve.wait_ge(lg_mm, TT)
            nc.vector.tensor_copy(lg[:, 0:4, :], ps[:, 7, 0:4 * EXP].rearrange("p (t e) -> p t e", e=EXP))
            link(nc.vector.tensor_copy(lg[0:64, 4:5, :],
                                       ps[0:64, 7, 4 * EXP:5 * EXP].rearrange("p (t e) -> p t e", e=EXP)))
            link(nc.vector.tensor_reduce(lm[:, :, :], lg[:, :, :], axis=AX.X, op=ALU.max))
            nc.vector.tensor_tensor(out=le[:, :, :], in0=lg[:, :, :], in1=lm[:, :, :].broadcast_to([P, TT, EXP]),
                                    op=ALU.subtract).then_inc(lsub, 1)
            for t in range(TT):
                ins = nc.vector.max(out=mx8[:, t, :], in_=lg[:, t, :])
            link(ins)
            for t in range(TT):
                ins = nc.vector.max_index(out=ix8[:, t, :], in_max=mx8[:, t, :], in_values=lg[:, t, :])
            link(ins)
            link(nc.vector.tensor_copy(ixf[:, :, :], ix8[:, :, 0:1]))
            nc.vector.tensor_tensor(out=oh[:, :, :], in0=ixf[:, :, :].broadcast_to([P, TT, EXP]),
                                    in1=const("iota").unsqueeze(1).broadcast_to([P, TT, EXP]),
                                    op=ALU.is_equal).then_inc(oh_done, 1)
            dve.wait_ge(oh_done, 1)
            nc.vector.tensor_scalar(routed[:, :, :], oh[:, :, 0:1], -1.0, 1.0, ALU.mult, ALU.add)
            dve.wait_ge(le_exp, 1)
            link(nc.vector.tensor_reduce(ls[:, :, :], le[:, :, :], axis=AX.X, op=ALU.add))
            link(nc.vector.reciprocal(pr[:, :, :], ls[:, :, :]))
            link(nc.vector.tensor_tensor(out=pe_w[:, :, :], in0=pr[:, :, :], in1=routed[:, :, :], op=ALU.mult))
            link(nc.vector.tensor_scalar(ome[:, :, :], pe_w[:, :, :], -1.0, 1.0, ALU.mult, ALU.add))
            nc.vector.tensor_tensor(out=cmix[:, :, 1:EXP], in0=oh[:, :, 1:EXP],
                                    in1=pe_w[:, :, :].broadcast_to([P, TT, EXP - 1]), op=ALU.mult)\
                .then_inc(cm_done, 1)
            nc.vector.tensor_copy(cmix[:, :, 0:1], ome[:, :, :]).then_inc(cm_done, 1)

            dve.wait_ge(rank_mm, 1)
            link(nc.vector.tensor_copy(nsum[:, :, 0], ps[:, 6, TT * 8:TT * 8 + 8]))
            link(nc.vector.tensor_tensor(out=over[:, :, :], in0=nsum[:, :, :].broadcast_to([P, 8, 5]),
                                         in1=const("steps").rearrange("p (e k) -> p e k", e=8),
                                         op=ALU.is_gt))
            link(nc.vector.tensor_reduce(ntile[:, :, :], over[:, :, :], axis=AX.X, op=ALU.add))
            link(nc.vector.tensor_tensor(out=prod[:, :, :],
                                         in0=ntile[:, :, :].rearrange("p e o -> p o e").broadcast_to([P, 8, 8]),
                                         in1=const("tri").rearrange("p (e k) -> p e k", e=8), op=ALU.mult))
            link(nc.vector.tensor_reduce(cum[:, :, :], prod[:, :, :], axis=AX.X, op=ALU.add))
            link(nc.vector.tensor_tensor(out=base[:, 0, :], in0=cum[:, :, 0], in1=ntile[:, :, 0],
                                         op=ALU.subtract))
            link(nc.vector.tensor_scalar(base[:, 0, :], base[:, 0, :], float(P), None, ALU.mult))
            link(nc.vector.tensor_tensor(out=rb[:, :, :],
                                         in0=ps[:, 6, 0:TT * 8].rearrange("p (t e) -> p t e", e=8),
                                         in1=base[:, :, :].broadcast_to([P, TT, 8]), op=ALU.add))
            link(nc.vector.tensor_tensor(out=rb2[:, :, :], in0=rb[:, :, :], in1=oh[:, :, 1:EXP], op=ALU.mult))
            nc.vector.tensor_tensor(out=spare[:, :, 0], in0=oh[:, :, 0], in1=const("spare"), op=ALU.mult)
            link(nc.vector.tensor_reduce(slot[:, :, :], rb2[:, :, :], axis=AX.X, op=ALU.add))
            link(nc.vector.tensor_tensor(out=slot_s[:, :, :], in0=slot[:, :, :], in1=spare[:, :, :], op=ALU.add))
            nc.vector.tensor_copy(idx_s[:, :], slot_s[:, :, 0])
            nc.vector.tensor_copy(idx_g[:, :], slot[:, :, 0]).then_inc(slots_done, 1)
            link(nc.vector.tensor_tensor(
                out=tge[:, :, :], in0=const("tile", 0, 1).unsqueeze(2).broadcast_to([1, SEL, 8]),
                in1=cum[0:1, :, :].rearrange("p e o -> p o e").broadcast_to([1, SEL, 8]), op=ALU.is_ge))
            link(nc.vector.tensor_reduce(tex[:, :, :], tge[:, :, :], axis=AX.X, op=ALU.add))
            link(nc.vector.tensor_scalar(tex2[:, :, :], tex[:, :, :], float(EXP - 2), 1.0, ALU.min, ALU.add))
            nc.vector.tensor_copy(texi[:, :], tex2[:, :, 0]).then_inc(texp_done, 1)
            dve.wait_ge(cT_mm, 1)
            nc.vector.tensor_copy(cT[0:EXP, 0:4, :], ps[0:EXP, 7, :].rearrange("p (t n) -> p t n", t=4))\
                .then_inc(cT_ev, 1)
            nc.vector.tensor_copy(cT[0:EXP, 4, :], ps[0:EXP, 5, 0:P]).then_inc(cT_ev, 1)
            for t in range(TT):
                n = rows(t)
                dve.wait_ge(c2_mm, t + 1)
                nc.vector.scalar_tensor_tensor(out=acc[0:n, t, :], in0=ps[0:n, t % 2, 0:D], scalar=ome[0:n, t, :],
                                               in1=h[0:n, t, :], op0=ALU.mult, op1=ALU.add).then_inc(acc_a, 1)
                dve.wait_ge(b2_mm, t + 1)
                dve.wait_ge(acc_a, t + 1)
                nc.vector.tensor_tensor(out=acc[0:n, t, :], in0=ps[0:n, 2 + t % 2, 0:D], in1=acc[0:n, t, :],
                                        op=ALU.add).then_inc(acc_b, 1)

            def xT_out(s, par):
                dve.wait_ge(xT_mm, s + 1)
                wait(dve, f1_mm, s - 1)
                nc.vector.tensor_copy(xT[par][0:DH], ps[0:DH, (4, 7)[par], 0:2 * P]
                                      .rearrange("p (k n) -> p k n", k=2)).then_inc(xT_ev, 1)

            def hT_out(s, par):
                dve.wait_ge(f2T_mm, s + 1)
                wait(dve, f2_mm, s - 1)
                nc.vector.tensor_copy(hT[par].rearrange("p (c m) n -> p c (m n)", c=2), ps[:, 2:4, 0:384])\
                    .then_inc(f2T_ev, 1)
            for s in range(3):
                xT_out(s, s % 2)
            hT_out(0, 0)
            for s in (1, 2):
                xT_out(s + 2, s % 2)
                hT_out(s, s % 2)
            with dve.Fori(1, (SEL - 4) // 2) as i:
                for j, par in ((1, 1), (2, 0)):
                    xT_out(2 * i + j + 2, par)
                    hT_out(2 * i + j, par)
            xT_out(SEL - 1, 1)
            hT_out(SEL - 3, 1)
            hT_out(SEL - 2, 0)
            hT_out(SEL - 1, 1)
            for t in range(TT):
                n = rows(t)
                dve.wait_ge(yg_in[t], 16)
                nc.vector.scalar_tensor_tensor(out=acc[0:n, t, :], in0=yg[0:n, t, :], scalar=pe_w[0:n, t, :],
                                               in1=acc[0:n, t, :], op0=ALU.mult, op1=ALU.add).then_inc(fin, 1)

        @block.scalar
        def _(act):
            act.wait_ge(lnw_in, 32)
            act.wait_ge(pw_in[0], 16)
            act.wait_ge(ph_in, 16)
            for s in range(XL):
                nc.scalar.activation(weff[0:ROWS, s, :], pw[0:ROWS, 0, s, :], ACT.Copy,
                                           scale=lnw_s[0:ROWS, s:s + 1]).then_inc(first_w, 1)
            act.wait_ge(xc_done, 2)
            for s in range(XL):
                nc.scalar.activation(sq[0:ROWS, s, :], xc[0:ROWS, s, :], ACT.Square).then_inc(sq_done, 1)

            def hT_out(i, t, bank, to):
                act.wait_ge(hT_mm, i + 1)
                n = rows(t)
                nc.scalar.activation(to[:, :, t * P:t * P + n],
                                     ps[0:DH, bank, 0:2 * P].rearrange("p (k n) -> p k n", k=2)[:, :, 0:n],
                                     ACT.Copy).then_inc(hT_ev, 1)
            for t in range(TT):
                hT_out(t, t, (7, 0)[t % 2], hnT)

            def tokens(s, par):
                wait(act, v_mm, s - 1)
                for k in range(2):
                    src = hnT[:, k, bass.ds(s * PT, PT)].rearrange("p (b n) -> p b n", b=2)
                    ins = nc.scalar.activation(hc[par][:, k, :, 0:N], src, ACT.Copy)
                ins.then_inc(hc_ev, 1)

            def k_out(s, par):
                act.wait_ge(k_mm, s + 1)
                wait(act, s_mm, s - 1)
                nc.scalar.activation(kT[par].rearrange("p m b n -> p (m b n)"), ps[:, 1, 0:HP * PT],
                                     ACT.Copy).then_inc(k_ev, 1)

            def v_out(s, par):
                act.wait_ge(v_mm, s + 1)
                wait(act, av_mm, s - 1)
                nc.scalar.activation(vv[par].rearrange("p (c h) d -> p c (h d)", c=2), ps[:, 2:4, 0:384],
                                     ACT.Copy).then_inc(v_ev, 1)

            def pT_out(s):
                for c in range(3):
                    act.wait_ge(t_mm, 3 * s + c + 1)
                    if c == 0:
                        wait(act, av_mm, s)
                    nc.scalar.activation(
                        pT[:, 4 * c:4 * c + 4, :, :],
                        ps[:, 2 + c % 2, :].rearrange("p (g b n) -> p g b n", g=4, b=2)[:, :, :, 0:N],
                        ACT.Copy).then_inc(t_ev, 1)

            def o_out(s):
                act.wait_ge(av_mm, s + 1)
                nc.scalar.activation(oT[:, :, bass.ds(s * PT, PT)],
                                     ps[:, 6, 0:HP * PT].rearrange("p (m n) -> p m n", m=HP), ACT.Copy)\
                    .then_inc(o_ev, 1)

            def exps(s, par):
                act.wait_ge(shifted, s + 1)
                nc.scalar.activation(dd[par], rr[par], ACT.Exp).then_inc(expd, 1)

            act.wait_ge(pads, 4)
            act.wait_ge(hT_ev, TT)
            tokens(0, 0)
            tokens(1, 1)
            k_out(0, 0)
            v_out(0, 0)
            k_out(1, 1)
            exps(0, 0)
            v_out(1, 1)
            tokens(2, 0)

            def pair(s, par):
                k_out(s, par)
                pT_out(s - 2)
                o_out(s - 2)
                tokens(s + 1, 1 - par)
                exps(s - 1, 1 - par)
                v_out(s, par)
            pair(2, 0)
            pair(3, 1)
            with act.Fori(2, PAIRS // 2) as i:
                for par in range(2):
                    pair(2 * i + par, par)
            pT_out(PAIRS - 2)
            exps(PAIRS - 1, 1)
            o_out(PAIRS - 2)
            pT_out(PAIRS - 1)
            o_out(PAIRS - 1)

            for t in range(TT):
                hT_out(TT + t, t, 2 + t % 2, xnT)
            act.wait_ge(lsub, 1)
            nc.scalar.activation(le[:, :, :], le[:, :, :], ACT.Exp).then_inc(le_exp, 1)
            for m in range(FM):
                act.wait_ge(c1_mm, m + 1)
                nc.scalar.activation(hcT[:, m, :].rearrange("p (a n) -> p a n", a=2),
                                     ps[:, m % 2 * 2:m % 2 * 2 + 2, 0:288], ACT.Gelu,
                                     bias=b1_s[:, m:m + 1]).then_inc(c1_ev, 1)

            def gelu(s, par):
                act.wait_ge(f1_mm, s + 1)
                wait(act, f2T_mm, s - 1)
                nc.scalar.activation(hs[par].rearrange("p (c m) n -> p c (m n)", c=2), ps[:, 0:2, 0:384],
                                     ACT.Gelu).then_inc(f1_ev, 1)

            def y_store(s, par):
                act.wait_ge(f2_mm, s + 1)
                wait(act, ys_out[par], (s // 2) * 16 if isinstance(s, int) else (s - par) * 8)
                nc.scalar.activation(ys[par][:, 0, :], ps[:, 5 + par, 0:D], ACT.Copy).then_inc(y_ev, 1)
                act.wait_ge(y_ev, s + 1)
                act.dma_start(yg_dram[bass.ds(s * P, P), :], ys[par][:, 0, :]).then_inc(ys_out[par], 16)
            gelu(0, 0)
            gelu(1, 1)
            for s in range(2, 4):
                gelu(s, s % 2)
                y_store(s - 2, s % 2)
            with act.Fori(2, SEL // 2) as i:
                for par in range(2):
                    gelu(2 * i + par, par)
                    y_store(2 * i + par - 2, par)
            y_store(SEL - 2, 0)
            y_store(SEL - 1, 1)

        @block.gpsimd
        def _(pool):
            pool.wait_ge(set_up, 2)
            pool.wait_ge(var_ev, 1)
            nc.gpsimd.tensor_tensor(out=rs[:, 0:4, 0], in0=var[:, 0:4, 0], in1=half[:, :].broadcast_to([P, 4]),
                                    op=ALU.pow).then_inc(rs_done, 1)
            nc.gpsimd.tensor_tensor(out=rs[0:64, 4, :], in0=var[0:64, 4, :], in1=half[0:64, :],
                                    op=ALU.pow).then_inc(rs_done, 1)

            def rstd(i, t):
                pool.wait_ge(ve_done, i + 1)
                n = rows(t)
                nc.gpsimd.tensor_tensor(out=rl[0:n, t, :], in0=ve[0:n, t, :], in1=half[0:n, :],
                                        op=ALU.pow).then_inc(rl_done, 1)
            for t in range(TT):
                rstd(t, t)
            pool.wait_ge(zeros_out, 32)
            pool.wait_ge(cst_in, 16)

            def logits(s, par):
                pool.wait_ge(dropped, s + 1)
                pool.wait_ge(se_done, s + 1)
                wait(pool, probs, 2 * s)
                nc.gpsimd.tensor_tensor(out=rr[par], in0=se.broadcast_to([P, HEADS, N]), in1=rr[par],
                                        op=ALU.subtract).then_inc(logit, 1)

            def normalise(s, par):
                pool.wait_ge(expd, s + 1)
                pool.wait_ge(invd, s + 1)
                wait(pool, t_mm, 3 * s - 3)
                for b in range(2):
                    r = slice(64 * b, 64 * b + 64)
                    nc.gpsimd.tensor_tensor(out=pblk[par][r, :, 64 * b:64 * b + N], in0=dd[par][r, :, ::-1],
                                            in1=inv[r].broadcast_to([64, HEADS, N]), op=ALU.mult)\
                        .then_inc(probs, 1)
            logits(0, 0)
            normalise(0, 0)
            logits(1, 1)
            normalise(1, 1)
            with pool.Fori(1, PAIRS // 2) as i:
                for par in range(2):
                    s = 2 * i + par
                    logits(s, par)
                    normalise(s, par)

            pool.wait_ge(probs, 2 * PAIRS)
            for t in range(TT):
                rstd(TT + t, t)
            pool.wait_ge(slots_done, 1)
            pool.wait_ge(hn_done, 2 * TT)
            for t in range(TT):
                n = rows(t)
                nc.gpsimd.indirect_dma_start(
                    out=xg_dram, out_offset=bass.IndirectOffsetOnAxis(ap=idx_s[0:n, t:t + 1], axis=0),
                    in_=hn[0:n, t, :], in_offset=None).then_inc(scattered, 16)
            for par in range(2):
                pool.wait_ge(ys_out[par], 16 * SEL // 2)
            for t in range(TT):
                n = rows(t)
                nc.gpsimd.indirect_dma_start(
                    out=yg[0:n, t, :], out_offset=None, in_=yg_dram,
                    in_offset=bass.IndirectOffsetOnAxis(ap=idx_g[0:n, t:t + 1], axis=0))\
                    .then_inc(yg_in[t], 16)


def kernel(x, L0_tok_ln_weight, L0_tok_ln_bias, L0_tok_proj_weight, L0_tok_proj_bias, L0_attn_w_qkv,
           L0_attn_scale, L0_attn_w_out, L0_attn_b_out, L0_ffn_Ws, L0_ffn_bs, L0_ffn_W1, L0_ffn_b1,
           L0_ffn_W2, L0_ffn_b2):
    import concourse.bacc as bacc
    from concourse.bass_utils import run_bass_kernel_spmd

    def whole(a):
        return np.ascontiguousarray(a)

    xi = np.asarray(x).reshape(B, C, IMG, IMG)
    xp = np.pad(xi, ((0, 0), (0, 0), (1, 1), (1, 1)))

    def patches(dy, dx):
        v = xp[:, :, 1 + dy:1 + dy + IMG, 1 + dx:1 + dx + IMG]
        return v.reshape(B, C, SIDE, PATCH, SIDE, PATCH).transpose(1, 3, 5, 0, 2, 4).reshape(
            C, PATCH, PATCH, TOK)

    def halo(left, right, top, bottom):
        s = np.stack([left, right, top, bottom])
        return s.reshape(4, C, 2, 8, -1).transpose(1, 3, 0, 2, 4).reshape(HALO, XL, -1)
    xk = np.concatenate([
        patches(0, 0).reshape(PIX, XL, TOK),
        halo(patches(0, -1)[:, :, 0], patches(0, 1)[:, :, PATCH - 1],
             patches(-1, 0)[:, 0], patches(1, 0)[:, PATCH - 1])])

    def by_pixel(a):
        w = np.moveaxis(np.asarray(a), -1, 0).reshape(PATCH, PATCH, SHIFTS, C, -1).transpose(2, 3, 0, 1, 4)
        z = np.pad(w, ((0, 0), (0, 0), (1, 1), (1, 1), (0, 0)))
        to = ((0, 0), (0, 1), (0, -1), (1, 0), (-1, 0))
        body = np.stack([z[f, :, 1 + dy:1 + dy + PATCH, 1 + dx:1 + dx + PATCH]
                         for f, (dy, dx) in enumerate(to)])
        body = body.reshape(SHIFTS, PIX, XL, -1).transpose(1, 0, 2, 3)
        edge = halo(w[1][:, :, 0], w[2][:, :, PATCH - 1], w[3][:, 0], w[4][:, PATCH - 1])
        return body, edge

    def vector(a):
        body, edge = by_pixel(np.asarray(a).reshape(1, -1))
        table = np.zeros((ROWS, SHIFTS, XL), body.dtype)
        table[:PIX] = body[..., 0]
        table[PIX:, 0] = edge[..., 0]
        return table.reshape(ROWS, SHIFTS * XL)
    pk, ph = by_pixel(L0_tok_proj_weight)
    w1 = np.asarray(L0_ffn_W1).transpose(1, 0, 2)
    w2 = np.asarray(L0_ffn_W2).reshape(EXP, FM, P, D).transpose(2, 0, 1, 3)
    arrays = {
        "xk": xk, "pk": pk, "ph": ph, "lnw": vector(L0_tok_ln_weight), "lnb": vector(L0_tok_ln_bias),
        "pb": np.asarray(L0_tok_proj_bias).reshape(1, D),
        "wqkv": np.asarray(L0_attn_w_qkv).reshape(2, DH, 3 * INNER).transpose(1, 0, 2),
        "scale": np.repeat(np.asarray(L0_attn_scale).reshape(HP, 2).T, HD, axis=0),
        "wout": np.asarray(L0_attn_w_out).reshape(HP, P, D).transpose(1, 0, 2),
        "bout": np.asarray(L0_attn_b_out).reshape(1, D),
        "ws": np.asarray(L0_ffn_Ws).reshape(2, DH, EXP).transpose(1, 0, 2),
        "bs": np.asarray(L0_ffn_bs).reshape(1, EXP),
        "w1": w1, "b1": np.asarray(L0_ffn_b1).reshape(1, EXP, FF), "w2": w2, "b2": np.asarray(L0_ffn_b2),
        "b1c": np.asarray(L0_ffn_b1)[0].reshape(FM, P).T,
        "consts": constants(),
    }
    arrays = {f"{k}_dram": whole(v) for k, v in arrays.items()}
    nc = bacc.Bacc("TRN2", target_bir_lowering=False, num_devices=1)
    args = [nc.dram_tensor(k, v.shape, mybir.dt.from_np(v.dtype), kind="ExternalInput").ap()
            for k, v in arrays.items()]
    out = nc.dram_tensor("out_dram", (TOK, D), mybir.dt.float32, kind="ExternalOutput").ap()
    build(nc, *args, out)
    r = run_bass_kernel_spmd(nc, [arrays], core_ids=[0])
    return r.results[0]["out_dram"].reshape(B, N, D)
```

```python
import numpy as np
import concourse.bass as bass
from concourse import mybir
from contextlib import ExitStack

B, C, IMG, PATCH, SIDE = 16, 3, 96, 16, 6
N = SIDE * SIDE
TOK = B * N
D = 192
DH = D // 2
XL = 8
PIX = C * PATCH * 2
HALO = 4 * C * PATCH // XL
ROWS = PIX + HALO
SHIFTS = 5
PATCH_DIM = PATCH * PATCH * C * SHIFTS
HEADS, HD = 12, 64
INNER = HEADS * HD
HP = HEADS // 2
KEEP = int(N * 0.75)
assert N - 1 - KEEP == 8
PAIRS = B // 2
PT = 2 * N
EXP, FF = 9, 768
FM = FF // 128
P = 128
TT = (TOK + P - 1) // P
GS = 64
GROUPS = (TOK + (EXP - 1) * (GS - 1)) // GS
TILES = (GROUPS + 1) // 2
SLOTS = TILES * P
STEPS = (TOK + GS - 1) // GS
ROW = D + 2
BIG = 1e30
EPS = 1e-5


POOL_SLOTS = 6
HN_BANK = (7, 0, 7, 5, 6)
XN_BANK = (2, 3, 2, 3, 6)


def HID_BANK(s):
    return 2 if s < TILES - 1 else 0


PROJ_BANK = (4, 5, 6, 1, 4)


def rows(t):
    return min(P, TOK - t * P)


CONST = {}
_at = 0
for _n, _w in (("ident", P), ("upper", P), ("diag", N), ("diag_out", N), ("tri", 64), ("iota", EXP),
               ("steps", 8 * STEPS), ("group", 2 * TILES), ("spare", TT), ("token", TT), ("count", XL)):
    CONST[_n] = (_at, _at + _w)
    _at += _w
CONST_W = _at


def constants():
    t = np.zeros((P, CONST_W), np.float32)

    def col(n):
        return t[:, CONST[n][0]:CONST[n][1]]

    col("ident")[:] = np.eye(P)
    col("upper")[:] = np.triu(np.ones((P, P)), 1)
    for p in range(P):
        if p % 64 < N:
            col("diag")[p, p % 64] = -BIG
            col("diag_out")[p, N - 1 - p % 64] = -3 * BIG
    col("tri")[:] = np.tril(np.ones((8, 8))).reshape(-1)
    col("iota")[:] = np.arange(EXP)
    col("steps")[:] = np.tile(np.arange(STEPS) * GS, 8)
    col("group")[:] = np.arange(2 * TILES)
    col("token")[:] = np.arange(P)[:, None] + P * np.arange(TT)
    col("spare")[:] = SLOTS + col("token")
    cnt = np.ones((C, PATCH, PATCH))
    cnt[:, :, 1:] += 1
    cnt[:, :, :-1] += 1
    cnt[:, 1:, :] += 1
    cnt[:, :-1, :] += 1
    col("count")[:PIX] = cnt.reshape(PIX, XL)
    col("count")[PIX:ROWS] = 1
    return t


def build(nc, xk, pk, ph, lnw, lnb, pb, wqkv, scale, wout, bout, ws, bs, w1, b1, w2, b2, b1c, consts, out):
    fp32 = mybir.dt.float32
    u32 = mybir.dt.uint32
    i32 = mybir.dt.int32
    ALU = mybir.AluOpType
    ACT = mybir.ActivationFunctionType
    AX = mybir.AxisListType

    xg_dram = nc.dram_tensor("xg_scratch", (SLOTS + TT * P, ROW), fp32).ap()
    acc_dram = nc.dram_tensor("acc_scratch", (TOK + 1, D), fp32).ap()

    with ExitStack() as ctx:
        def sb(name, shape, dt=fp32):
            return ctx.enter_context(nc.sbuf_tensor(name, shape, dt))

        def sem(name):
            return ctx.enter_context(nc.semaphore(name))

        A_W = 2 * EXP * FF + EXP * FM * D
        region = sb("region", [P, A_W])
        at = 0

        def take(width, shape, **kw):
            nonlocal at
            v = region[:, at:at + width].rearrange(shape, **kw)
            at += width
            return v
        xs = take(XL * TOK, "p (s n) -> p s n", s=XL)
        xc = take(XL * TOK, "p (s n) -> p s n", s=XL)
        pw = take(SHIFTS * XL * D, "p (f s d) -> p f s d", f=SHIFTS, s=XL)
        weff = take(XL * D, "p (s d) -> p s d", s=XL)
        sq = take(XL * TOK, "p (s n) -> p s n", s=XL)
        xsum = take(TOK, "p (a n) -> p a n", a=1)
        sqsum = take(TOK, "p (a n) -> p a n", a=1)
        assert at <= A_W, (at, A_W)
        w1a = region[:, 0:EXP * FF].rearrange("p (e f) -> p e f", e=EXP)
        w1b = region[:, EXP * FF:2 * EXP * FF].rearrange("p (e f) -> p e f", e=EXP)
        w2s = region[:, 2 * EXP * FF:A_W].rearrange("p (e m d) -> p e m d", e=EXP, m=FM)

        cst = sb("cst", [P, CONST_W])

        def const(n, p0=0, p1=P):
            return cst[p0:p1, CONST[n][0]:CONST[n][1]]
        ones = sb("ones", [P, P])
        half = sb("half", [P, 1])
        lnw_s = sb("lnw_s", [P, SHIFTS * XL])
        lnb_s = sb("lnb_s", [P, SHIFTS * XL])
        rowv = sb("rowv", [1, D])
        bout_s = sb("bout_s", [P, 1, D])
        bs_s = sb("bs_s", [P, 1, EXP])
        wq_all = sb("wq_s", [P, 6 * INNER])
        wq_s = wq_all[0:DH, :].rearrange("p (k n) -> p k n", k=2)
        wo_s = sb("wo_s", [P, HP, D])
        ws_s = sb("ws_s", [DH, 2, EXP])
        b2_s = sb("b2_s", [EXP, D])
        b1_s = sb("b1_s", [P, FM])
        scq = sb("scq", [P, HP])
        bias = sb("bias", [P, D])
        var = sb("var", [P, TT, 1])
        rs = sb("rs", [P, TT, 1])
        h = sb("h", [P, TT, D])
        hn = sb("hn", [P, TT, ROW])
        st = sb("st", [P, TT, 6])
        mv = sb("mv", [P, TT, 2])
        ve = sb("ve", [P, TT, 1])
        rl = sb("rl", [P, TT, 1])
        hnT = sb("hnT", [DH, 2, TOK])
        xnT = hnT
        qT = sb("qT", [P, HP, TOK])[:, :, :]
        kT = sb("kT", [P, HP, TOK])
        oT = kT
        hcT = oT[:, :, :]

        work = sb("work", [P, 6912])
        at = 0

        def take2(width, shape, **kw):
            nonlocal at
            v = work[:, at:at + width].rearrange(shape, **kw)
            at += width
            return v
        vv = [take2(INNER, "p (h d) -> p h d", h=HEADS) for _ in range(2)]
        dd = take2(HEADS * N, "p (h n) -> p h n", h=HEADS)
        rr = [take2(HEADS * N, "p (h n) -> p h n", h=HEADS) for _ in range(2)]
        ee = [take2(HEADS * N, "p (h n) -> p h n", h=HEADS) for _ in range(2)]
        pT = take2(HEADS * PT, "p (h b n) -> p h b n", h=HEADS, b=2)
        sraw = take2(N, "p (h n) -> p h n", h=1)
        mx = take2(HEADS * 8, "p (h n) -> p h n", h=HEADS)
        se = take2(N, "p (h n) -> p h n", h=1)
        rowm = take2(HEADS, "p (h n) -> p h n", h=HEADS)
        sums = take2(HEADS, "p (h n) -> p h n", h=HEADS)
        inv = take2(HEADS, "p (h n) -> p h n", h=HEADS)
        pblk = [sb(f"pblk{i}", [P, HEADS, PT]) for i in range(2)]

        assert at <= 5000
        thirty2 = work[:, 5800:5800 + P]
        bias4 = work[:, 6000:6000 + D]
        scaled = work[:, 6200:6200 + (XL - POOL_SLOTS) * D].rearrange("p (s d) -> p s d", d=D)
        empty = work[:, 5000:5000 + SLOTS // 2 // P * ROW].rearrange("p (a d) -> p a d", d=ROW)

        at = 0
        xg = [take2(D, "p (a d) -> p a d", a=1) for _ in range(2)]
        xT = [take2(2 * P, "p (k n) -> p k n", k=2) for _ in range(2)]
        hs = [take2(FF, "p (m n) -> p m n", m=FM) for _ in range(2)]
        hT = [take2(FF, "p (m n) -> p m n", m=FM) for _ in range(2)]
        ys = [take2(D, "p (a d) -> p a d", a=1) for _ in range(2)]
        ag = [take2(D, "p (a d) -> p a d", a=1) for _ in range(2)]
        acc = take2(TT * D, "p (t d) -> p t d", t=TT)
        cT = take2(TT * P, "p (t n) -> p t n", t=TT)
        wb1 = [wq_all[:, i * 2 * FF:(i + 1) * 2 * FF].rearrange("p (k f) -> p k f", k=2) for i in range(2)]
        qflat = qT.rearrange("p m n -> p (m n)")
        wb2 = [qflat[:, i * FM * D:(i + 1) * FM * D].rearrange("p (m d) -> p m d", m=FM) for i in range(2)]

        lg = sb("lg", [P, TT, EXP])
        le = sb("le", [P, TT, EXP])
        lm = sb("lm", [P, TT, 1])
        ls = sb("ls", [P, TT, 1])
        pr = sb("pr", [P, TT, 1])
        mx8 = sb("mx8", [P, TT, 8])
        ix8 = sb("ix8", [P, TT, 8], u32)
        ixf = sb("ixf", [P, TT, 1])
        oh = sb("oh", [P, TT, EXP])
        routed = sb("routed", [P, TT, 1])
        pe_w = sb("pe_w", [P, TT, 1])
        ome = sb("ome", [P, TT, 1])
        cmix = sb("cmix", [P, TT, EXP])
        over = sb("over", [P, 8, STEPS])
        pf = sb("pf", [P, TT + 1, 8])
        ntile = sb("ntile", [P, 8, 1])
        prod = sb("prod", [P, 8, 8])
        cum = sb("cum", [P, 8, 1])
        base = sb("base", [P, 1, 8])
        rb = sb("rb", [P, TT, 8])
        rb2 = sb("rb2", [P, TT, 8])
        slot = sb("slot", [P, TT, 1])
        spare = sb("spare", [P, TT, 1])
        slot_s = sb("slot_s", [P, TT, 1])
        idx_s = sb("idx_s", [P, TT], u32)
        tge = sb("tge", [1, 2 * TILES, 8])
        tex = sb("tex", [1, 2 * TILES, 1])
        tex2 = sb("tex2", [1, 2 * TILES, 1])
        texi = sb("texi", [1, 2 * TILES], i32)
        meta = sb("meta", [P, TILES, 2])
        row_i = sb("row_i", [P, TILES], u32)
        nsum = sb("nsum", [P, 8, 1])

        ps = ctx.enter_context(nc.psum_tensor("ps", [P, 8, 512], fp32))

        x_in = [sem(f"x_in{i}") for i in range(4)]
        lnw_in, cst_in, count_in, ph_in, wq_in, wo_in, small_in = (sem(f"{n}_in") for n in (
            "lnw", "cst", "count", "halo_w", "wqkv", "wout", "small"))
        pw_in = [sem(f"pw_in{f}") for f in range(SHIFTS)]
        w1_in, w2_in, wc_in = sem("w1_in"), sem("w2_in"), sem("common_w_in")
        set_up, pads, zeroed = sem("ones_set"), sem("pads_zeroed"), sem("blocks_zeroed")
        xsum_done, sqsum_done = sem("pixel_sums"), sem("square_sums")
        mean_mm, xc_done, sq_done, var_mm, bias_mm, bias_ev = (sem(n) for n in (
            "mean_mm", "centred", "squared", "var_mm", "bias_mm", "bias_ev"))
        fold, fold_pool, first_w, var_ev, rs_done, proj_mm = (sem(n) for n in (
            "folded", "folded_pool", "fold_first", "var_ev", "rstd_done", "proj_mm"))
        h_done, h_out_b, s_cleared = sem("h_done"), sem("h_with_b_out"), sem("dots_banks_cleared")
        ln_chain, ve_done, rl_done, hn_done, hT_mm, hT_ev = (sem(n) for n in (
            "ln_chain", "ln_var", "ln_rstd", "hn_done", "hnT_mm", "hnT_ev"))
        qk_mm, v_mm, s_mm, t_mm, av_mm = (sem(n) for n in (
            "qk_mm", "v_mm", "s_mm", "pT_mm", "av_mm"))
        qk_ev, v_ev, d_ev, t_ev, o_ev = (sem(n) for n in (
            "qk_ev", "v_ev", "dots_ev", "pT_ev", "oT_ev"))
        top8, dropped, se_sum, se_done, logit, rmax, shifted, expd, summed, invd, probs = (sem(n) for n in (
            "top8", "dropped", "se_sum", "se_done", "logits_ready", "row_max", "shifted", "exp_done",
            "row_sum", "row_inv", "probs_ready"))
        zeros_out = sem("zero_rows_written")
        om_mm, h2_done, lg_mm, lg_ev, le_exp, route, oh_done, rank_mm, cm_done, cT_mm, cT_ev = (
            sem(n) for n in ("out_mm", "h2_done", "router_mm", "router_ev", "router_exp", "route",
                             "onehot", "rank_mm", "mix_done", "mixT_mm", "mixT_ev"))
        lsub, slots_done, pf_done, texp_done, scattered = (sem(n) for n in (
            "logits_less_max", "slots_done", "earlier_tokens", "tile_expert", "scattered"))
        c1_mm, c1_ev, c2_mm, b2_mm, acc_a, acc_b = (sem(n) for n in (
            "common1_mm", "common1_ev", "common2_mm", "b2_mm", "acc_a", "acc_b"))
        xg_in = [sem(f"xg_in{i}") for i in range(2)]
        xT_mm, xT_ev, f1_mm, f1_ev, f2T_mm, f2T_ev, f2_mm, y_ev = (sem(n) for n in (
            "xT_mm", "xT_ev", "up_mm", "gelu_done", "hT_mm", "hT_ev2", "down_mm", "y_ev"))
        meta_in, rows_ready, stored, rows_out = (sem(n) for n in (
            "meta_in", "row_numbers", "common_stored", "rows_out"))
        ag_in = [sem(f"common_in{i}") for i in range(2)]
        empty_set, wb1_ready, wb2_ready, bias4_mm, bias4_ev, sq4_mm = (sem(n) for n in (
            "empty_set", "second_up_weights", "second_down_weights", "bias4_mm", "bias4_ev", "squares4_mm"))

        def wait(eng, s, n):
            if not isinstance(n, int) or n > 0:
                eng.wait_ge(s, n)

        block = ctx.enter_context(nc.Block())

        @block.sync
        def _(sp):
            first = slice(*CONST["count"])
            sp.dma_start(cst[:, first], consts[:, first]).then_inc(count_in, 16)
            for i in range(4):
                sp.dma_start(xs[0:ROWS, 2 * i:2 * i + 2], xk[:, 2 * i:2 * i + 2]).then_inc(x_in[i], 16)
            sp.dma_start(lnw_s[0:ROWS], lnw).then_inc(lnw_in, 16)
            sp.dma_start(lnb_s[0:ROWS], lnb).then_inc(lnw_in, 16)
            for f in range(SHIFTS):
                sp.dma_start(pw[0:PIX, f], pk[:, f]).then_inc(pw_in[f], 16)
                if f == 0:
                    sp.dma_start(pw[PIX:ROWS, 0], ph).then_inc(ph_in, 16)
            rest = slice(0, CONST["count"][0])
            sp.dma_start(cst[:, rest], consts[:, rest]).then_inc(cst_in, 16)
            sp.dma_start(rowv[0:1, 0:D], pb).then_inc(small_in, 16)
            sp.dma_start(bout_s[:, 0, :], bout.broadcast_to([P, D])).then_inc(small_in, 16)
            sp.dma_start(bs_s[:, 0, :], bs.broadcast_to([P, EXP])).then_inc(small_in, 16)
            sp.dma_start(scq[:, :], scale).then_inc(small_in, 16)
            sp.dma_start(ws_s[:, :, :], ws).then_inc(small_in, 16)
            sp.dma_start(b2_s[:, :], b2).then_inc(small_in, 16)
            sp.dma_start(b1_s[:, :], b1c).then_inc(small_in, 16)
            sp.dma_start(wq_s[:, :, :], wqkv).then_inc(wq_in, 16)
            sp.dma_start(wo_s[:, :, :], wout).then_inc(wo_in, 16)
            sp.wait_ge(empty_set, 2)
            for i in range(2):
                sp.dma_start(xg_dram[i * SLOTS // 2:(i + 1) * SLOTS // 2, :]
                             .rearrange("(p a) d -> p (a d)", p=P), empty.rearrange("p a d -> p (a d)"))\
                    .then_inc(zeros_out, 16)
            sp.dma_start(acc_dram[TOK:TOK + 1, :], empty[0:1, 0, 0:D]).then_inc(zeros_out, 16)
            sp.wait_ge(proj_mm, TT)
            sp.dma_start(w1a[0:DH, 0], w1[0:DH, 0]).then_inc(wc_in, 16)
            sp.dma_start(w1b[0:DH, 0], w1[DH:D, 0]).then_inc(wc_in, 16)
            sp.dma_start(w2s[:, 0], w2[:, 0]).then_inc(wc_in, 16)
            sp.dma_start(w1a[0:DH, 1:EXP], w1[0:DH, 1:EXP]).then_inc(w1_in, 16)
            sp.dma_start(w1b[0:DH, 1:EXP], w1[DH:D, 1:EXP]).then_inc(w1_in, 16)
            sp.dma_start(w1b[DH:DH + 1, :], b1).then_inc(w1_in, 16)
            sp.dma_start(w2s[:, 1:EXP], w2[:, 1:EXP]).then_inc(w2_in, 16)

            sp.wait_ge(scattered, 16 * TT)

            def load_tile(s):
                wait(sp, xT_mm, s - 1)
                sp.dma_start(xg[s % 2][:, 0, :], xg_dram[s * P:(s + 1) * P, 0:D]).then_inc(xg_in[s % 2], 16)
            load_tile(0)
            load_tile(1)
            sp.dma_start(meta[:, :, :], xg_dram[0:SLOTS, D:ROW].rearrange("(t p) c -> p t c", p=P))\
                .then_inc(meta_in, 16)
            for t in range(TT):
                if t >= TT - 2:
                    load_tile(t - TT + 4)
                sp.wait_ge(acc_b, t + 1)
                for to in (acc_dram, out):
                    sp.dma_start(to[t * P:t * P + rows(t), :], acc[0:rows(t), t, :]).then_inc(stored, 16)
            for s in range(4, TILES):
                load_tile(s)
            sp.wait_ge(rows_out, 16 * TILES)

        @block.tensor
        def _(pe):
            pe.wait_ge(set_up, 2)
            pe.wait_ge(xsum_done, XL)
            for half_ in range(2):
                nc.tensor.matmul(ps[0:ROWS, half_, 0:288], ones[0:ROWS, 0:ROWS],
                                 xsum[0:ROWS, 0, half_ * 288:half_ * 288 + 288], start=True, stop=True)\
                    .then_inc(mean_mm, 1)
            pe.wait_ge(lnw_in, 32)
            pe.wait_ge(ph_in, 16)
            for f in range(SHIFTS):
                pe.wait_ge(pw_in[f], 16)
                n = ROWS if f == 0 else PIX
                for s in range(XL):
                    o = 32 * (s % 4)
                    mm = nc.tensor.matmul(ps[o:o + 32, 2, 0:D],
                                          lnb_s[0:n, f * XL + s:f * XL + s + 1].broadcast_to([n, 32]),
                                          pw[0:n, f, s, :], start=(f == 0 and s < 4),
                                          stop=(f == SHIFTS - 1 and s >= 4))
            mm.then_inc(bias4_mm, 1)
            for s in range(XL):
                pe.wait_ge(sq_done, s + 1)
                o = 32 * (s % 4)
                for half_ in range(2):
                    mm = nc.tensor.matmul(ps[o:o + 32, 6 + half_, 0:288],
                                          const("count", 0, ROWS)[:, s:s + 1].broadcast_to([ROWS, 32]),
                                          sq[0:ROWS, s, half_ * 288:half_ * 288 + 288],
                                          start=(s < 4), stop=(s >= 4))
            mm.then_inc(sq4_mm, 1)
            pe.wait_ge(xc_done, 2)
            pe.wait_ge(fold, SHIFTS - 1)

            def transposes(t, ready, bank):
                pe.wait_ge(hn_done, ready)
                for k in range(2):
                    mm = nc.tensor.transpose(ps[0:DH, bank, k * P:k * P + rows(t)],
                                             hn[0:rows(t), t, k * DH:(k + 1) * DH],
                                             const("ident", 0, rows(t))[:, 0:rows(t)])
                mm.then_inc(hT_mm, 1)
            for t in range(TT):
                if t == 4:
                    pe.wait_ge(h_done, 1)
                for s in range(XL):
                    if s == POOL_SLOTS:
                        pe.wait_ge(fold_pool, 2 * (SHIFTS - 1))
                    if s == XL - 1 and t >= 2:
                        if t == 2:
                            pe.wait_ge(bias_ev, 1)
                        if t == 4:
                            pe.wait_ge(hT_ev, 1)
                        transposes(t - 2, t - 1, HN_BANK[t - 2])
                    mm = nc.tensor.matmul(ps[0:rows(t), PROJ_BANK[t], 0:D],
                                          xc[0:ROWS, s, t * P:t * P + rows(t)], weff[0:ROWS, s, :],
                                          start=(s == 0), stop=(s == XL - 1))
                mm.then_inc(proj_mm, 1)
                if t == 0:
                    pe.wait_ge(small_in, 16 * 7)
                    pe.wait_ge(bias4_ev, 1)
                    nc.tensor.matmul(ps[:, 0, 0:D], ones[0:1, :], rowv[0:1, 0:D], start=True, stop=False)
                    nc.tensor.matmul(ps[:, 0, 0:D], thirty2[:, :], bias4[:, :], start=False, stop=True)\
                        .then_inc(bias_mm, 1)
                    pe.wait_ge(sqsum_done, 1)
                    for u in range(TT):
                        mm = nc.tensor.matmul(ps[0:rows(u), 3, u:u + 1], sqsum[:, 0, u * P:u * P + rows(u)],
                                              thirty2[:, 0:1], start=True, stop=True)
                    mm.then_inc(var_mm, 1)

            pe.wait_ge(wq_in, 16)

            def qk(half_, m):
                for which in range(2):
                    n = (half_ * HP + m) * 2 + which
                    wait(pe, qk_ev, n - 3)
                    for k in range(2):
                        mm = nc.tensor.matmul(ps[:, (2, 3, 0, 1)[n % 4], 0:288],
                                              wq_s[:, k, which * INNER + m * P:which * INNER + (m + 1) * P],
                                              hnT[:, k, half_ * 288:half_ * 288 + 288],
                                              start=(k == 0), stop=(k == 1))
                    mm.then_inc(qk_mm, 1)

            def probs_T(s):
                pe.wait_ge(probs, 2 * s + 2)
                for c, bank in enumerate((0, 1, 7)):
                    for g in range(4):
                        mm = nc.tensor.transpose(ps[0:PT, bank, g * P:(g + 1) * P],
                                                 pblk[s % 2][:, 4 * c + g, :], const("ident"))
                    mm.then_inc(t_mm, 1)

            def av(s):
                pe.wait_ge(v_ev, s + 1)
                wait(pe, o_ev, s)
                pe.wait_ge(t_ev, 3 * s + 3)
                for m in range(HP):
                    for odd in range(2):
                        mm = nc.tensor.matmul(ps[64 * odd:64 * odd + 64, 6, m * PT:(m + 1) * PT],
                                              vv[s % 2][0:PT, 2 * m + odd, :], pT[0:PT, odd * HP + m, :, :],
                                              start=True, stop=True)
                mm.then_inc(av_mm, 1)

            def values(s):
                wait(pe, v_ev, s)
                for c in range(2):
                    for k in range(2):
                        mm = nc.tensor.matmul(ps[0:PT, 2 + c, 0:384], hnT[:, k, s * PT:(s + 1) * PT],
                                              wq_s[:, k, 2 * INNER + c * 384:2 * INNER + (c + 1) * 384],
                                              start=(k == 0), stop=(k == 1))
                mm.then_inc(v_mm, 1)

            def dots(s):
                if s == 0:
                    pe.wait_ge(s_cleared, 1)
                wait(pe, d_ev, 2 * s)
                for m in range(HP):
                    for b in range(2):
                        c0 = s * PT + b * N
                        for odd in range(2):
                            o = 64 * odd
                            mm = nc.tensor.matmul(ps[64 * b:64 * b + N, 4 + odd, m * N:(m + 1) * N],
                                                  qT[o:o + 64, m, c0:c0 + N], kT[o:o + 64, m, c0:c0 + N],
                                                  start=True, stop=True)
                mm.then_inc(s_mm, 1)

            pe.wait_ge(hT_ev, 3)
            for m in range(HP):
                qk(0, m)
                if m < 2:
                    transposes(3 + m, 4 + m, HN_BANK[3 + m])
            pe.wait_ge(hT_ev, 5)
            for m in range(HP):
                qk(1, m)
                if m in (0, 3):
                    pe.wait_ge(qk_ev, 2 * HP)
                    dots(m // 3)
            pe.wait_ge(qk_ev, 4 * HP - 2)
            values(0)
            pe.wait_ge(qk_ev, 4 * HP)
            dots(2)
            values(1)
            for s in range(3, PAIRS + 1):
                if s < PAIRS:
                    dots(s)
                probs_T(s - 3)
                values(s - 1)
                av(s - 3)

            pe.wait_ge(wo_in, 16)

            def out_proj(t):
                pe.wait_ge(o_ev, min(PAIRS, (t * P + rows(t) + PT - 1) // PT))
                wait(pe, h2_done, t - 1)
                bank = 4 + t % 2
                for m in range(HP):
                    mm = nc.tensor.matmul(ps[0:rows(t), bank, 0:D], oT[:, m, t * P:t * P + rows(t)],
                                          wo_s[:, m, :], start=(m == 0), stop=(m == HP - 1))
                mm.then_inc(om_mm, 1)

            def router(t):
                pe.wait_ge(hT_ev, TT + t + 1)
                for k in range(2):
                    mm = nc.tensor.matmul(ps[0:rows(t), 7, t * EXP:(t + 1) * EXP],
                                     xnT[:, k, t * P:t * P + rows(t)], ws_s[:, k, :],
                                     start=(k == 0), stop=(k == 1))
                mm.then_inc(lg_mm, 1)
            pe.wait_ge(d_ev, 2 * PAIRS)
            out_proj(0)
            probs_T(PAIRS - 2)
            out_proj(1)
            av(PAIRS - 2)
            probs_T(PAIRS - 1)
            out_proj(2)
            av(PAIRS - 1)
            pe.wait_ge(v_ev, PAIRS)
            transposes(0, TT + 1, XN_BANK[0])
            out_proj(3)
            transposes(1, TT + 2, XN_BANK[1])
            out_proj(4)

            def common_up(m, half_):
                for k, w in enumerate((w1a, w1b)):
                    mm = nc.tensor.matmul(ps[:, m % 3 * 2 + half_, 0:288], w[0:DH, 0, m * P:(m + 1) * P],
                                          xnT[:, k, half_ * 288:half_ * 288 + 288],
                                          start=(k == 0), stop=(k == 1))
                mm.then_inc(c1_mm, 1)

            pe.wait_ge(hT_ev, TT + 1)
            transposes(2, TT + 3, XN_BANK[2])
            for t in range(3):
                router(t)
            pe.wait_ge(wc_in, 48)
            common_up(0, 0)
            pe.wait_ge(hT_ev, TT + 2)
            transposes(3, TT + 4, XN_BANK[3])
            pe.wait_ge(hT_ev, TT + 3)
            common_up(1, 0)
            transposes(4, TT + 5, XN_BANK[4])
            router(3)
            router(4)

            for m in range(FM):
                if m == 1:
                    pe.wait_ge(hT_ev, TT + 4)
                if m == 2:
                    pe.wait_ge(h2_done, TT)
                if m >= 3:
                    pe.wait_ge(c1_ev, m - 2)
                if m >= 2:
                    common_up(m, 0)
                common_up(m, 1)
                if m == 2:
                    pe.wait_ge(pf_done, TT)
                    for to, table, rhs, first, last in (
                            (ps[:, 6, 0:TT * 8], const("upper"), oh[:, :, 1:EXP], True, False),
                            (ps[:, 6, 0:TT * 8], ones[:, :], pf[:, 0:TT, :], False, True),
                            (ps[:, 6, TT * 8:TT * 8 + 8], ones[:, :], pf[:, TT, :], True, True)):
                        mm = nc.tensor.matmul(to, table, rhs, start=first, stop=last)
                    mm.then_inc(rank_mm, 1)
            pe.wait_ge(cm_done, 2)
            pe.wait_ge(slots_done, 3)
            for t in range(TT):
                mm = nc.tensor.transpose(ps[0:EXP, (7 if t < 4 else 6), t % 4 * P:t % 4 * P + P], cmix[:, t, :], const("ident"))
            mm.then_inc(cT_mm, 1)
            def tile_T(s):
                par = s % 2
                pe.wait_ge(xg_in[par], 16 * (s // 2 + 1))
                wait(pe, xT_ev, s - 1)
                for k in range(2):
                    mm = nc.tensor.transpose(ps[0:DH, (4, 7)[par], k * P:(k + 1) * P],
                                             xg[par][:, 0, k * DH:(k + 1) * DH], const("ident"))
                mm.then_inc(xT_mm, 1)

            def up(s):
                par = s % 2
                e = pe.value_load(texi[0:1, 2 * s:2 * s + 1], min_val=1, max_val=EXP - 1)
                pe.wait_ge(xT_ev, s + 1)
                pe.wait_ge(wb1_ready, s + 1)
                wait(pe, f1_ev, s)
                for c in range(2):
                    cols = slice(c * 384, (c + 1) * 384)
                    for k, (n, w) in enumerate(((DH, w1a), (DH + 1, w1b))):
                        nc.tensor.matmul(ps[0:GS, c, 0:384], xT[par][0:n, k, 0:GS],
                                         w[0:n, bass.ds(e, 1), cols], start=(k == 0), stop=(k == 1))
                        mm = nc.tensor.matmul(ps[GS:P, c, 0:384], xT[par][0:n, k, GS:P],
                                              wb1[par][0:n, k, cols], start=(k == 0), stop=(k == 1))
                mm.then_inc(f1_mm, 1)

            def hidden_T(s):
                pe.wait_ge(f1_ev, s + 1)
                b = HID_BANK(s)
                if b == 2:
                    wait(pe, f2T_ev, s)
                for m in range(FM):
                    mm = nc.tensor.transpose(ps[:, b + m // 3, m % 3 * P:(m % 3 + 1) * P], hs[s % 2][:, m, :],
                                             const("ident"))
                mm.then_inc(f2T_mm, 1)

            def down(s):
                par = s % 2
                e = pe.value_load(texi[0:1, 2 * s:2 * s + 1], min_val=1, max_val=EXP - 1)
                pe.wait_ge(f2T_ev, s + 1)
                pe.wait_ge(wb2_ready, s + 1)
                wait(pe, y_ev, s - 1)
                for m in range(FM):
                    nc.tensor.matmul(ps[0:GS, 5 + par, 0:D], hT[par][:, m, 0:GS], w2s[:, bass.ds(e, 1), m, :],
                                     start=(m == 0), stop=(m == FM - 1))
                    mm = nc.tensor.matmul(ps[GS:P, 5 + par, 0:D], hT[par][:, m, GS:P], wb2[par][:, m, :],
                                          start=(m == 0), stop=(m == FM - 1))
                mm.then_inc(f2_mm, 1)
            pe.wait_ge(c1_ev, FM)
            for t in range(TT):
                if t == TT - 2:
                    tile_T(0)
                if t == TT - 1:
                    tile_T(1)
                    pe.wait_ge(texp_done, 1)
                    pe.wait_ge(w1_in, 48)
                    up(0)
                if t >= 2:
                    pe.wait_ge(acc_a, t - 1)
                    pe.wait_ge(acc_b, t - 1)
                for m in range(FM):
                    mm = nc.tensor.matmul(ps[0:rows(t), 2 + t % 2, 0:D], hcT[:, m, t * P:t * P + rows(t)],
                                          w2s[:, 0, m, :], start=(m == 0), stop=(m == FM - 1))
                mm.then_inc(c2_mm, 1)
                if t == 0:
                    pe.wait_ge(cT_ev, 2)
                nc.tensor.matmul(ps[0:rows(t), 5 + t % 2, 0:D], cT[0:EXP, t, 0:rows(t)], b2_s[:, :],
                                 start=True, stop=True).then_inc(b2_mm, 1)
            pe.wait_ge(w2_in, 16)
            for s in range(TILES):
                if s + 1 < TILES:
                    up(s + 1)
                if s + 2 < TILES:
                    tile_T(s + 2)
                if 1 <= s < TILES - 1:
                    down(s - 1)
                if s == 0:
                    pe.wait_ge(acc_b, TT)
                hidden_T(s)
            down(TILES - 2)
            down(TILES - 1)

        @block.vector
        def _(dve):
            nc.vector.memset(ones[:, :], 1.0).then_inc(set_up, 1)
            nc.vector.memset(half[:, :], -0.5).then_inc(set_up, 1)
            nc.vector.memset(thirty2[:, :], 1 / 32)
            nc.vector.memset(var[64:P, TT - 1, :], 1.0)
            nc.vector.memset(pf[:, 0, :], 0.0)
            nc.vector.memset(lg[:, :, :], 0.0).then_inc(pads, 1)
            cnt = const("count", 0, ROWS)
            dve.wait_ge(count_in, 16)
            for s in range(XL):
                if s % 2 == 0:
                    dve.wait_ge(x_in[s // 2], 16)
                if s == 0:
                    nc.vector.tensor_scalar(xsum[0:ROWS, 0, :], xs[0:ROWS, 0, :], cnt[:, 0:1], None, ALU.mult)\
                        .then_inc(xsum_done, 1)
                else:
                    dve.wait_ge(xsum_done, s)
                    nc.vector.scalar_tensor_tensor(out=xsum[0:ROWS, 0, :], in0=xs[0:ROWS, s, :],
                                                   scalar=cnt[:, s:s + 1], in1=xsum[0:ROWS, 0, :],
                                                   op0=ALU.mult, op1=ALU.add).then_inc(xsum_done, 1)
            for half_ in range(2):
                dve.wait_ge(mean_mm, half_ + 1)
                c0 = half_ * 288
                nc.vector.scalar_tensor_tensor(
                    out=xc[0:ROWS, :, c0:c0 + 288],
                    in0=ps[0:ROWS, half_:half_ + 1, 0:288].broadcast_to([ROWS, XL, 288]),
                    scalar=-1.0 / PATCH_DIM, in1=xs[0:ROWS, :, c0:c0 + 288], op0=ALU.mult, op1=ALU.add)\
                    .then_inc(xc_done, 1)
            dve.wait_ge(first_w, XL)
            for f in range(1, SHIFTS):
                dve.wait_ge(pw_in[f], 16)
                if f > 1:
                    dve.wait_ge(fold, f - 1)
                for s in range(POOL_SLOTS):
                    c = f * XL + s
                    ins = nc.vector.scalar_tensor_tensor(
                        out=weff[0:PIX, s, :], in0=pw[0:PIX, f, s, :], scalar=lnw_s[0:PIX, c:c + 1],
                        in1=weff[0:PIX, s, :], op0=ALU.mult, op1=ALU.add)
                ins.then_inc(fold, 1)
            dve.wait_ge(bias_mm, 1)
            nc.vector.tensor_copy(bias[:, :], ps[:, 0, 0:D]).then_inc(bias_ev, 1)
            dve.wait_ge(var_mm, 1)
            nc.vector.tensor_scalar(var[:, 0:4, 0], ps[:, 3, 0:4], 1.0 / PATCH_DIM, EPS, ALU.mult, ALU.add)
            nc.vector.tensor_scalar(var[0:64, 4:5, 0], ps[0:64, 3, 4:5], 1.0 / PATCH_DIM, EPS,
                                    ALU.mult, ALU.add).then_inc(var_ev, 1)
            dve.wait_ge(rs_done, 1)
            chain = 0

            def norm(t, which, chain):
                n = rows(t)
                nc.vector.bn_stats(st[0:n, t, :], h[0:n, t, :]).then_inc(ln_chain, 1)
                dve.wait_ge(ln_chain, chain + 1)
                nc.vector.bn_aggr(mv[0:n, t, :], st[0:n, t, :]).then_inc(ln_chain, 1)
                dve.wait_ge(ln_chain, chain + 2)
                nc.vector.tensor_scalar(ve[0:n, t, :], mv[0:n, t, 1:2], EPS, None, ALU.add)\
                    .then_inc(ve_done, 1)
                return chain + 2

            def normed(t, which):
                n = rows(t)
                dve.wait_ge(rl_done, which * TT + t + 1)
                nc.vector.tensor_scalar(hn[0:n, t, 0:D], h[0:n, t, :], mv[0:n, t, 0:1], rl[0:n, t, :],
                                        ALU.subtract, ALU.mult).then_inc(hn_done, 1)
            dve.wait_ge(bias_ev, 1)
            for t in range(TT):
                n = rows(t)
                dve.wait_ge(proj_mm, t + 1)
                nc.vector.scalar_tensor_tensor(out=h[0:n, t, :], in0=ps[0:n, PROJ_BANK[t], 0:D],
                                               scalar=rs[0:n, t, :], in1=bias[0:n, :], op0=ALU.mult,
                                               op1=ALU.add).then_inc(h_done, 1)
                dve.wait_ge(h_done, t + 1)
                chain = norm(t, 0, chain)
                if t >= 1:
                    normed(t - 1, 0)
            normed(TT - 1, 0)
            dve.wait_ge(small_in, 16 * 7)
            dve.wait_ge(hn_done, TT)
            nc.vector.tensor_tensor(out=h[:, 0:4, :], in0=h[:, 0:4, :], in1=bout_s.broadcast_to([P, 4, D]),
                                    op=ALU.add).then_inc(h_out_b, 1)
            nc.vector.tensor_tensor(out=h[0:64, 4:5, :], in0=h[0:64, 4:5, :], in1=bout_s[0:64],
                                    op=ALU.add).then_inc(h_out_b, 1)

            dve.wait_ge(hT_ev, 4)
            nc.vector.memset(ps[:, 4:6, 0:HP * N], 0.0).then_inc(s_cleared, 1)

            def negated_dots(s):
                dve.wait_ge(s_mm, s + 1)
                wait(dve, dropped, s)
                for odd in range(2):
                    nc.vector.scalar_tensor_tensor(
                        out=dd[:, odd * HP:(odd + 1) * HP, ::-1],
                        in0=ps[:, 4 + odd, 0:HP * N].rearrange("p (m n) -> p m n", m=HP), scalar=-1.0,
                        in1=const("diag").unsqueeze(1).broadcast_to([P, HP, N]), op0=ALU.mult, op1=ALU.add)\
                        .then_inc(d_ev, 1)
                dve.wait_ge(d_ev, 2 * s + 2)
                nc.vector.tensor_reduce(sraw[:, 0, :], dd.rearrange("p h n -> p n h"), axis=AX.X,
                                        op=ALU.add).then_inc(se_sum, 1)
                for g in range(HEADS):
                    ins = nc.vector.max(out=mx[:, g, :], in_=dd[:, g, :])
                ins.then_inc(top8, 1)

            def drop(s, par):
                dve.wait_ge(se_sum, s + 1)
                dve.wait_ge(top8, s + 1)
                nc.vector.scalar_tensor_tensor(out=se[:, 0, :], in0=sraw[:, 0, :], scalar=-1.0 / HEADS,
                                               in1=const("diag_out"), op0=ALU.mult, op1=ALU.add)\
                    .then_inc(se_done, 1)
                for g in range(HEADS):
                    ins = nc.vector.match_replace(out=rr[par][:, g, :], in_to_replace=mx[:, g, :],
                                                  in_values=dd[:, g, :], imm_value=BIG)
                ins.then_inc(dropped, 1)

            def row_max(s, par):
                dve.wait_ge(logit, s + 1)
                nc.vector.tensor_reduce(rowm[:, :, 0:1], rr[par], axis=AX.X, op=ALU.max).then_inc(rmax, 1)

            def row_sums(s, par):
                dve.wait_ge(expd, s + 1)
                nc.vector.tensor_reduce(sums[:, :, 0:1], ee[par], axis=AX.X, op=ALU.add).then_inc(summed, 1)
                dve.wait_ge(summed, s + 1)
                wait(dve, probs, 2 * s)
                nc.vector.reciprocal(inv, sums).then_inc(invd, 1)

            def pair(s, par):
                negated_dots(s)
                row_max(s - 1, 1 - par)
                drop(s, par)
                row_sums(s - 1, 1 - par)
            negated_dots(0)
            drop(0, 0)
            pair(1, 1)
            with dve.Fori(1, PAIRS // 2) as i:
                for par in range(2):
                    pair(2 * i + par, par)
            row_max(PAIRS - 1, 1)
            row_sums(PAIRS - 1, 1)

            dve.wait_ge(h_out_b, 2)
            for t in range(TT):
                n = rows(t)
                dve.wait_ge(om_mm, t + 1)
                nc.vector.tensor_tensor(out=h[0:n, t, :], in0=ps[0:n, 4 + t % 2, 0:D], in1=h[0:n, t, :],
                                        op=ALU.add).then_inc(h2_done, 1)
                dve.wait_ge(h2_done, t + 1)
                chain = norm(t, 1, chain)
                if t >= 1:
                    normed(t - 1, 1)
            normed(TT - 1, 1)
            for i in range(2):
                ins = nc.vector.memset(xT[i][DH:DH + 1, 1, :], 1.0)
            ins.then_inc(set_up, 1)

            n_route = 0

            def link(ins):
                nonlocal n_route
                n_route += 1
                ins.then_inc(route, 1)
                dve.wait_ge(route, n_route)
            dve.wait_ge(lg_mm, TT)
            nc.vector.tensor_tensor(out=lg[:, 0:4, :], in0=ps[:, 7, 0:4 * EXP].rearrange("p (t e) -> p t e", e=EXP),
                                    in1=bs_s.broadcast_to([P, 4, EXP]), op=ALU.add)
            link(nc.vector.tensor_tensor(out=lg[0:64, 4:5, :],
                                         in0=ps[0:64, 7, 4 * EXP:5 * EXP].rearrange("p (t e) -> p t e", e=EXP),
                                         in1=bs_s[0:64], op=ALU.add))
            link(nc.vector.tensor_reduce(lm[:, :, :], lg[:, :, :], axis=AX.X, op=ALU.max))
            nc.vector.tensor_tensor(out=le[:, :, :], in0=lg[:, :, :], in1=lm[:, :, :].broadcast_to([P, TT, EXP]),
                                    op=ALU.subtract).then_inc(lsub, 1)
            for t in range(TT):
                ins = nc.vector.max(out=mx8[:, t, :], in_=lg[:, t, :])
            link(ins)
            for t in range(TT):
                ins = nc.vector.max_index(out=ix8[:, t, :], in_max=mx8[:, t, :], in_values=lg[:, t, :])
            link(ins)
            link(nc.vector.tensor_copy(ixf[:, :, :], ix8[:, :, 0:1]))
            nc.vector.tensor_tensor(out=oh[:, :, :], in0=ixf[:, :, :].broadcast_to([P, TT, EXP]),
                                    in1=const("iota").unsqueeze(1).broadcast_to([P, TT, EXP]),
                                    op=ALU.is_equal).then_inc(oh_done, 1)
            dve.wait_ge(oh_done, 1)
            nc.vector.tensor_copy(pf[:, 1, :], oh[:, 0, 1:EXP]).then_inc(pf_done, 1)
            for t in range(1, TT):
                dve.wait_ge(pf_done, t)
                nc.vector.tensor_tensor(out=pf[:, t + 1, :], in0=pf[:, t, :], in1=oh[:, t, 1:EXP], op=ALU.add)\
                    .then_inc(pf_done, 1)
            nc.vector.tensor_scalar(routed[:, :, :], oh[:, :, 0:1], -1.0, 1.0, ALU.mult, ALU.add)
            dve.wait_ge(le_exp, 1)
            link(nc.vector.tensor_reduce(ls[:, :, :], le[:, :, :], axis=AX.X, op=ALU.add))
            link(nc.vector.reciprocal(pr[:, :, :], ls[:, :, :]))
            link(nc.vector.tensor_tensor(out=pe_w[:, :, :], in0=pr[:, :, :], in1=routed[:, :, :], op=ALU.mult))
            link(nc.vector.tensor_scalar(ome[:, :, :], pe_w[:, :, :], -1.0, 1.0, ALU.mult, ALU.add))
            nc.vector.tensor_tensor(out=cmix[:, :, 1:EXP], in0=oh[:, :, 1:EXP],
                                    in1=pe_w[:, :, :].broadcast_to([P, TT, EXP - 1]), op=ALU.mult)\
                .then_inc(cm_done, 1)
            nc.vector.tensor_copy(cmix[:, :, 0:1], ome[:, :, :]).then_inc(cm_done, 1)

            dve.wait_ge(rank_mm, 1)
            link(nc.vector.tensor_copy(nsum[:, :, 0], ps[:, 6, TT * 8:TT * 8 + 8]))
            link(nc.vector.tensor_tensor(out=over[:, :, :], in0=nsum[:, :, :].broadcast_to([P, 8, STEPS]),
                                         in1=const("steps").rearrange("p (e k) -> p e k", e=8),
                                         op=ALU.is_gt))
            link(nc.vector.tensor_reduce(ntile[:, :, :], over[:, :, :], axis=AX.X, op=ALU.add))
            link(nc.vector.tensor_tensor(out=prod[:, :, :],
                                         in0=ntile[:, :, :].rearrange("p e o -> p o e").broadcast_to([P, 8, 8]),
                                         in1=const("tri").rearrange("p (e k) -> p e k", e=8), op=ALU.mult))
            link(nc.vector.tensor_reduce(cum[:, :, :], prod[:, :, :], axis=AX.X, op=ALU.add))
            link(nc.vector.tensor_tensor(out=base[:, 0, :], in0=cum[:, :, 0], in1=ntile[:, :, 0],
                                         op=ALU.subtract))
            link(nc.vector.tensor_scalar(base[:, 0, :], base[:, 0, :], float(GS), None, ALU.mult))
            link(nc.vector.tensor_tensor(out=rb[:, :, :],
                                         in0=ps[:, 6, 0:TT * 8].rearrange("p (t e) -> p t e", e=8),
                                         in1=base[:, :, :].broadcast_to([P, TT, 8]), op=ALU.add))
            link(nc.vector.tensor_tensor(out=rb2[:, :, :], in0=rb[:, :, :], in1=oh[:, :, 1:EXP], op=ALU.mult))
            nc.vector.tensor_tensor(out=spare[:, :, 0], in0=oh[:, :, 0], in1=const("spare"), op=ALU.mult)
            link(nc.vector.tensor_reduce(slot[:, :, :], rb2[:, :, :], axis=AX.X, op=ALU.add))
            link(nc.vector.tensor_tensor(out=slot_s[:, :, :], in0=slot[:, :, :], in1=spare[:, :, :], op=ALU.add))
            nc.vector.tensor_copy(hn[:, :, D], pr[:, :, 0]).then_inc(slots_done, 1)
            nc.vector.tensor_copy(hn[:, :, D + 1], const("token")).then_inc(slots_done, 1)
            nc.vector.tensor_copy(idx_s[:, :], slot_s[:, :, 0]).then_inc(slots_done, 1)
            link(nc.vector.tensor_tensor(
                out=tge[:, :, :], in0=const("group", 0, 1).unsqueeze(2).broadcast_to([1, 2 * TILES, 8]),
                in1=cum[0:1, :, :].rearrange("p e o -> p o e").broadcast_to([1, 2 * TILES, 8]), op=ALU.is_ge))
            link(nc.vector.tensor_reduce(tex[:, :, :], tge[:, :, :], axis=AX.X, op=ALU.add))
            link(nc.vector.tensor_scalar(tex2[:, :, :], tex[:, :, :], float(EXP - 2), 1.0, ALU.min, ALU.add))
            nc.vector.tensor_copy(texi[:, :], tex2[:, :, 0]).then_inc(texp_done, 1)
            def second_up(s):
                e = dve.value_load(texi[0:1, 2 * s + 1:2 * s + 2], min_val=1, max_val=EXP - 1)
                wait(dve, f1_mm, s - 1)
                for k, (n, w) in enumerate(((DH, w1a), (DH + 1, w1b))):
                    ins = nc.vector.tensor_copy(wb1[s % 2][0:n, k, :], w[0:n, bass.ds(e, 1), :])
                ins.then_inc(wb1_ready, 1)

            def second_down(s):
                e = dve.value_load(texi[0:1, 2 * s + 1:2 * s + 2], min_val=1, max_val=EXP - 1)
                wait(dve, f2_mm, s - 1)
                nc.vector.tensor_copy(wb2[s % 2], w2s[:, bass.ds(e, 1), :, :]).then_inc(wb2_ready, 1)

            def xT_out(s):
                dve.wait_ge(xT_mm, s + 1)
                wait(dve, f1_mm, s - 1)
                nc.vector.tensor_copy(xT[s % 2][0:DH], ps[0:DH, (4, 7)[s % 2], 0:2 * P]
                                      .rearrange("p (k n) -> p k n", k=2)).then_inc(xT_ev, 1)

            def hT_out(s):
                dve.wait_ge(f2T_mm, s + 1)
                wait(dve, f2_mm, s - 1)
                nc.vector.tensor_copy(hT[s % 2].rearrange("p (c m) n -> p c (m n)", c=2), ps[:, HID_BANK(s):HID_BANK(s) + 2, 0:384])\
                    .then_inc(f2T_ev, 1)

            def y_out(s):
                par = s % 2
                dve.wait_ge(f2_mm, s + 1)
                dve.wait_ge(ag_in[par], 16 * (s // 2 + 1))
                wait(dve, rows_out, 16 * (s - 1))
                nc.vector.scalar_tensor_tensor(out=ys[par][:, 0, :], in0=ps[:, 5 + par, 0:D],
                                               scalar=meta[:, s, 0:1], in1=ag[par][:, 0, :], op0=ALU.mult,
                                               op1=ALU.add).then_inc(y_ev, 1)
            dve.wait_ge(texp_done, 1)
            dve.wait_ge(w1_in, 48)
            dve.wait_ge(w2_in, 16)
            for s in range(2):
                second_up(s)
                second_down(s)
            dve.wait_ge(cT_mm, 1)
            nc.vector.tensor_copy(cT[0:EXP, 0:4, :], ps[0:EXP, 7, :].rearrange("p (t n) -> p t n", t=4))\
                .then_inc(cT_ev, 1)
            nc.vector.tensor_copy(cT[0:EXP, 4, :], ps[0:EXP, 6, 0:P]).then_inc(cT_ev, 1)
            for t in range(TT):
                if t >= TT - 2:
                    xT_out(t - TT + 2)
                n = rows(t)
                dve.wait_ge(c2_mm, t + 1)
                nc.vector.scalar_tensor_tensor(out=acc[0:n, t, :], in0=ps[0:n, 2 + t % 2, 0:D], scalar=ome[0:n, t, :],
                                               in1=h[0:n, t, :], op0=ALU.mult, op1=ALU.add).then_inc(acc_a, 1)
                dve.wait_ge(b2_mm, t + 1)
                dve.wait_ge(acc_a, t + 1)
                nc.vector.tensor_tensor(out=acc[0:n, t, :], in0=ps[0:n, 5 + t % 2, 0:D], in1=acc[0:n, t, :],
                                        op=ALU.add).then_inc(acc_b, 1)
            dve.wait_ge(meta_in, 16)
            nc.vector.tensor_copy(row_i[:, :], meta[:, :, 1]).then_inc(rows_ready, 1)
            for s in range(TILES):
                if s + 2 < TILES:
                    second_up(s + 2)
                    xT_out(s + 2)
                if 1 <= s < TILES - 1:
                    y_out(s - 1)
                hT_out(s)
                if 1 <= s < TILES - 1:
                    second_down(s + 1)
            y_out(TILES - 2)
            y_out(TILES - 1)

        @block.scalar
        def _(act):
            act.wait_ge(lnw_in, 32)
            act.wait_ge(pw_in[0], 16)
            act.wait_ge(ph_in, 16)
            for s in range(XL):
                nc.scalar.activation(weff[0:ROWS, s, :], pw[0:ROWS, 0, s, :], ACT.Copy,
                                           scale=lnw_s[0:ROWS, s:s + 1]).then_inc(first_w, 1)
            act.wait_ge(xc_done, 2)
            for s in range(XL):
                nc.scalar.activation(sq[0:ROWS, s, :], xc[0:ROWS, s, :], ACT.Square).then_inc(sq_done, 1)
            act.wait_ge(bias4_mm, 1)
            nc.scalar.activation(bias4[:, :], ps[:, 2, 0:D], ACT.Copy).then_inc(bias4_ev, 1)
            act.wait_ge(sq4_mm, 1)
            nc.scalar.activation(sqsum.rearrange("p o (a n) -> p (o a) n", a=2), ps[:, 6:8, 0:288], ACT.Copy)\
                .then_inc(sqsum_done, 1)

            def hT_out(i, t, bank, to):
                act.wait_ge(hT_mm, i + 1)
                n = rows(t)
                nc.scalar.activation(to[:, :, t * P:t * P + n],
                                     ps[0:DH, bank, 0:2 * P].rearrange("p (k n) -> p k n", k=2)[:, :, 0:n],
                                     ACT.Copy).then_inc(hT_ev, 1)
            for t in range(3):
                hT_out(t, t, HN_BANK[t], hnT)

            act.wait_ge(small_in, 16 * 7)
            for half_ in range(2):
                for m in range(HP):
                    if half_ == 0 and m in (1, 2):
                        hT_out(2 + m, 2 + m, HN_BANK[2 + m], hnT)
                    for which in range(2):
                        n = (half_ * HP + m) * 2 + which
                        act.wait_ge(qk_mm, n + 1)
                        nc.scalar.activation((qT, kT)[which][:, m, half_ * 288:half_ * 288 + 288],
                                             ps[:, (2, 3, 0, 1)[n % 4], 0:288], ACT.Copy,
                                             scale=(scq[:, m:m + 1], 1.0)[which]).then_inc(qk_ev, 1)

            def v_out(s, par):
                act.wait_ge(v_mm, s + 1)
                wait(act, av_mm, s - 1)
                nc.scalar.activation(vv[par][0:PT].rearrange("p (c h) d -> p c (h d)", c=2), ps[0:PT, 2:4, 0:384],
                                     ACT.Copy).then_inc(v_ev, 1)

            def pT_out(s):
                for c, bank in enumerate((0, 1, 7)):
                    act.wait_ge(t_mm, 3 * s + c + 1)
                    if c == 0:
                        wait(act, av_mm, s)
                    nc.scalar.activation(
                        pT[0:PT, 4 * c:4 * c + 4, :, :],
                        ps[0:PT, bank, :].rearrange("p (g b n) -> p g b n", g=4, b=2)[:, :, :, 0:N],
                        ACT.Copy).then_inc(t_ev, 1)

            def o_out(s):
                act.wait_ge(av_mm, s + 1)
                nc.scalar.activation(oT[:, :, bass.ds(s * PT, PT)],
                                     ps[:, 6, 0:HP * PT].rearrange("p (m n) -> p m n", m=HP), ACT.Copy)\
                    .then_inc(o_ev, 1)

            def exps(s, par):
                act.wait_ge(shifted, s + 1)
                wait(act, probs, 2 * s - 2)
                nc.scalar.activation(ee[par], rr[par], ACT.Exp).then_inc(expd, 1)

            exps(0, 0)
            v_out(0, 0)
            v_out(1, 1)

            def pair(s, par):
                pT_out(s - 3)
                exps(s - 2, par)
                o_out(s - 3)
                v_out(s - 1, 1 - par)
            pair(3, 1)
            pair(4, 0)
            with act.Fori(2, PAIRS // 2) as i:
                for par in range(2):
                    pair(2 * i + 1 + par, 1 - par)
            exps(PAIRS - 1, 1)
            for s in (PAIRS - 2, PAIRS - 1):
                pT_out(s)
                o_out(s)

            for t in range(TT):
                hT_out(TT + t, t, XN_BANK[t], xnT)
            act.wait_ge(lsub, 1)
            nc.scalar.activation(le[:, :, :], le[:, :, :], ACT.Exp).then_inc(le_exp, 1)
            for m in range(FM):
                act.wait_ge(c1_mm, 2 * m + 2 if m else 3)
                nc.scalar.activation(hcT[:, m, :].rearrange("p (a n) -> p a n", a=2),
                                     ps[:, m % 3 * 2:m % 3 * 2 + 2, 0:288], ACT.Gelu,
                                     bias=b1_s[:, m:m + 1]).then_inc(c1_ev, 1)

            for s in range(TILES):
                act.wait_ge(f1_mm, s + 1)
                wait(act, f2T_mm, s - 1)
                nc.scalar.activation(hs[s % 2].rearrange("p (c m) n -> p c (m n)", c=2), ps[:, 0:2, 0:384],
                                     ACT.Gelu).then_inc(f1_ev, 1)

        @block.gpsimd
        def _(pool):
            for i in range(2):
                nc.gpsimd.memset(pblk[i][:, :, :], 0.0).then_inc(zeroed, 1)
            pool.wait_ge(zeroed, 2)
            nc.gpsimd.memset(empty[:, :, :], 0.0).then_inc(empty_set, 1)
            pool.wait_ge(empty_set, 1)
            nc.gpsimd.memset(empty[:, :, D + 1:ROW], float(TOK)).then_inc(empty_set, 1)
            pool.wait_ge(first_w, XL)
            for f in range(1, SHIFTS):
                pool.wait_ge(pw_in[f], 16)
                wait(pool, fold_pool, 2 * f - 2)
                c = slice(f * XL + POOL_SLOTS, (f + 1) * XL)
                nc.gpsimd.tensor_tensor(out=scaled[0:PIX], in0=pw[0:PIX, f, POOL_SLOTS:, :],
                                        in1=lnw_s[0:PIX, c].unsqueeze(2).broadcast_to([PIX, XL - POOL_SLOTS, D]),
                                        op=ALU.mult).then_inc(fold_pool, 1)
                pool.wait_ge(fold_pool, 2 * f - 1)
                nc.gpsimd.tensor_tensor(out=weff[0:PIX, POOL_SLOTS:, :], in0=scaled[0:PIX],
                                        in1=weff[0:PIX, POOL_SLOTS:, :], op=ALU.add).then_inc(fold_pool, 1)
            pool.wait_ge(set_up, 2)
            pool.wait_ge(var_ev, 1)
            nc.gpsimd.tensor_tensor(out=rs[:, :, 0], in0=var[:, :, 0], in1=half[:, :].broadcast_to([P, TT]),
                                    op=ALU.pow).then_inc(rs_done, 1)

            def rstd(i, t):
                pool.wait_ge(ve_done, i + 1)
                n = rows(t)
                nc.gpsimd.tensor_tensor(out=rl[0:n, t, :], in0=ve[0:n, t, :], in1=half[0:n, :],
                                        op=ALU.pow).then_inc(rl_done, 1)
            for t in range(TT):
                rstd(t, t)
            pool.wait_ge(zeros_out, 48)
            pool.wait_ge(cst_in, 16)

            def logits(s, par):
                pool.wait_ge(dropped, s + 1)
                pool.wait_ge(se_done, s + 1)
                nc.gpsimd.tensor_tensor(out=rr[par], in0=se.broadcast_to([P, HEADS, N]), in1=rr[par],
                                        op=ALU.subtract).then_inc(logit, 1)

            def less_max(s, par):
                pool.wait_ge(rmax, s + 1)
                wait(pool, probs, 2 * s)
                nc.gpsimd.tensor_tensor(out=rr[par], in0=rr[par], in1=rowm.broadcast_to([P, HEADS, N]),
                                        op=ALU.subtract).then_inc(shifted, 1)

            def normalise(s, par):
                pool.wait_ge(expd, s + 1)
                pool.wait_ge(invd, s + 1)
                pool.wait_ge(logit, min(PAIRS, s + 2) if isinstance(s, int) else s + 2)
                wait(pool, t_mm, 3 * s - 3)
                for b in range(2):
                    r = slice(64 * b, 64 * b + 64)
                    nc.gpsimd.tensor_tensor(out=pblk[par][r, :, b * N:(b + 1) * N], in0=ee[par][r, :, ::-1],
                                            in1=inv[r].broadcast_to([64, HEADS, N]), op=ALU.mult)\
                        .then_inc(probs, 1)
            logits(0, 0)
            less_max(0, 0)
            logits(1, 1)
            normalise(0, 0)
            with pool.Fori(1, PAIRS // 2) as i:
                for par in range(2):
                    s = 2 * i + par
                    less_max(s - 1, 1 - par)
                    logits(s, par)
                    normalise(s - 1, 1 - par)
            less_max(PAIRS - 1, 1)
            pool.wait_ge(shifted, PAIRS)
            normalise(PAIRS - 1, 1)

            pool.wait_ge(probs, 2 * PAIRS)
            for t in range(TT):
                rstd(TT + t, t)
            pool.wait_ge(slots_done, 3)
            pool.wait_ge(hn_done, 2 * TT)
            for t in range(TT):
                n = rows(t)
                nc.gpsimd.indirect_dma_start(
                    out=xg_dram, out_offset=bass.IndirectOffsetOnAxis(ap=idx_s[0:n, t:t + 1], axis=0),
                    in_=hn[0:n, t, :], in_offset=None).then_inc(scattered, 16)
            pool.wait_ge(rows_ready, 1)
            pool.wait_ge(stored, 32 * TT)

            def common_rows(s):
                wait(pool, y_ev, s - 1)
                nc.gpsimd.indirect_dma_start(
                    out=ag[s % 2][:, 0, :], out_offset=None, in_=acc_dram,
                    in_offset=bass.IndirectOffsetOnAxis(ap=row_i[:, s:s + 1], axis=0)).then_inc(ag_in[s % 2], 16)
            common_rows(0)
            common_rows(1)
            for s in range(TILES):
                pool.wait_ge(y_ev, s + 1)
                wait(pool, rows_out, 16 * s)
                nc.gpsimd.indirect_dma_start(
                    out=out, out_offset=bass.IndirectOffsetOnAxis(ap=row_i[:, s:s + 1], axis=0),
                    in_=ys[s % 2][:, 0, :], in_offset=None).then_inc(rows_out, 16)
                if s + 2 < TILES:
                    common_rows(s + 2)


def kernel(x, L0_tok_ln_weight, L0_tok_ln_bias, L0_tok_proj_weight, L0_tok_proj_bias, L0_attn_w_qkv,
           L0_attn_scale, L0_attn_w_out, L0_attn_b_out, L0_ffn_Ws, L0_ffn_bs, L0_ffn_W1, L0_ffn_b1,
           L0_ffn_W2, L0_ffn_b2):
    import concourse.bacc as bacc
    from concourse.bass_utils import run_bass_kernel_spmd

    def whole(a):
        return np.ascontiguousarray(a)

    xi = np.asarray(x).reshape(B, C, IMG, IMG)
    xp = np.pad(xi, ((0, 0), (0, 0), (1, 1), (1, 1)))

    def patches(dy, dx):
        v = xp[:, :, 1 + dy:1 + dy + IMG, 1 + dx:1 + dx + IMG]
        return v.reshape(B, C, SIDE, PATCH, SIDE, PATCH).transpose(1, 3, 5, 0, 2, 4).reshape(
            C, PATCH, PATCH, TOK)

    def halo(left, right, top, bottom):
        s = np.stack([left, right, top, bottom])
        return s.reshape(4, C, 2, 8, -1).transpose(1, 3, 0, 2, 4).reshape(HALO, XL, -1)
    xk = np.concatenate([
        patches(0, 0).reshape(PIX, XL, TOK),
        halo(patches(0, -1)[:, :, 0], patches(0, 1)[:, :, PATCH - 1],
             patches(-1, 0)[:, 0], patches(1, 0)[:, PATCH - 1])])

    def by_pixel(a):
        w = np.moveaxis(np.asarray(a), -1, 0).reshape(PATCH, PATCH, SHIFTS, C, -1).transpose(2, 3, 0, 1, 4)
        z = np.pad(w, ((0, 0), (0, 0), (1, 1), (1, 1), (0, 0)))
        to = ((0, 0), (0, 1), (0, -1), (1, 0), (-1, 0))
        body = np.stack([z[f, :, 1 + dy:1 + dy + PATCH, 1 + dx:1 + dx + PATCH]
                         for f, (dy, dx) in enumerate(to)])
        body = body.reshape(SHIFTS, PIX, XL, -1).transpose(1, 0, 2, 3)
        edge = halo(w[1][:, :, 0], w[2][:, :, PATCH - 1], w[3][:, 0], w[4][:, PATCH - 1])
        return body, edge

    def vector(a):
        body, edge = by_pixel(np.asarray(a).reshape(1, -1))
        table = np.zeros((ROWS, SHIFTS, XL), body.dtype)
        table[:PIX] = body[..., 0]
        table[PIX:, 0] = edge[..., 0]
        return table.reshape(ROWS, SHIFTS * XL)
    pk, ph = by_pixel(L0_tok_proj_weight)
    w1 = np.asarray(L0_ffn_W1).transpose(1, 0, 2)
    w2 = np.asarray(L0_ffn_W2).reshape(EXP, FM, P, D).transpose(2, 0, 1, 3)
    arrays = {
        "xk": xk, "pk": pk, "ph": ph, "lnw": vector(L0_tok_ln_weight), "lnb": vector(L0_tok_ln_bias),
        "pb": np.asarray(L0_tok_proj_bias).reshape(1, D),
        "wqkv": np.asarray(L0_attn_w_qkv).reshape(2, DH, 3 * INNER).transpose(1, 0, 2),
        "scale": np.repeat(np.asarray(L0_attn_scale).reshape(HP, 2).T, HD, axis=0),
        "wout": np.asarray(L0_attn_w_out).reshape(HP, P, D).transpose(1, 0, 2),
        "bout": np.asarray(L0_attn_b_out).reshape(1, D),
        "ws": np.asarray(L0_ffn_Ws).reshape(2, DH, EXP).transpose(1, 0, 2),
        "bs": np.asarray(L0_ffn_bs).reshape(1, EXP),
        "w1": w1, "b1": np.asarray(L0_ffn_b1).reshape(1, EXP, FF), "w2": w2, "b2": np.asarray(L0_ffn_b2),
        "b1c": np.asarray(L0_ffn_b1)[0].reshape(FM, P).T,
        "consts": constants(),
    }
    arrays = {f"{k}_dram": whole(v) for k, v in arrays.items()}
    nc = bacc.Bacc("TRN2", target_bir_lowering=False, num_devices=1)
    args = [nc.dram_tensor(k, v.shape, mybir.dt.from_np(v.dtype), kind="ExternalInput").ap()
            for k, v in arrays.items()]
    out = nc.dram_tensor("out_dram", (TOK + 1, D), mybir.dt.float32, kind="ExternalOutput").ap()
    build(nc, *args, out)
    r = run_bass_kernel_spmd(nc, [arrays], core_ids=[0])
    return r.results[0]["out_dram"][:TOK].reshape(B, N, D)
```

```python
import numpy as np
import concourse.bass as bass
from concourse import mybir
from contextlib import ExitStack

B, C, IMG, PATCH, SIDE = 16, 3, 96, 16, 6
N = SIDE * SIDE
TOK = B * N
D = 192
DH = D // 2
XL = 8
PIX = C * PATCH * 2
HALO = 4 * C * PATCH // XL
ROWS = PIX + HALO
SHIFTS = 5
PATCH_DIM = PATCH * PATCH * C * SHIFTS
HEADS, HD = 12, 64
INNER = HEADS * HD
HP = HEADS // 2
KEEP = int(N * 0.75)
assert N - 1 - KEEP == 8
PAIRS = B // 2
PT = 2 * N
EXP, FF = 9, 768
FM = FF // 128
P = 128
TT = (TOK + P - 1) // P
GS = 64
GROUPS = (TOK + (EXP - 1) * (GS - 1)) // GS
TILES = (GROUPS + 1) // 2
SLOTS = TILES * P
STEPS = (TOK + GS - 1) // GS
ROW = D + 2
BIG = 1e30
EPS = 1e-5

POOL_SLOTS = 6

PROJ_BANK = (4, 5, 6, 1, 4)
HN_BANK = (7, 0, 7, 5, 6)
XN_BANK = (2, 3, 2, 3, 6)


def hidden_bank(s):
    return 2 if s < TILES - 1 else 0


def rows(t):
    return min(P, TOK - t * P)


CONST = {}
_at = 0
for _n, _w in (("ident", P), ("upper", P), ("diag", N), ("diag_out", N), ("tri", 64), ("iota", EXP),
               ("steps", 8 * STEPS), ("group", 2 * TILES), ("spare", TT), ("token", TT), ("count", XL)):
    CONST[_n] = (_at, _at + _w)
    _at += _w
CONST_W = _at


def constants():
    t = np.zeros((P, CONST_W), np.float32)

    def col(n):
        return t[:, CONST[n][0]:CONST[n][1]]

    col("ident")[:] = np.eye(P)
    col("upper")[:] = np.triu(np.ones((P, P)), 1)
    for p in range(P):
        if p % 64 < N:
            col("diag")[p, p % 64] = -BIG
            col("diag_out")[p, N - 1 - p % 64] = -3 * BIG
    col("tri")[:] = np.tril(np.ones((8, 8))).reshape(-1)
    col("iota")[:] = np.arange(EXP)
    col("steps")[:] = np.tile(np.arange(STEPS) * GS, 8)
    col("group")[:] = np.arange(2 * TILES)
    col("token")[:] = np.arange(P)[:, None] + P * np.arange(TT)
    col("spare")[:] = SLOTS + col("token")
    cnt = np.ones((C, PATCH, PATCH))
    cnt[:, :, 1:] += 1
    cnt[:, :, :-1] += 1
    cnt[:, 1:, :] += 1
    cnt[:, :-1, :] += 1
    col("count")[:PIX] = cnt.reshape(PIX, XL)
    col("count")[PIX:ROWS] = 1
    return t


def build(nc, xk, pk, ph, lnw, lnb, pb, wqkv, scale, wout, bout, ws, bs, w1, b1, w2, b2, b1c, consts, out):
    fp32 = mybir.dt.float32
    fp22 = mybir.dt.float32r
    u32 = mybir.dt.uint32
    i32 = mybir.dt.int32
    ALU = mybir.AluOpType
    ACT = mybir.ActivationFunctionType
    AX = mybir.AxisListType

    xg_dram = nc.dram_tensor("xg_scratch", (SLOTS + TT * P, ROW), fp32).ap()
    acc_dram = nc.dram_tensor("acc_scratch", (TOK + 1, D), fp32).ap()

    with ExitStack() as ctx:
        def sb(name, shape, dt=fp32):
            return ctx.enter_context(nc.sbuf_tensor(name, shape, dt))

        def sem(name):
            return ctx.enter_context(nc.semaphore(name))

        A_W = 2 * EXP * FF + EXP * FM * D
        with nc.sbuf_tensor("region_tokenizer", [P, A_W], fp32) as region:
            pass
        with nc.sbuf_tensor("wq_high", [P, 6 * INNER], fp22) as wq_high_all:
            pass
        region_experts = sb("region_experts", [P, A_W])
        at = 0

        def take(width, shape, **kw):
            nonlocal at
            v = region[:, at:at + width].rearrange(shape, **kw)
            at += width
            return v
        xs = take(XL * TOK, "p (s n) -> p s n", s=XL)
        xc = take(XL * TOK, "p (s n) -> p s n", s=XL)
        pw = take(SHIFTS * XL * D, "p (f s d) -> p f s d", f=SHIFTS, s=XL)
        weff = take(XL * D, "p (s d) -> p s d", s=XL)
        sq = take(XL * TOK, "p (s n) -> p s n", s=XL)
        xsum = take(TOK, "p (a n) -> p a n", a=1)
        sqsum = take(TOK, "p (a n) -> p a n", a=1)
        assert at <= A_W, (at, A_W)
        COMMON = EXP - 1
        w1a = region_experts[:, 0:EXP * FF].rearrange("p (e f) -> p e f", e=EXP)
        w1b = region_experts[:, EXP * FF:2 * EXP * FF].rearrange("p (e f) -> p e f", e=EXP)
        w2s = region_experts[:, 2 * EXP * FF:A_W].rearrange("p (e m d) -> p e m d", e=EXP, m=FM)

        cst = sb("cst", [P, CONST_W])

        def const(n, p0=0, p1=P):
            return cst[p0:p1, CONST[n][0]:CONST[n][1]]
        ones = sb("ones", [P, P])
        half = sb("half", [P, 1])
        lnw_s = sb("lnw_s", [P, SHIFTS * XL])
        lnb_s = sb("lnb_s", [P, SHIFTS * XL])
        rowv = sb("rowv", [1, D])
        bout_s = sb("bout_s", [P, 1, D])
        bs_s = sb("bs_s", [P, 1, EXP])
        with nc.sbuf_tensor("wq_s", [P, 6 * INNER], fp32) as wq_all:
            pass
        with nc.sbuf_tensor("wq_low", [P, 6 * INNER], fp22) as wq_low_all:
            pass
        wb1_all = sb("second_up_w", [P, 4 * FF])
        common_low = sb("common_up_low", [P, 2 * FF], fp22)[0:DH, :].rearrange("p (k f) -> p k f", k=2)
        wq_s, wq_high, wq_low = (w[0:DH, :].rearrange("p (k n) -> p k n", k=2)
                                 for w in (wq_all, wq_high_all, wq_low_all))
        wo_s = sb("wo_s", [P, HP, D])
        ws_s = sb("ws_s", [DH, 2, EXP])
        b2_s = sb("b2_s", [EXP, D])
        b1_s = sb("b1_s", [P, FM])
        scq = sb("scq", [P, HP])
        nscq = sb("nscq", [P, HP])
        bias = sb("bias", [P, D])
        var = sb("var", [P, TT, 1])
        rs = sb("rs", [P, TT, 1])
        h = sb("h", [P, TT, D])
        hn = sb("hn", [P, TT, ROW])
        st = sb("st", [P, TT, 6])
        mv = sb("mv", [P, TT, 2])
        ve = sb("ve", [P, TT, 1])
        rl = sb("rl", [P, TT, 1])
        with nc.sbuf_tensor("hnT_high", [DH, 2, TOK], fp22) as hnT_high:
            pass
        xnT = sb("xnT", [DH, 2, TOK])
        hnT_low = sb("hnT_low", [DH, 2, TOK], fp22)
        with nc.sbuf_tensor("qT", [P, HP, TOK], fp32) as qT:
            pass
        wb2_all = sb("second_down_w", [P, 2 * FM * D])
        xn_high = sb("xn_high", [DH, 2, TOK], fp22)
        xn_low = hnT_low
        kT = sb("kT", [P, HP, TOK])
        oT = kT
        hcT = oT[:, :, :]

        with nc.sbuf_tensor("before_common_high", [P, 5000], fp32) as _:
            with nc.sbuf_tensor("common_up_high", [P, 2 * FF], fp22) as common_high_all:
                pass
        common_high = common_high_all[0:DH, :].rearrange("p (k f) -> p k f", k=2)
        work = sb("work", [P, 6912])
        at = 0

        def take2(width, shape, **kw):
            nonlocal at
            v = work[:, at:at + width].rearrange(shape, **kw)
            at += width
            return v
        vv = [take2(INNER, "p (h d) -> p h d", h=HEADS) for _ in range(2)]
        dd = take2(HEADS * N, "p (h n) -> p h n", h=HEADS)
        rr = [take2(HEADS * N, "p (h n) -> p h n", h=HEADS) for _ in range(2)]
        ee = [take2(HEADS * N, "p (h n) -> p h n", h=HEADS) for _ in range(2)]
        pT = take2(HEADS * PT, "p (h b n) -> p h b n", h=HEADS, b=2)
        sraw = take2(N, "p (h n) -> p h n", h=1)
        mx = take2(HEADS * 8, "p (h n) -> p h n", h=HEADS)
        se = take2(N, "p (h n) -> p h n", h=1)
        rowm = take2(HEADS, "p (h n) -> p h n", h=HEADS)
        sums = take2(HEADS, "p (h n) -> p h n", h=HEADS)
        inv = take2(HEADS, "p (h n) -> p h n", h=HEADS)
        pblk = [sb(f"pblk{i}", [P, HEADS, PT]) for i in range(2)]

        assert at <= 5000
        thirty2 = work[:, 5800:5800 + P]
        bias4 = work[:, 6000:6000 + D]
        scaled = work[:, 6200:6200 + (XL - POOL_SLOTS) * D].rearrange("p (s d) -> p s d", d=D)
        empty = work[:, 5000:5000 + SLOTS // 2 // P * ROW].rearrange("p (a d) -> p a d", d=ROW)

        at = 0
        xg = [take2(D, "p (a d) -> p a d", a=1) for _ in range(2)]
        xT = [take2(2 * P, "p (k n) -> p k n", k=2) for _ in range(2)]
        hs = [take2(FF, "p (m n) -> p m n", m=FM) for _ in range(2)]
        hT = [take2(FF, "p (m n) -> p m n", m=FM) for _ in range(2)]
        ys = [take2(D, "p (a d) -> p a d", a=1) for _ in range(2)]
        ag = [take2(D, "p (a d) -> p a d", a=1) for _ in range(2)]
        acc = take2(TT * D, "p (t d) -> p t d", t=TT)
        cT = take2(TT * P, "p (t n) -> p t n", t=TT)
        wb1 = [wb1_all[:, i * 2 * FF:(i + 1) * 2 * FF].rearrange("p (k f) -> p k f", k=2) for i in range(2)]
        wb2 = [wb2_all[:, i * FM * D:(i + 1) * FM * D].rearrange("p (m d) -> p m d", m=FM) for i in range(2)]

        lg = sb("lg", [P, TT, EXP])
        le = sb("le", [P, TT, EXP])
        lm = sb("lm", [P, TT, 1])
        ls = sb("ls", [P, TT, 1])
        pr = sb("pr", [P, TT, 1])
        mx8 = sb("mx8", [P, TT, 8])
        ix8 = sb("ix8", [P, TT, 8], u32)
        ixf = sb("ixf", [P, TT, 1])
        oh = sb("oh", [P, TT, EXP])
        routed = sb("routed", [P, TT, 1])
        pe_w = sb("pe_w", [P, TT, 1])
        ome = sb("ome", [P, TT, 1])
        cmix = sb("cmix", [P, TT, EXP])
        over = sb("over", [P, 8, STEPS])
        pf = sb("pf", [P, TT + 1, 8])
        ntile = sb("ntile", [P, 8, 1])
        prod = sb("prod", [P, 8, 8])
        cum = sb("cum", [P, 8, 1])
        base = sb("base", [P, 1, 8])
        rb = sb("rb", [P, TT, 8])
        rb2 = sb("rb2", [P, TT, 8])
        slot = sb("slot", [P, TT, 1])
        spare = sb("spare", [P, TT, 1])
        slot_s = sb("slot_s", [P, TT, 1])
        idx_s = sb("idx_s", [P, TT], u32)
        tge = sb("tge", [1, 2 * TILES, 8])
        tex = sb("tex", [1, 2 * TILES, 1])
        tex2 = sb("tex2", [1, 2 * TILES, 1])
        texi = sb("texi", [1, 2 * TILES], i32)
        meta = sb("meta", [P, TILES, 2])
        row_i = sb("row_i", [P, TILES], u32)
        nsum = sb("nsum", [P, 8, 1])

        ps = ctx.enter_context(nc.psum_tensor("ps", [P, 8, 512], fp32))

        x_in = [sem(f"x_in{i}") for i in range(4)]
        lnw_in, cst_in, count_in, ph_in, wq_in, wo_in, small_in = (sem(f"{n}_in") for n in (
            "lnw", "cst", "count", "halo_w", "wqkv", "wout", "small"))
        pw_in = [sem(f"pw_in{f}") for f in range(SHIFTS)]
        w1_in, w2_in = sem("w1_in"), sem("w2_in")
        set_up, pads, zeroed = sem("ones_set"), sem("pads_zeroed"), sem("blocks_zeroed")
        xsum_done, sqsum_done = sem("pixel_sums"), sem("square_sums")
        mean_mm, xc_done, sq_done, var_mm, bias_mm, bias_ev = (sem(n) for n in (
            "mean_mm", "centred", "squared", "var_mm", "bias_mm", "bias_ev"))
        fold, fold_pool, first_w, var_ev, rs_done, proj_mm = (sem(n) for n in (
            "folded", "folded_pool", "fold_first", "var_ev", "rstd_done", "proj_mm"))
        neg_scale, high_w, low_w, hT_low, last_probs = (sem(n) for n in (
            "neg_scale", "high_weights", "low_weights", "hnT_low", "last_probs"))
        common_high_w, common_low_w, xn_high_ev, xn_low_done, common_up_in, common_down_in = (sem(n) for n in (
            "common_high_weights", "common_low_weights", "xn_high", "xn_low", "common_up_in", "common_down_in"))
        h_done, h_out_b, s_cleared = sem("h_done"), sem("h_with_b_out"), sem("dots_banks_cleared")
        ln_chain, ve_done, rl_done, hn_done, hT_mm, hT_ev = (sem(n) for n in (
            "ln_chain", "ln_var", "ln_rstd", "hn_done", "hnT_mm", "hnT_ev"))
        qk_mm, v_mm, s_mm, t_mm, av_mm = (sem(n) for n in (
            "qk_mm", "v_mm", "s_mm", "pT_mm", "av_mm"))
        qk_ev, v_ev, d_ev, t_ev, o_ev = (sem(n) for n in (
            "qk_ev", "v_ev", "dots_ev", "pT_ev", "oT_ev"))
        top8, dropped, se_sum, se_done, logit, rmax, shifted, expd, summed, invd, probs = (sem(n) for n in (
            "top8", "dropped", "se_sum", "se_done", "logits_ready", "row_max", "shifted", "exp_done",
            "row_sum", "row_inv", "probs_ready"))
        zeros_out = sem("zero_rows_written")
        om_mm, h2_done, lg_mm, le_exp, route, oh_done, rank_mm, cm_done, cT_mm, cT_ev = (
            sem(n) for n in ("out_mm", "h2_done", "router_mm", "router_exp", "route",
                             "onehot", "rank_mm", "mix_done", "mixT_mm", "mixT_ev"))
        lsub, slots_done, pf_done, texp_done, scattered = (sem(n) for n in (
            "logits_less_max", "slots_done", "earlier_tokens", "tile_expert", "scattered"))
        c1_mm, c1_ev, c2_mm, b2_mm, acc_a, acc_b = (sem(n) for n in (
            "common1_mm", "common1_ev", "common2_mm", "b2_mm", "acc_a", "acc_b"))
        xg_in = [sem(f"xg_in{i}") for i in range(2)]
        xT_mm, xT_ev, f1_mm, f1_ev, f2T_mm, f2T_ev, f2_mm, y_ev = (sem(n) for n in (
            "xT_mm", "xT_ev", "up_mm", "gelu_done", "hT_mm", "hT_ev2", "down_mm", "y_ev"))
        meta_in, rows_ready, stored, rows_out = (sem(n) for n in (
            "meta_in", "row_numbers", "common_stored", "rows_out"))
        ag_in = [sem(f"common_in{i}") for i in range(2)]
        empty_set, wb1_ready, wb2_ready, bias4_mm, bias4_ev, sq4_mm = (sem(n) for n in (
            "empty_set", "second_up_weights", "second_down_weights", "bias4_mm", "bias4_ev", "squares4_mm"))

        def wait(eng, s, n):
            if not isinstance(n, int) or n > 0:
                eng.wait_ge(s, n)

        block = ctx.enter_context(nc.Block())

        @block.sync
        def _(sp):
            first = slice(*CONST["count"])
            sp.dma_start(cst[:, first], consts[:, first]).then_inc(count_in, 16)
            for i in range(4):
                sp.dma_start(xs[0:ROWS, 2 * i:2 * i + 2], xk[:, 2 * i:2 * i + 2]).then_inc(x_in[i], 16)
            sp.dma_start(lnw_s[0:ROWS], lnw).then_inc(lnw_in, 16)
            sp.dma_start(lnb_s[0:ROWS], lnb).then_inc(lnw_in, 16)
            for f in range(SHIFTS):
                sp.dma_start(pw[0:PIX, f], pk[:, f]).then_inc(pw_in[f], 16)
                if f == 0:
                    sp.dma_start(pw[PIX:ROWS, 0], ph).then_inc(ph_in, 16)
            rest = slice(0, CONST["count"][0])
            sp.dma_start(cst[:, rest], consts[:, rest]).then_inc(cst_in, 16)
            sp.dma_start(rowv[0:1, 0:D], pb).then_inc(small_in, 16)
            sp.dma_start(bout_s[:, 0, :], bout.broadcast_to([P, D])).then_inc(small_in, 16)
            sp.dma_start(bs_s[:, 0, :], bs.broadcast_to([P, EXP])).then_inc(small_in, 16)
            sp.dma_start(scq[:, :], scale).then_inc(small_in, 16)
            sp.dma_start(ws_s[:, :, :], ws).then_inc(small_in, 16)
            sp.dma_start(b2_s[:, :], b2).then_inc(small_in, 16)
            sp.dma_start(b1_s[:, :], b1c).then_inc(small_in, 16)
            sp.dma_start(wq_s[:, :, :], wqkv).then_inc(wq_in, 16)
            sp.dma_start(wo_s[:, :, :], wout).then_inc(wo_in, 16)
            sp.wait_ge(empty_set, 2)
            for i in range(2):
                sp.dma_start(xg_dram[i * SLOTS // 2:(i + 1) * SLOTS // 2, :]
                             .rearrange("(p a) d -> p (a d)", p=P), empty.rearrange("p a d -> p (a d)"))\
                    .then_inc(zeros_out, 16)
            sp.dma_start(acc_dram[TOK:TOK + 1, :], empty[0:1, 0, 0:D]).then_inc(zeros_out, 16)
            sp.wait_ge(proj_mm, TT)
            sp.dma_start(w1a[0:DH, COMMON], w1[0:DH, 0]).then_inc(common_up_in, 16)
            sp.dma_start(w1b[0:DH, COMMON], w1[DH:D, 0]).then_inc(common_up_in, 16)
            sp.dma_start(w2s[:, COMMON], w2[:, 0]).then_inc(common_down_in, 16)
            sp.dma_start(w1b[0:DH, 0:COMMON], w1[DH:D, 1:EXP]).then_inc(w1_in, 16)
            sp.dma_start(w1b[DH:DH + 1, 0:COMMON], b1[:, 1:EXP]).then_inc(w1_in, 16)
            sp.dma_start(w2s[:, 0:COMMON], w2[:, 1:EXP]).then_inc(w2_in, 16)
            sp.wait_ge(v_mm, PAIRS)
            sp.dma_start(w1a[0:DH, 0:COMMON], w1[0:DH, 1:EXP]).then_inc(w1_in, 16)

            sp.wait_ge(scattered, 16 * TT)

            def load_tile(s):
                wait(sp, xT_mm, s - 1)
                sp.dma_start(xg[s % 2][:, 0, :], xg_dram[s * P:(s + 1) * P, 0:D]).then_inc(xg_in[s % 2], 16)
            load_tile(0)
            load_tile(1)
            sp.dma_start(meta[:, :, :], xg_dram[0:SLOTS, D:ROW].rearrange("(t p) c -> p t c", p=P))\
                .then_inc(meta_in, 16)
            for t in range(TT):
                if t >= TT - 2:
                    load_tile(t - TT + 4)
                sp.wait_ge(acc_b, t + 1)
                for to in (acc_dram, out):
                    sp.dma_start(to[t * P:t * P + rows(t), :], acc[0:rows(t), t, :]).then_inc(stored, 16)
            for s in range(4, TILES):
                load_tile(s)
            sp.wait_ge(rows_out, 16 * TILES)

        @block.tensor
        def _(pe):
            pe.wait_ge(set_up, 2)
            pe.wait_ge(xsum_done, XL)
            for half_ in range(2):
                nc.tensor.matmul(ps[0:ROWS, half_, 0:288], ones[0:ROWS, 0:ROWS],
                                 xsum[0:ROWS, 0, half_ * 288:half_ * 288 + 288], start=True, stop=True)\
                    .then_inc(mean_mm, 1)
            pe.wait_ge(lnw_in, 32)
            pe.wait_ge(ph_in, 16)
            for f in range(SHIFTS):
                pe.wait_ge(pw_in[f], 16)
                n = ROWS if f == 0 else PIX
                for s in range(XL):
                    o = 32 * (s % 4)
                    mm = nc.tensor.matmul(ps[o:o + 32, 2, 0:D],
                                          lnb_s[0:n, f * XL + s:f * XL + s + 1].broadcast_to([n, 32]),
                                          pw[0:n, f, s, :], start=(f == 0 and s < 4),
                                          stop=(f == SHIFTS - 1 and s >= 4))
            mm.then_inc(bias4_mm, 1)
            for s in range(XL):
                pe.wait_ge(sq_done, s + 1)
                o = 32 * (s % 4)
                for half_ in range(2):
                    mm = nc.tensor.matmul(ps[o:o + 32, 6 + half_, 0:288],
                                          const("count", 0, ROWS)[:, s:s + 1].broadcast_to([ROWS, 32]),
                                          sq[0:ROWS, s, half_ * 288:half_ * 288 + 288],
                                          start=(s < 4), stop=(s >= 4))
            mm.then_inc(sq4_mm, 1)
            pe.wait_ge(xc_done, 2)
            pe.wait_ge(fold, SHIFTS - 1)

            def transposes(t, ready, bank):
                pe.wait_ge(hn_done, ready)
                for k in range(2):
                    mm = nc.tensor.transpose(ps[0:DH, bank, k * P:k * P + rows(t)],
                                             hn[0:rows(t), t, k * DH:(k + 1) * DH],
                                             const("ident", 0, rows(t))[:, 0:rows(t)])
                mm.then_inc(hT_mm, 1)
            for t in range(TT):
                if t == 4:
                    pe.wait_ge(h_done, 1)
                for s in range(XL):
                    if s == POOL_SLOTS:
                        pe.wait_ge(fold_pool, 2 * (SHIFTS - 1))
                    if s == XL - 3 and t >= 2:
                        if t == 2:
                            pe.wait_ge(bias_ev, 1)
                        if t == 4:
                            pe.wait_ge(hT_low, 1)
                        transposes(t - 2, t - 1, HN_BANK[t - 2])
                    mm = nc.tensor.matmul(ps[0:rows(t), PROJ_BANK[t], 0:D],
                                          xc[0:ROWS, s, t * P:t * P + rows(t)], weff[0:ROWS, s, :],
                                          start=(s == 0), stop=(s == XL - 1))
                mm.then_inc(proj_mm, 1)
                if t == 0:
                    pe.wait_ge(small_in, 16 * 7)
                    pe.wait_ge(bias4_ev, 1)
                    nc.tensor.matmul(ps[:, 0, 0:D], ones[0:1, :], rowv[0:1, 0:D], start=True, stop=False)
                    nc.tensor.matmul(ps[:, 0, 0:D], thirty2[:, :], bias4[:, :], start=False, stop=True)\
                        .then_inc(bias_mm, 1)
                    pe.wait_ge(sqsum_done, 1)
                    for u in range(TT):
                        mm = nc.tensor.matmul(ps[0:rows(u), 3, u:u + 1], sqsum[:, 0, u * P:u * P + rows(u)],
                                              thirty2[:, 0:1], start=True, stop=True)
                    mm.then_inc(var_mm, 1)

            pe.wait_ge(low_w, 1)
            split_terms = [(w, x, k) for w, x in ((wq_high, hnT_high), (wq_high, hnT_low), (wq_low, hnT_high))
                           for k in range(2)]

            def qk(half_, m):
                for which in range(2):
                    n = (half_ * HP + m) * 2 + which
                    wait(pe, qk_ev, n - 3)
                    for i, (w, x, k) in enumerate(split_terms):
                        mm = nc.tensor.matmul(ps[:, (2, 3, 0, 1)[n % 4], 0:288],
                                              w[:, k, which * INNER + m * P:which * INNER + (m + 1) * P],
                                              x[:, k, half_ * 288:half_ * 288 + 288],
                                              start=(i == 0), stop=(i == len(split_terms) - 1))
                    mm.then_inc(qk_mm, 1)

            def probs_T(s):
                if s < PAIRS - 1:
                    pe.wait_ge(probs, 2 * s + 2)
                else:
                    pe.wait_ge(last_probs, 2)
                for c, bank in enumerate((0, 1, 7)):
                    for g in range(4):
                        mm = nc.tensor.transpose(ps[0:PT, bank, g * P:(g + 1) * P],
                                                 pblk[s % 2][:, 4 * c + g, :], const("ident"))
                    mm.then_inc(t_mm, 1)

            def av(s):
                pe.wait_ge(v_ev, s + 1)
                wait(pe, o_ev, s)
                pe.wait_ge(t_ev, 3 * s + 3)
                for m in range(HP):
                    for odd in range(2):
                        mm = nc.tensor.matmul(ps[64 * odd:64 * odd + 64, 6, m * PT:(m + 1) * PT],
                                              vv[s % 2][0:PT, 2 * m + odd, :], pT[0:PT, odd * HP + m, :, :],
                                              start=True, stop=True)
                mm.then_inc(av_mm, 1)

            def values(s):
                wait(pe, v_ev, s)
                for c in range(2):
                    for i, (w, x, k) in enumerate(split_terms):
                        mm = nc.tensor.matmul(ps[0:PT, 2 + c, 0:384], x[:, k, s * PT:(s + 1) * PT],
                                              w[:, k, 2 * INNER + c * 384:2 * INNER + (c + 1) * 384],
                                              start=(i == 0), stop=(i == len(split_terms) - 1))
                mm.then_inc(v_mm, 1)

            def dots(s):
                if s == 0:
                    pe.wait_ge(s_cleared, 1)
                wait(pe, d_ev, s)
                for m in range(HP):
                    for b in range(2):
                        c0 = s * PT + b * N
                        for odd in range(2):
                            o = 64 * odd
                            mm = nc.tensor.matmul(ps[64 * b:64 * b + N, 4 + odd, m * N:(m + 1) * N],
                                                  qT[o:o + 64, m, c0:c0 + N], kT[o:o + 64, m, c0:c0 + N],
                                                  start=True, stop=True)
                mm.then_inc(s_mm, 1)

            pe.wait_ge(hT_low, 3)
            for m in range(HP):
                qk(0, m)
                if m < 2:
                    transposes(3 + m, 4 + m, HN_BANK[3 + m])
            pe.wait_ge(hT_low, 5)
            for m in range(HP):
                qk(1, m)
                if m in (0, 3):
                    pe.wait_ge(qk_ev, 2 * HP)
                    dots(m // 3)
            pe.wait_ge(qk_ev, 4 * HP - 2)
            pe.wait_ge(low_w, 2)
            values(0)
            pe.wait_ge(qk_ev, 4 * HP)
            dots(2)
            values(1)
            for s in range(3, PAIRS):
                dots(s)
                probs_T(s - 3)
                values(s - 1)
                av(s - 3)

            pe.wait_ge(wo_in, 16)

            def out_proj(t):
                pe.wait_ge(o_ev, min(PAIRS, (t * P + rows(t) + PT - 1) // PT))
                wait(pe, h2_done, t - 1)
                bank = 4 + t % 2
                for m in range(HP):
                    mm = nc.tensor.matmul(ps[0:rows(t), bank, 0:D], oT[:, m, t * P:t * P + rows(t)],
                                          wo_s[:, m, :], start=(m == 0), stop=(m == HP - 1))
                mm.then_inc(om_mm, 1)

            def router(t):
                pe.wait_ge(hT_ev, TT + t + 1)
                for k in range(2):
                    mm = nc.tensor.matmul(ps[0:rows(t), 7, t * EXP:(t + 1) * EXP],
                                          xnT[:, k, t * P:t * P + rows(t)], ws_s[:, k, :],
                                          start=(k == 0), stop=(k == 1))
                mm.then_inc(lg_mm, 1)
            pe.wait_ge(d_ev, PAIRS)
            out_proj(0)
            probs_T(PAIRS - 3)
            values(PAIRS - 1)
            av(PAIRS - 3)
            out_proj(1)
            probs_T(PAIRS - 2)
            out_proj(2)
            av(PAIRS - 2)
            probs_T(PAIRS - 1)
            pe.wait_ge(v_ev, PAIRS)
            transposes(0, TT + 1, XN_BANK[0])
            av(PAIRS - 1)
            transposes(1, TT + 2, XN_BANK[1])
            out_proj(3)
            out_proj(4)

            def common_up(m, half_):
                terms = [(w, x, k) for w, x in ((common_high, xn_high), (common_low, xn_high),
                                                (common_high, xn_low)) for k in range(2)]
                for i, (w, x, k) in enumerate(terms):
                    if i == 4:
                        pe.wait_ge(xn_low_done, (3, TT)[half_])
                    mm = nc.tensor.matmul(ps[:, m % 3 * 2 + half_, 0:288], w[:, k, m * P:(m + 1) * P],
                                          x[:, k, half_ * 288:half_ * 288 + 288],
                                          start=(i == 0), stop=(i == len(terms) - 1))
                mm.then_inc(c1_mm, 1)

            pe.wait_ge(hT_ev, TT + 1)
            transposes(2, TT + 3, XN_BANK[2])
            for t in range(3):
                router(t)
            pe.wait_ge(common_low_w, 2)
            pe.wait_ge(xn_high_ev, 3)
            common_up(0, 0)
            pe.wait_ge(hT_ev, TT + 2)
            transposes(3, TT + 4, XN_BANK[3])
            pe.wait_ge(hT_ev, TT + 3)
            common_up(1, 0)
            transposes(4, TT + 5, XN_BANK[4])
            router(3)
            router(4)

            pe.wait_ge(xn_high_ev, TT)
            for m in range(FM):
                if m == 1:
                    pe.wait_ge(hT_ev, TT + 4)
                if m == 2:
                    pe.wait_ge(h2_done, TT)
                if m >= 3:
                    pe.wait_ge(c1_ev, m - 2)
                if m >= 2:
                    common_up(m, 0)
                common_up(m, 1)
                if m == 2:
                    pe.wait_ge(pf_done, TT)
                    for to, table, rhs, first, last in (
                            (ps[:, 6, 0:TT * 8], const("upper"), oh[:, :, 1:EXP], True, False),
                            (ps[:, 6, 0:TT * 8], ones[:, :], pf[:, 0:TT, :], False, True),
                            (ps[:, 6, TT * 8:TT * 8 + 8], ones[:, :], pf[:, TT, :], True, True)):
                        mm = nc.tensor.matmul(to, table, rhs, start=first, stop=last)
                    mm.then_inc(rank_mm, 1)
            pe.wait_ge(cm_done, 2)
            pe.wait_ge(slots_done, 3)
            for t in range(TT):
                mm = nc.tensor.transpose(ps[0:EXP, (7 if t < 4 else 6), t % 4 * P:t % 4 * P + P],
                                         cmix[:, t, :], const("ident"))
            mm.then_inc(cT_mm, 1)
            def tile_T(s):
                par = s % 2
                pe.wait_ge(xg_in[par], 16 * (s // 2 + 1))
                wait(pe, xT_ev, s - 1)
                for k in range(2):
                    mm = nc.tensor.transpose(ps[0:DH, (4, 7)[par], k * P:(k + 1) * P],
                                             xg[par][:, 0, k * DH:(k + 1) * DH], const("ident"))
                mm.then_inc(xT_mm, 1)

            def up(s):
                par = s % 2
                e = pe.value_load(texi[0:1, 2 * s:2 * s + 1], min_val=0, max_val=EXP - 2)
                pe.wait_ge(xT_ev, s + 1)
                pe.wait_ge(wb1_ready, s + 1)
                wait(pe, f1_ev, s)
                for c in range(2):
                    cols = slice(c * 384, (c + 1) * 384)
                    for k, (n, w) in enumerate(((DH, w1a), (DH + 1, w1b))):
                        nc.tensor.matmul(ps[0:GS, c, 0:384], xT[par][0:n, k, 0:GS],
                                         w[0:n, bass.ds(e, 1), cols], start=(k == 0), stop=(k == 1))
                        mm = nc.tensor.matmul(ps[GS:P, c, 0:384], xT[par][0:n, k, GS:P],
                                              wb1[par][0:n, k, cols], start=(k == 0), stop=(k == 1))
                mm.then_inc(f1_mm, 1)

            def hidden_T(s):
                pe.wait_ge(f1_ev, s + 1)
                b = hidden_bank(s)
                if b == 2:
                    wait(pe, f2T_ev, s)
                for m in range(FM):
                    mm = nc.tensor.transpose(ps[:, b + m // 3, m % 3 * P:(m % 3 + 1) * P], hs[s % 2][:, m, :],
                                             const("ident"))
                mm.then_inc(f2T_mm, 1)

            def down(s):
                par = s % 2
                e = pe.value_load(texi[0:1, 2 * s:2 * s + 1], min_val=0, max_val=EXP - 2)
                pe.wait_ge(f2T_ev, s + 1)
                pe.wait_ge(wb2_ready, s + 1)
                wait(pe, y_ev, s - 1)
                for m in range(FM):
                    nc.tensor.matmul(ps[0:GS, 5 + par, 0:D], hT[par][:, m, 0:GS], w2s[:, bass.ds(e, 1), m, :],
                                     start=(m == 0), stop=(m == FM - 1))
                    mm = nc.tensor.matmul(ps[GS:P, 5 + par, 0:D], hT[par][:, m, GS:P], wb2[par][:, m, :],
                                          start=(m == 0), stop=(m == FM - 1))
                mm.then_inc(f2_mm, 1)
            pe.wait_ge(common_down_in, 16)
            pe.wait_ge(c1_ev, FM)
            for t in range(TT):
                if t == TT - 2:
                    tile_T(0)
                if t == TT - 1:
                    tile_T(1)
                    pe.wait_ge(texp_done, 1)
                    pe.wait_ge(w1_in, 48)
                    up(0)
                if t >= 2:
                    pe.wait_ge(acc_a, t - 1)
                    pe.wait_ge(acc_b, t - 1)
                for m in range(FM):
                    mm = nc.tensor.matmul(ps[0:rows(t), 2 + t % 2, 0:D], hcT[:, m, t * P:t * P + rows(t)],
                                          w2s[:, COMMON, m, :], start=(m == 0), stop=(m == FM - 1))
                mm.then_inc(c2_mm, 1)
                if t == 0:
                    pe.wait_ge(cT_ev, 2)
                nc.tensor.matmul(ps[0:rows(t), 5 + t % 2, 0:D], cT[0:EXP, t, 0:rows(t)], b2_s[:, :],
                                 start=True, stop=True).then_inc(b2_mm, 1)
            pe.wait_ge(w2_in, 16)
            for s in range(TILES):
                if s + 1 < TILES:
                    up(s + 1)
                if s + 2 < TILES:
                    tile_T(s + 2)
                if 1 <= s < TILES - 1:
                    down(s - 1)
                if s == 0:
                    pe.wait_ge(acc_b, TT)
                hidden_T(s)
            down(TILES - 2)
            down(TILES - 1)

        @block.vector
        def _(dve):
            nc.vector.memset(ones[:, :], 1.0).then_inc(set_up, 1)
            nc.vector.memset(half[:, :], -0.5).then_inc(set_up, 1)
            nc.vector.memset(thirty2[:, :], 1 / 32)
            nc.vector.memset(var[64:P, TT - 1, :], 1.0)
            nc.vector.memset(pf[:, 0, :], 0.0)
            nc.vector.memset(lg[:, :, :], 0.0).then_inc(pads, 1)
            cnt = const("count", 0, ROWS)
            dve.wait_ge(count_in, 16)
            for s in range(XL):
                if s % 2 == 0:
                    dve.wait_ge(x_in[s // 2], 16)
                if s == 0:
                    nc.vector.tensor_scalar(xsum[0:ROWS, 0, :], xs[0:ROWS, 0, :], cnt[:, 0:1], None, ALU.mult)\
                        .then_inc(xsum_done, 1)
                else:
                    dve.wait_ge(xsum_done, s)
                    nc.vector.scalar_tensor_tensor(out=xsum[0:ROWS, 0, :], in0=xs[0:ROWS, s, :],
                                                   scalar=cnt[:, s:s + 1], in1=xsum[0:ROWS, 0, :],
                                                   op0=ALU.mult, op1=ALU.add).then_inc(xsum_done, 1)
            for half_ in range(2):
                dve.wait_ge(mean_mm, half_ + 1)
                c0 = half_ * 288
                nc.vector.scalar_tensor_tensor(
                    out=xc[0:ROWS, :, c0:c0 + 288],
                    in0=ps[0:ROWS, half_:half_ + 1, 0:288].broadcast_to([ROWS, XL, 288]),
                    scalar=-1.0 / PATCH_DIM, in1=xs[0:ROWS, :, c0:c0 + 288], op0=ALU.mult, op1=ALU.add)\
                    .then_inc(xc_done, 1)
            dve.wait_ge(first_w, XL)
            for f in range(1, SHIFTS):
                dve.wait_ge(pw_in[f], 16)
                if f > 1:
                    dve.wait_ge(fold, f - 1)
                for s in range(POOL_SLOTS):
                    c = f * XL + s
                    ins = nc.vector.scalar_tensor_tensor(
                        out=weff[0:PIX, s, :], in0=pw[0:PIX, f, s, :], scalar=lnw_s[0:PIX, c:c + 1],
                        in1=weff[0:PIX, s, :], op0=ALU.mult, op1=ALU.add)
                ins.then_inc(fold, 1)
            dve.wait_ge(small_in, 16 * 7)
            nc.vector.tensor_scalar(nscq[:, :], scq[:, :], -1.0, None, ALU.mult).then_inc(neg_scale, 1)
            def low_weights(n0, n1):
                nc.vector.tensor_tensor(out=wq_low[:, :, n0:n1], in0=wq_s[:, :, n0:n1],
                                        in1=wq_high[:, :, n0:n1].bitcast(fp32), op=ALU.subtract)\
                    .then_inc(low_w, 1)
            dve.wait_ge(high_w, 1)
            low_weights(0, 2 * INNER)
            dve.wait_ge(bias_mm, 1)
            nc.vector.tensor_copy(bias[:, :], ps[:, 0, 0:D]).then_inc(bias_ev, 1)
            dve.wait_ge(var_mm, 1)
            nc.vector.tensor_scalar(var[:, 0:4, 0], ps[:, 3, 0:4], 1.0 / PATCH_DIM, EPS, ALU.mult, ALU.add)
            nc.vector.tensor_scalar(var[0:64, 4:5, 0], ps[0:64, 3, 4:5], 1.0 / PATCH_DIM, EPS,
                                    ALU.mult, ALU.add).then_inc(var_ev, 1)
            dve.wait_ge(rs_done, 1)
            chain = 0

            def norm(t, which, chain):
                n = rows(t)
                nc.vector.bn_stats(st[0:n, t, :], h[0:n, t, :]).then_inc(ln_chain, 1)
                dve.wait_ge(ln_chain, chain + 1)
                nc.vector.bn_aggr(mv[0:n, t, :], st[0:n, t, :]).then_inc(ln_chain, 1)
                dve.wait_ge(ln_chain, chain + 2)
                nc.vector.tensor_scalar(ve[0:n, t, :], mv[0:n, t, 1:2], EPS, None, ALU.add)\
                    .then_inc(ve_done, 1)
                return chain + 2

            def normed(t, which):
                n = rows(t)
                dve.wait_ge(rl_done, which * TT + t + 1)
                nc.vector.tensor_scalar(hn[0:n, t, 0:D], h[0:n, t, :], mv[0:n, t, 0:1], rl[0:n, t, :],
                                        ALU.subtract, ALU.mult).then_inc(hn_done, 1)

            def hnT_low_out(t):
                n = rows(t)
                dve.wait_ge(hT_ev, t + 1)
                nc.vector.tensor_tensor(
                    out=hnT_low[:, :, t * P:t * P + n],
                    in0=ps[0:DH, HN_BANK[t], 0:2 * P].rearrange("p (k n) -> p k n", k=2)[:, :, 0:n],
                    in1=hnT_high[:, :, t * P:t * P + n].bitcast(fp32), op=ALU.subtract).then_inc(hT_low, 1)
            dve.wait_ge(bias_ev, 1)
            for t in range(TT):
                if t == 3:
                    hnT_low_out(0)
                if t == 4:
                    hnT_low_out(1)
                    hnT_low_out(2)
                n = rows(t)
                dve.wait_ge(proj_mm, t + 1)
                nc.vector.scalar_tensor_tensor(out=h[0:n, t, :], in0=ps[0:n, PROJ_BANK[t], 0:D],
                                               scalar=rs[0:n, t, :], in1=bias[0:n, :], op0=ALU.mult,
                                               op1=ALU.add).then_inc(h_done, 1)
                dve.wait_ge(h_done, t + 1)
                chain = norm(t, 0, chain)
                if t >= 1:
                    normed(t - 1, 0)
            normed(TT - 1, 0)
            for t in range(3, TT):
                hnT_low_out(t)
            dve.wait_ge(high_w, 2)
            low_weights(2 * INNER, 3 * INNER)
            dve.wait_ge(small_in, 16 * 7)
            dve.wait_ge(hn_done, TT)
            nc.vector.tensor_tensor(out=h[:, 0:4, :], in0=h[:, 0:4, :], in1=bout_s.broadcast_to([P, 4, D]),
                                    op=ALU.add).then_inc(h_out_b, 1)
            nc.vector.tensor_tensor(out=h[0:64, 4:5, :], in0=h[0:64, 4:5, :], in1=bout_s[0:64],
                                    op=ALU.add).then_inc(h_out_b, 1)

            dve.wait_ge(hT_low, 4)
            nc.vector.memset(ps[:, 4:6, 0:HP * N], 0.0).then_inc(s_cleared, 1)

            def negated_dots(s):
                dve.wait_ge(s_mm, s + 1)
                wait(dve, dropped, s)
                nc.vector.tensor_tensor(
                    out=dd.rearrange("p (o m) n -> p o m n", o=2)[:, :, :, ::-1],
                    in0=ps[:, 4:6, 0:HP * N].rearrange("p o (m n) -> p o m n", m=HP),
                    in1=const("diag").unsqueeze(1).unsqueeze(1).broadcast_to([P, 2, HP, N]), op=ALU.add)\
                    .then_inc(d_ev, 1)

            def select(s):
                dve.wait_ge(d_ev, s + 1)
                nc.vector.tensor_reduce(sraw[:, 0, :], dd.rearrange("p h n -> p n h"), axis=AX.X,
                                        op=ALU.add).then_inc(se_sum, 1)
                for g in range(HEADS):
                    ins = nc.vector.max(out=mx[:, g, :], in_=dd[:, g, :])
                ins.then_inc(top8, 1)

            def drop(s, par):
                dve.wait_ge(se_sum, s + 1)
                dve.wait_ge(top8, s + 1)
                nc.vector.scalar_tensor_tensor(out=se[:, 0, :], in0=sraw[:, 0, :], scalar=-1.0 / HEADS,
                                               in1=const("diag_out"), op0=ALU.mult, op1=ALU.add)\
                    .then_inc(se_done, 1)
                for g in range(HEADS):
                    ins = nc.vector.match_replace(out=rr[par][:, g, :], in_to_replace=mx[:, g, :],
                                                  in_values=dd[:, g, :], imm_value=BIG)
                ins.then_inc(dropped, 1)

            def row_max(s, par):
                dve.wait_ge(logit, s + 1)
                nc.vector.tensor_reduce(rowm[:, :, 0:1], rr[par], axis=AX.X, op=ALU.max).then_inc(rmax, 1)

            def row_sums(s, par):
                dve.wait_ge(expd, s + 1)
                nc.vector.tensor_reduce(sums[:, :, 0:1], ee[par], axis=AX.X, op=ALU.add).then_inc(summed, 1)
                dve.wait_ge(summed, s + 1)
                wait(dve, probs, 2 * s)
                nc.vector.reciprocal(inv, sums).then_inc(invd, 1)

            def pair(s, par):
                negated_dots(s)
                row_sums(s - 2, par)
                select(s)
                row_max(s - 1, 1 - par)
                drop(s, par)
            negated_dots(0)
            select(0)
            drop(0, 0)
            negated_dots(1)
            select(1)
            row_max(0, 0)
            drop(1, 1)
            pair(2, 0)
            pair(3, 1)
            with dve.Fori(2, PAIRS // 2) as i:
                for par in range(2):
                    pair(2 * i + par, par)
            def residual(t):
                n = rows(t)
                dve.wait_ge(om_mm, t + 1)
                nc.vector.tensor_tensor(out=h[0:n, t, :], in0=ps[0:n, 4 + t % 2, 0:D], in1=h[0:n, t, :],
                                        op=ALU.add).then_inc(h2_done, 1)
            dve.wait_ge(h_out_b, 2)
            dve.wait_ge(dropped, PAIRS)
            dve.wait_ge(se_done, PAIRS)
            nc.vector.tensor_tensor(out=rr[1], in0=se.broadcast_to([P, HEADS, N]), in1=rr[1],
                                    op=ALU.subtract).then_inc(logit, 1)
            row_sums(PAIRS - 2, 0)
            row_max(PAIRS - 1, 1)
            dve.wait_ge(rmax, PAIRS)
            nc.vector.tensor_tensor(out=rr[1], in0=rr[1], in1=rowm.broadcast_to([P, HEADS, N]),
                                    op=ALU.subtract).then_inc(shifted, 1)
            residual(0)
            row_sums(PAIRS - 1, 1)
            dve.wait_ge(invd, PAIRS)
            dve.wait_ge(t_mm, 3 * PAIRS - 6)
            for b in range(2):
                r = slice(64 * b, 64 * b + 64)
                nc.vector.tensor_tensor(out=pblk[1][r, :, b * N:(b + 1) * N], in0=ee[1][r, :, ::-1],
                                        in1=inv[r].broadcast_to([64, HEADS, N]), op=ALU.mult)\
                    .then_inc(last_probs, 1)

            residual(1)
            def common_low_out(k):
                dve.wait_ge(common_high_w, k + 1)
                nc.vector.tensor_tensor(out=common_low[:, k, :], in0=(w1a, w1b)[k][0:DH, COMMON, :],
                                        in1=common_high[:, k, :].bitcast(fp32), op=ALU.subtract)\
                    .then_inc(common_low_w, 1)

            def xn_low_out(t):
                tile = slice(t * P, t * P + rows(t))
                dve.wait_ge(xn_high_ev, t + 1)
                nc.vector.tensor_tensor(out=xn_low[:, :, tile], in0=xnT[:, :, tile],
                                        in1=xn_high[:, :, tile].bitcast(fp32), op=ALU.subtract)\
                    .then_inc(xn_low_done, 1)
            for t in range(TT):
                n = rows(t)
                if t == 3:
                    common_low_out(0)
                    common_low_out(1)
                    xn_low_out(0)
                    xn_low_out(1)
                if t >= 2:
                    residual(t)
                dve.wait_ge(h2_done, t + 1)
                chain = norm(t, 1, chain)
                if t >= 1:
                    normed(t - 1, 1)
            xn_low_out(2)
            normed(TT - 1, 1)
            for t in range(3, TT):
                xn_low_out(t)
            for i in range(2):
                ins = nc.vector.memset(xT[i][DH:DH + 1, 1, :], 1.0)
            ins.then_inc(set_up, 1)

            n_route = 0

            def link(ins):
                nonlocal n_route
                n_route += 1
                ins.then_inc(route, 1)
                dve.wait_ge(route, n_route)
            dve.wait_ge(lg_mm, TT)
            nc.vector.tensor_tensor(out=lg[:, 0:4, :], in0=ps[:, 7, 0:4 * EXP].rearrange("p (t e) -> p t e", e=EXP),
                                    in1=bs_s.broadcast_to([P, 4, EXP]), op=ALU.add)
            link(nc.vector.tensor_tensor(out=lg[0:64, 4:5, :],
                                         in0=ps[0:64, 7, 4 * EXP:5 * EXP].rearrange("p (t e) -> p t e", e=EXP),
                                         in1=bs_s[0:64], op=ALU.add))
            link(nc.vector.tensor_reduce(lm[:, :, :], lg[:, :, :], axis=AX.X, op=ALU.max))
            nc.vector.tensor_tensor(out=le[:, :, :], in0=lg[:, :, :], in1=lm[:, :, :].broadcast_to([P, TT, EXP]),
                                    op=ALU.subtract).then_inc(lsub, 1)
            for t in range(TT):
                ins = nc.vector.max(out=mx8[:, t, :], in_=lg[:, t, :])
            link(ins)
            for t in range(TT):
                ins = nc.vector.max_index(out=ix8[:, t, :], in_max=mx8[:, t, :], in_values=lg[:, t, :])
            link(ins)
            link(nc.vector.tensor_copy(ixf[:, :, :], ix8[:, :, 0:1]))
            nc.vector.tensor_tensor(out=oh[:, :, :], in0=ixf[:, :, :].broadcast_to([P, TT, EXP]),
                                    in1=const("iota").unsqueeze(1).broadcast_to([P, TT, EXP]),
                                    op=ALU.is_equal).then_inc(oh_done, 1)
            dve.wait_ge(oh_done, 1)
            nc.vector.tensor_copy(pf[:, 1, :], oh[:, 0, 1:EXP]).then_inc(pf_done, 1)
            for t in range(1, TT):
                dve.wait_ge(pf_done, t)
                nc.vector.tensor_tensor(out=pf[:, t + 1, :], in0=pf[:, t, :], in1=oh[:, t, 1:EXP], op=ALU.add)\
                    .then_inc(pf_done, 1)
            nc.vector.tensor_scalar(routed[:, :, :], oh[:, :, 0:1], -1.0, 1.0, ALU.mult, ALU.add)
            dve.wait_ge(le_exp, 1)
            link(nc.vector.tensor_reduce(ls[:, :, :], le[:, :, :], axis=AX.X, op=ALU.add))
            link(nc.vector.reciprocal(pr[:, :, :], ls[:, :, :]))
            link(nc.vector.tensor_tensor(out=pe_w[:, :, :], in0=pr[:, :, :], in1=routed[:, :, :], op=ALU.mult))
            link(nc.vector.tensor_scalar(ome[:, :, :], pe_w[:, :, :], -1.0, 1.0, ALU.mult, ALU.add))
            nc.vector.tensor_tensor(out=cmix[:, :, 1:EXP], in0=oh[:, :, 1:EXP],
                                    in1=pe_w[:, :, :].broadcast_to([P, TT, EXP - 1]), op=ALU.mult)\
                .then_inc(cm_done, 1)
            nc.vector.tensor_copy(cmix[:, :, 0:1], ome[:, :, :]).then_inc(cm_done, 1)

            dve.wait_ge(rank_mm, 1)
            link(nc.vector.tensor_copy(nsum[:, :, 0], ps[:, 6, TT * 8:TT * 8 + 8]))
            link(nc.vector.tensor_tensor(out=over[:, :, :], in0=nsum[:, :, :].broadcast_to([P, 8, STEPS]),
                                         in1=const("steps").rearrange("p (e k) -> p e k", e=8),
                                         op=ALU.is_gt))
            link(nc.vector.tensor_reduce(ntile[:, :, :], over[:, :, :], axis=AX.X, op=ALU.add))
            link(nc.vector.tensor_tensor(out=prod[:, :, :],
                                         in0=ntile[:, :, :].rearrange("p e o -> p o e").broadcast_to([P, 8, 8]),
                                         in1=const("tri").rearrange("p (e k) -> p e k", e=8), op=ALU.mult))
            link(nc.vector.tensor_reduce(cum[:, :, :], prod[:, :, :], axis=AX.X, op=ALU.add))
            link(nc.vector.tensor_tensor(out=base[:, 0, :], in0=cum[:, :, 0], in1=ntile[:, :, 0],
                                         op=ALU.subtract))
            link(nc.vector.tensor_scalar(base[:, 0, :], base[:, 0, :], float(GS), None, ALU.mult))
            link(nc.vector.tensor_tensor(out=rb[:, :, :],
                                         in0=ps[:, 6, 0:TT * 8].rearrange("p (t e) -> p t e", e=8),
                                         in1=base[:, :, :].broadcast_to([P, TT, 8]), op=ALU.add))
            link(nc.vector.tensor_tensor(out=rb2[:, :, :], in0=rb[:, :, :], in1=oh[:, :, 1:EXP], op=ALU.mult))
            nc.vector.tensor_tensor(out=spare[:, :, 0], in0=oh[:, :, 0], in1=const("spare"), op=ALU.mult)
            link(nc.vector.tensor_reduce(slot[:, :, :], rb2[:, :, :], axis=AX.X, op=ALU.add))
            link(nc.vector.tensor_tensor(out=slot_s[:, :, :], in0=slot[:, :, :], in1=spare[:, :, :], op=ALU.add))
            nc.vector.tensor_copy(hn[:, :, D], pr[:, :, 0]).then_inc(slots_done, 1)
            nc.vector.tensor_copy(hn[:, :, D + 1], const("token")).then_inc(slots_done, 1)
            nc.vector.tensor_copy(idx_s[:, :], slot_s[:, :, 0]).then_inc(slots_done, 1)
            link(nc.vector.tensor_tensor(
                out=tge[:, :, :], in0=const("group", 0, 1).unsqueeze(2).broadcast_to([1, 2 * TILES, 8]),
                in1=cum[0:1, :, :].rearrange("p e o -> p o e").broadcast_to([1, 2 * TILES, 8]), op=ALU.is_ge))
            link(nc.vector.tensor_reduce(tex[:, :, :], tge[:, :, :], axis=AX.X, op=ALU.add))
            link(nc.vector.tensor_scalar(tex2[:, :, :], tex[:, :, :], float(EXP - 2), None, ALU.min))
            nc.vector.tensor_copy(texi[:, :], tex2[:, :, 0]).then_inc(texp_done, 1)
            def second_up(s):
                e = dve.value_load(texi[0:1, 2 * s + 1:2 * s + 2], min_val=0, max_val=EXP - 2)
                wait(dve, f1_mm, s - 1)
                for k, (n, w) in enumerate(((DH, w1a), (DH + 1, w1b))):
                    ins = nc.vector.tensor_copy(wb1[s % 2][0:n, k, :], w[0:n, bass.ds(e, 1), :])
                ins.then_inc(wb1_ready, 1)

            def second_down(s):
                e = dve.value_load(texi[0:1, 2 * s + 1:2 * s + 2], min_val=0, max_val=EXP - 2)
                wait(dve, f2_mm, s - 1)
                nc.vector.tensor_copy(wb2[s % 2], w2s[:, bass.ds(e, 1), :, :]).then_inc(wb2_ready, 1)

            def xT_out(s):
                dve.wait_ge(xT_mm, s + 1)
                wait(dve, f1_mm, s - 1)
                nc.vector.tensor_copy(xT[s % 2][0:DH], ps[0:DH, (4, 7)[s % 2], 0:2 * P]
                                      .rearrange("p (k n) -> p k n", k=2)).then_inc(xT_ev, 1)

            def hT_out(s):
                dve.wait_ge(f2T_mm, s + 1)
                wait(dve, f2_mm, s - 1)
                b = hidden_bank(s)
                nc.vector.tensor_copy(hT[s % 2].rearrange("p (c m) n -> p c (m n)", c=2),
                                      ps[:, b:b + 2, 0:384]).then_inc(f2T_ev, 1)

            def y_out(s):
                par = s % 2
                dve.wait_ge(f2_mm, s + 1)
                dve.wait_ge(ag_in[par], 16 * (s // 2 + 1))
                wait(dve, rows_out, 16 * (s - 1))
                nc.vector.scalar_tensor_tensor(out=ys[par][:, 0, :], in0=ps[:, 5 + par, 0:D],
                                               scalar=meta[:, s, 0:1], in1=ag[par][:, 0, :], op0=ALU.mult,
                                               op1=ALU.add).then_inc(y_ev, 1)
            dve.wait_ge(texp_done, 1)
            dve.wait_ge(w1_in, 48)
            dve.wait_ge(w2_in, 16)
            second_up(0)
            second_down(0)
            dve.wait_ge(cT_mm, 1)
            nc.vector.tensor_copy(cT[0:EXP, 0:4, :], ps[0:EXP, 7, :].rearrange("p (t n) -> p t n", t=4))\
                .then_inc(cT_ev, 1)
            nc.vector.tensor_copy(cT[0:EXP, 4, :], ps[0:EXP, 6, 0:P]).then_inc(cT_ev, 1)
            second_up(1)
            second_down(1)
            for t in range(TT):
                if t >= TT - 2:
                    xT_out(t - TT + 2)
                n = rows(t)
                dve.wait_ge(c2_mm, t + 1)
                nc.vector.scalar_tensor_tensor(out=acc[0:n, t, :], in0=ps[0:n, 2 + t % 2, 0:D], scalar=ome[0:n, t, :],
                                               in1=h[0:n, t, :], op0=ALU.mult, op1=ALU.add).then_inc(acc_a, 1)
                dve.wait_ge(b2_mm, t + 1)
                dve.wait_ge(acc_a, t + 1)
                nc.vector.tensor_tensor(out=acc[0:n, t, :], in0=ps[0:n, 5 + t % 2, 0:D], in1=acc[0:n, t, :],
                                        op=ALU.add).then_inc(acc_b, 1)
            dve.wait_ge(meta_in, 16)
            nc.vector.tensor_copy(row_i[:, :], meta[:, :, 1]).then_inc(rows_ready, 1)
            for s in range(TILES):
                if s + 2 < TILES:
                    second_up(s + 2)
                    xT_out(s + 2)
                if 1 <= s < TILES - 1:
                    y_out(s - 1)
                hT_out(s)
                if 1 <= s < TILES - 1:
                    second_down(s + 1)
            y_out(TILES - 2)
            y_out(TILES - 1)

        @block.scalar
        def _(act):
            act.wait_ge(lnw_in, 32)
            act.wait_ge(pw_in[0], 16)
            act.wait_ge(ph_in, 16)
            for s in range(XL):
                nc.scalar.activation(weff[0:ROWS, s, :], pw[0:ROWS, 0, s, :], ACT.Copy,
                                           scale=lnw_s[0:ROWS, s:s + 1]).then_inc(first_w, 1)
            act.wait_ge(xc_done, 2)
            for s in range(XL):
                nc.scalar.activation(sq[0:ROWS, s, :], xc[0:ROWS, s, :], ACT.Square).then_inc(sq_done, 1)
            act.wait_ge(bias4_mm, 1)
            nc.scalar.activation(bias4[:, :], ps[:, 2, 0:D], ACT.Copy).then_inc(bias4_ev, 1)
            act.wait_ge(sq4_mm, 1)
            nc.scalar.activation(sqsum.rearrange("p o (a n) -> p (o a) n", a=2), ps[:, 6:8, 0:288], ACT.Copy)\
                .then_inc(sqsum_done, 1)

            act.wait_ge(wq_in, 16)
            for n0, n1 in ((0, 2 * INNER), (2 * INNER, 3 * INNER)):
                nc.scalar.activation(wq_high[:, :, n0:n1], wq_s[:, :, n0:n1], ACT.Copy).then_inc(high_w, 1)

            def hT_out(i, t, bank, to):
                act.wait_ge(hT_mm, i + 1)
                n = rows(t)
                nc.scalar.activation(to[:, :, t * P:t * P + n],
                                     ps[0:DH, bank, 0:2 * P].rearrange("p (k n) -> p k n", k=2)[:, :, 0:n],
                                     ACT.Copy).then_inc(hT_ev, 1)
            for t in range(3):
                hT_out(t, t, HN_BANK[t], hnT_high)

            act.wait_ge(neg_scale, 1)
            for half_ in range(2):
                for m in range(HP):
                    if half_ == 0 and m in (1, 2):
                        hT_out(2 + m, 2 + m, HN_BANK[2 + m], hnT_high)
                    for which in range(2):
                        n = (half_ * HP + m) * 2 + which
                        act.wait_ge(qk_mm, n + 1)
                        nc.scalar.activation((qT, kT)[which][:, m, half_ * 288:half_ * 288 + 288],
                                             ps[:, (2, 3, 0, 1)[n % 4], 0:288], ACT.Copy,
                                             scale=(nscq[:, m:m + 1], 1.0)[which]).then_inc(qk_ev, 1)

            def v_out(s, par):
                act.wait_ge(v_mm, s + 1)
                wait(act, av_mm, s - 1)
                nc.scalar.activation(vv[par][0:PT].rearrange("p (c h) d -> p c (h d)", c=2), ps[0:PT, 2:4, 0:384],
                                     ACT.Copy).then_inc(v_ev, 1)

            def pT_out(s):
                for c, bank in enumerate((0, 1, 7)):
                    act.wait_ge(t_mm, 3 * s + c + 1)
                    if c == 0:
                        wait(act, av_mm, s)
                    nc.scalar.activation(
                        pT[0:PT, 4 * c:4 * c + 4, :, :],
                        ps[0:PT, bank, :].rearrange("p (g b n) -> p g b n", g=4, b=2)[:, :, :, 0:N],
                        ACT.Copy).then_inc(t_ev, 1)

            def o_out(s):
                act.wait_ge(av_mm, s + 1)
                nc.scalar.activation(oT[:, :, bass.ds(s * PT, PT)],
                                     ps[:, 6, 0:HP * PT].rearrange("p (m n) -> p m n", m=HP), ACT.Copy)\
                    .then_inc(o_ev, 1)

            def exps(s, par):
                act.wait_ge(shifted, s + 1)
                wait(act, probs, 2 * s - 2)
                nc.scalar.activation(ee[par], rr[par], ACT.Exp).then_inc(expd, 1)

            exps(0, 0)
            v_out(0, 0)
            v_out(1, 1)

            def pair(s, par):
                pT_out(s - 3)
                exps(s - 2, par)
                o_out(s - 3)
                v_out(s - 1, 1 - par)
            def common_high_out(k):
                act.wait_ge(common_up_in, 32)
                nc.scalar.activation(common_high[:, k, :], (w1a, w1b)[k][0:DH, COMMON, :], ACT.Copy)\
                    .then_inc(common_high_w, 1)
            pair(3, 1)
            act.wait_ge(zeros_out, 48)
            common_high_out(0)
            pair(4, 0)
            common_high_out(1)
            with act.Fori(2, PAIRS // 2) as i:
                for par in range(2):
                    pair(2 * i + 1 + par, 1 - par)
            exps(PAIRS - 1, 1)
            for s in (PAIRS - 2, PAIRS - 1):
                pT_out(s)
                o_out(s)
            for t in range(TT):
                hT_out(TT + t, t, XN_BANK[t], xnT)
                act.wait_ge(hT_ev, TT + t + 1)
                tile = slice(t * P, t * P + rows(t))
                nc.scalar.activation(xn_high[:, :, tile], xnT[:, :, tile], ACT.Copy).then_inc(xn_high_ev, 1)
            act.wait_ge(lsub, 1)
            nc.scalar.activation(le[:, :, :], le[:, :, :], ACT.Exp).then_inc(le_exp, 1)
            for m in range(FM):
                act.wait_ge(c1_mm, 2 * m + 2 if m else 3)
                nc.scalar.activation(hcT[:, m, :].rearrange("p (a n) -> p a n", a=2),
                                     ps[:, m % 3 * 2:m % 3 * 2 + 2, 0:288], ACT.Gelu,
                                     bias=b1_s[:, m:m + 1]).then_inc(c1_ev, 1)

            for s in range(TILES):
                act.wait_ge(f1_mm, s + 1)
                wait(act, f2T_mm, s - 1)
                nc.scalar.activation(hs[s % 2].rearrange("p (c m) n -> p c (m n)", c=2), ps[:, 0:2, 0:384],
                                     ACT.Gelu).then_inc(f1_ev, 1)

        @block.gpsimd
        def _(pool):
            for i in range(2):
                nc.gpsimd.memset(pblk[i][:, :, :], 0.0).then_inc(zeroed, 1)
            pool.wait_ge(zeroed, 2)
            nc.gpsimd.memset(empty[:, :, :], 0.0).then_inc(empty_set, 1)
            pool.wait_ge(empty_set, 1)
            nc.gpsimd.memset(empty[:, :, D + 1:ROW], float(TOK)).then_inc(empty_set, 1)
            pool.wait_ge(first_w, XL)
            for f in range(1, SHIFTS):
                pool.wait_ge(pw_in[f], 16)
                wait(pool, fold_pool, 2 * f - 2)
                c = slice(f * XL + POOL_SLOTS, (f + 1) * XL)
                nc.gpsimd.tensor_tensor(out=scaled[0:PIX], in0=pw[0:PIX, f, POOL_SLOTS:, :],
                                        in1=lnw_s[0:PIX, c].unsqueeze(2).broadcast_to([PIX, XL - POOL_SLOTS, D]),
                                        op=ALU.mult).then_inc(fold_pool, 1)
                pool.wait_ge(fold_pool, 2 * f - 1)
                nc.gpsimd.tensor_tensor(out=weff[0:PIX, POOL_SLOTS:, :], in0=scaled[0:PIX],
                                        in1=weff[0:PIX, POOL_SLOTS:, :], op=ALU.add).then_inc(fold_pool, 1)
            pool.wait_ge(set_up, 2)
            pool.wait_ge(var_ev, 1)
            nc.gpsimd.tensor_tensor(out=rs[:, :, 0], in0=var[:, :, 0], in1=half[:, :].broadcast_to([P, TT]),
                                    op=ALU.pow).then_inc(rs_done, 1)

            def rstd(i, t):
                pool.wait_ge(ve_done, i + 1)
                n = rows(t)
                nc.gpsimd.tensor_tensor(out=rl[0:n, t, :], in0=ve[0:n, t, :], in1=half[0:n, :],
                                        op=ALU.pow).then_inc(rl_done, 1)
            for t in range(TT):
                rstd(t, t)
            pool.wait_ge(zeros_out, 48)
            pool.wait_ge(cst_in, 16)

            def logits(s, par):
                pool.wait_ge(dropped, s + 1)
                pool.wait_ge(se_done, s + 1)
                nc.gpsimd.tensor_tensor(out=rr[par], in0=se.broadcast_to([P, HEADS, N]), in1=rr[par],
                                        op=ALU.subtract).then_inc(logit, 1)

            def less_max(s, par):
                pool.wait_ge(rmax, s + 1)
                wait(pool, probs, 2 * s)
                nc.gpsimd.tensor_tensor(out=rr[par], in0=rr[par], in1=rowm.broadcast_to([P, HEADS, N]),
                                        op=ALU.subtract).then_inc(shifted, 1)

            def normalise(s, par):
                pool.wait_ge(expd, s + 1)
                pool.wait_ge(invd, s + 1)
                pool.wait_ge(logit, min(PAIRS - 1, s + 2) if isinstance(s, int) else s + 2)
                wait(pool, t_mm, 3 * s - 3)
                for b in range(2):
                    r = slice(64 * b, 64 * b + 64)
                    nc.gpsimd.tensor_tensor(out=pblk[par][r, :, b * N:(b + 1) * N], in0=ee[par][r, :, ::-1],
                                            in1=inv[r].broadcast_to([64, HEADS, N]), op=ALU.mult)\
                        .then_inc(probs, 1)
            logits(0, 0)
            less_max(0, 0)
            logits(1, 1)

            def pair(s, par):
                normalise(s - 2, par)
                less_max(s - 1, 1 - par)
                logits(s, par)
            pair(2, 0)
            pair(3, 1)
            with pool.Fori(2, PAIRS // 2 - 1) as i:
                for par in range(2):
                    pair(2 * i + par, par)
            pair(PAIRS - 2, 0)
            normalise(PAIRS - 3, 1)
            less_max(PAIRS - 2, 0)
            pool.wait_ge(shifted, PAIRS - 1)
            normalise(PAIRS - 2, 0)

            pool.wait_ge(probs, 2 * PAIRS - 2)
            for t in range(TT):
                rstd(TT + t, t)
            pool.wait_ge(slots_done, 3)
            pool.wait_ge(hn_done, 2 * TT)
            for t in range(TT):
                n = rows(t)
                nc.gpsimd.indirect_dma_start(
                    out=xg_dram, out_offset=bass.IndirectOffsetOnAxis(ap=idx_s[0:n, t:t + 1], axis=0),
                    in_=hn[0:n, t, :], in_offset=None).then_inc(scattered, 16)
            pool.wait_ge(rows_ready, 1)
            pool.wait_ge(stored, 32 * TT)

            def common_rows(s):
                wait(pool, y_ev, s - 1)
                nc.gpsimd.indirect_dma_start(
                    out=ag[s % 2][:, 0, :], out_offset=None, in_=acc_dram,
                    in_offset=bass.IndirectOffsetOnAxis(ap=row_i[:, s:s + 1], axis=0)).then_inc(ag_in[s % 2], 16)
            common_rows(0)
            common_rows(1)
            for s in range(TILES):
                pool.wait_ge(y_ev, s + 1)
                wait(pool, rows_out, 16 * s)
                nc.gpsimd.indirect_dma_start(
                    out=out, out_offset=bass.IndirectOffsetOnAxis(ap=row_i[:, s:s + 1], axis=0),
                    in_=ys[s % 2][:, 0, :], in_offset=None).then_inc(rows_out, 16)
                if s + 2 < TILES:
                    common_rows(s + 2)


def kernel(x, L0_tok_ln_weight, L0_tok_ln_bias, L0_tok_proj_weight, L0_tok_proj_bias, L0_attn_w_qkv,
           L0_attn_scale, L0_attn_w_out, L0_attn_b_out, L0_ffn_Ws, L0_ffn_bs, L0_ffn_W1, L0_ffn_b1,
           L0_ffn_W2, L0_ffn_b2):
    import concourse.bacc as bacc
    from concourse.bass_utils import run_bass_kernel_spmd

    def whole(a):
        return np.ascontiguousarray(a)

    xi = np.asarray(x).reshape(B, C, IMG, IMG)
    xp = np.pad(xi, ((0, 0), (0, 0), (1, 1), (1, 1)))

    def patches(dy, dx):
        v = xp[:, :, 1 + dy:1 + dy + IMG, 1 + dx:1 + dx + IMG]
        return v.reshape(B, C, SIDE, PATCH, SIDE, PATCH).transpose(1, 3, 5, 0, 2, 4).reshape(
            C, PATCH, PATCH, TOK)

    def halo(left, right, top, bottom):
        s = np.stack([left, right, top, bottom])
        return s.reshape(4, C, 2, 8, -1).transpose(1, 3, 0, 2, 4).reshape(HALO, XL, -1)
    xk = np.concatenate([
        patches(0, 0).reshape(PIX, XL, TOK),
        halo(patches(0, -1)[:, :, 0], patches(0, 1)[:, :, PATCH - 1],
             patches(-1, 0)[:, 0], patches(1, 0)[:, PATCH - 1])])

    def by_pixel(a):
        w = np.moveaxis(np.asarray(a), -1, 0).reshape(PATCH, PATCH, SHIFTS, C, -1).transpose(2, 3, 0, 1, 4)
        z = np.pad(w, ((0, 0), (0, 0), (1, 1), (1, 1), (0, 0)))
        to = ((0, 0), (0, 1), (0, -1), (1, 0), (-1, 0))
        body = np.stack([z[f, :, 1 + dy:1 + dy + PATCH, 1 + dx:1 + dx + PATCH]
                         for f, (dy, dx) in enumerate(to)])
        body = body.reshape(SHIFTS, PIX, XL, -1).transpose(1, 0, 2, 3)
        edge = halo(w[1][:, :, 0], w[2][:, :, PATCH - 1], w[3][:, 0], w[4][:, PATCH - 1])
        return body, edge

    def vector(a):
        body, edge = by_pixel(np.asarray(a).reshape(1, -1))
        table = np.zeros((ROWS, SHIFTS, XL), body.dtype)
        table[:PIX] = body[..., 0]
        table[PIX:, 0] = edge[..., 0]
        return table.reshape(ROWS, SHIFTS * XL)
    pk, ph = by_pixel(L0_tok_proj_weight)
    w1 = np.asarray(L0_ffn_W1).transpose(1, 0, 2)
    w2 = np.asarray(L0_ffn_W2).reshape(EXP, FM, P, D).transpose(2, 0, 1, 3)
    arrays = {
        "xk": xk, "pk": pk, "ph": ph, "lnw": vector(L0_tok_ln_weight), "lnb": vector(L0_tok_ln_bias),
        "pb": np.asarray(L0_tok_proj_bias).reshape(1, D),
        "wqkv": np.asarray(L0_attn_w_qkv).reshape(2, DH, 3 * INNER).transpose(1, 0, 2),
        "scale": np.repeat(np.asarray(L0_attn_scale).reshape(HP, 2).T, HD, axis=0),
        "wout": np.asarray(L0_attn_w_out).reshape(HP, P, D).transpose(1, 0, 2),
        "bout": np.asarray(L0_attn_b_out).reshape(1, D),
        "ws": np.asarray(L0_ffn_Ws).reshape(2, DH, EXP).transpose(1, 0, 2),
        "bs": np.asarray(L0_ffn_bs).reshape(1, EXP),
        "w1": w1, "b1": np.asarray(L0_ffn_b1).reshape(1, EXP, FF), "w2": w2, "b2": np.asarray(L0_ffn_b2),
        "b1c": np.asarray(L0_ffn_b1)[0].reshape(FM, P).T,
        "consts": constants(),
    }
    arrays = {f"{k}_dram": whole(v) for k, v in arrays.items()}
    nc = bacc.Bacc("TRN2", target_bir_lowering=False, num_devices=1)
    args = [nc.dram_tensor(k, v.shape, mybir.dt.from_np(v.dtype), kind="ExternalInput").ap()
            for k, v in arrays.items()]
    out = nc.dram_tensor("out_dram", (TOK + 1, D), mybir.dt.float32, kind="ExternalOutput").ap()
    build(nc, *args, out)
    r = run_bass_kernel_spmd(nc, [arrays], core_ids=[0])
    return r.results[0]["out_dram"][:TOK].reshape(B, N, D)
```
